# Optimizing a Trainium2 kernel written in Bass

```python
import numpy as np
import jax
import jax.numpy as jnp

def _softmax(x, axis=-1):
    return jax.nn.softmax(x, axis=axis)

def _gelu(x):
    return jax.nn.gelu(x, approximate=True)

def _silu(x):
    return jax.nn.silu(x)

def _sigmoid(x):
    return jax.nn.sigmoid(x)

def _layernorm(x, axis=-1, eps=1e-05):
    m = jnp.mean(x, axis=axis, keepdims=True)
    v = jnp.var(x, axis=axis, keepdims=True)
    return (x - m) / jnp.sqrt(v + eps)

def _scatter_add(tgt, idx, src, axis=0):
    return tgt.at[idx].add(src)

def _segment_sum(src, seg, n):
    return jax.ops.segment_sum(src, seg, n)
kernel_name = 'mk_decoder_preln_d1_seqx_r8_a5c6de'

def setup_inputs(seed: int=0):
    np.random.seed(seed)
    _w = jnp.asarray

    def _rec_inputs():
        import jax
        import jax.numpy as jnp
        _rk = jax.random.key(seed)
        x = -0.0002928 + 1 * jax.random.normal(jax.random.fold_in(_rk, 1), (64, 64, 128), jnp.float32)
        _lenS = 64 - jax.random.randint(jax.random.fold_in(_rk, 7), (64,), 0, max(1, 64 // 4) + 1, jnp.int32)
        _lenS2 = 64 - jax.random.randint(jax.random.fold_in(_rk, 8), (64,), 0, max(1, 64 // 4) + 1, jnp.int32)
        _ctx_1024P = jax.random.normal(jax.random.fold_in(_rk, 11), (64, 16, 128), jnp.float32)
        _ctx_1024c = jax.random.dirichlet(jax.random.fold_in(_rk, 511), 0.3 * jnp.ones((16,), jnp.float32), (64, 64))
        _ctx_1024t = jnp.einsum('bsk,bkd->bsd', _ctx_1024c, _ctx_1024P)
        _ctx_1024t = _ctx_1024t * jax.lax.rsqrt(jnp.mean(jnp.square(_ctx_1024t)) + 1e-12) * 0.953939
        ctx_1024 = -1.39393e-06 + 0.999914 * (_ctx_1024t + 0.3 * jax.random.normal(jax.random.fold_in(_rk, 611), (64, 64, 128), jnp.float32))
        return (x, ctx_1024)
    x, ctx_1024 = _rec_inputs()

    def _L0_attn_setup():
        import jax, jax.numpy as jnp
        import numpy as np
        import math
        D_MODEL = 128
        NUM_HEADS = 16
        HEAD_DIM = D_MODEL // NUM_HEADS
        WINDOW = 5
        key = jax.random.key(seed)
        ks = jax.random.split(key, 9)
        B, S = (2, 256)
        x = jax.random.normal(ks[0], (B, S, D_MODEL), dtype=jnp.float32)
        lim = math.sqrt(6.0 / (D_MODEL + D_MODEL))

        def w(k):
            return jax.random.uniform(k, (D_MODEL, D_MODEL), dtype=jnp.float32, minval=-lim, maxval=lim)
        return {'x': x, 'Wq': w(ks[1]), 'bq': jnp.zeros((D_MODEL,), jnp.float32), 'Wk': w(ks[2]), 'bk': jnp.zeros((D_MODEL,), jnp.float32), 'Wv': w(ks[3]), 'bv': jnp.zeros((D_MODEL,), jnp.float32), 'Wo': w(ks[4]), 'bo': jnp.zeros((D_MODEL,), jnp.float32)}
    _L0_attn_all = _L0_attn_setup()
    _L0_attn_in = {k: v for k, v in _L0_attn_all.items() if k in ('Wq', 'bq', 'Wk', 'bk', 'Wv', 'bv', 'Wo', 'bo')}
    del _L0_attn_all

    def _L0_xattn_setup():
        import jax, jax.numpy as jnp
        import numpy as np
        B, S, E, NH = (2, 256, 128, 4)
        HD = E // NH

        def _mlstm_head(q, k, v, ig, fg, eps=1e-06):
            s, dh = q.shape
            log_f = jax.nn.log_sigmoid(fg)
            cs = jnp.concatenate([jnp.zeros((1, 1), log_f.dtype), jnp.cumsum(log_f, axis=0)], axis=0)
            neg = jnp.asarray(-0.7 * jnp.finfo(cs.dtype).max, cs.dtype)
            log_d = jnp.where(jnp.tri(s, dtype=bool), (cs - cs.T)[1:, 1:] + ig.T, neg)
            m = jnp.max(log_d, axis=-1, keepdims=True)
            d = jnp.exp(log_d - m)
            c = q @ (k.T / jnp.sqrt(dh)) * d
            n = jnp.maximum(jnp.sum(c, axis=-1, keepdims=True), jnp.exp(-m))
            return c / (n + eps) @ v
        key = jax.random.key(seed)
        ks = jax.random.split(key, 8)
        return {'q': jax.random.normal(ks[0], (B, S, E), jnp.float32), 'k': jax.random.normal(ks[1], (B, S, E), jnp.float32), 'v': jax.random.normal(ks[2], (B, S, E), jnp.float32), 'igate_kernel': jax.random.normal(ks[3], (3 * E, NH), jnp.float32) * 0.02, 'igate_bias': jax.random.normal(ks[4], (NH,), jnp.float32) * 0.1, 'fgate_kernel': jax.random.normal(ks[5], (3 * E, NH), jnp.float32) * 0.02, 'fgate_bias': jnp.linspace(3.0, 6.0, NH, dtype=jnp.float32), 'rms_scale': jax.random.normal(ks[6], (HD,), jnp.float32) * 0.02}
    _L0_xattn_all = _L0_xattn_setup()
    _L0_xattn_in = {k: v for k, v in _L0_xattn_all.items() if k in ('igate_kernel', 'igate_bias', 'fgate_kernel', 'fgate_bias', 'rms_scale')}
    del _L0_xattn_all

    def _L0_ffn_setup():
        import jax, jax.numpy as jnp
        import numpy as np
        DIM = 128
        DEPTH = 2
        HEADS = 8
        DIM_HEAD = 64
        WINDOW = 64
        INNER = HEADS * DIM_HEAD
        HID = int(DIM * 4 * 2 / 3)
        B, N = (2, 1024)
        QK_SCALE = 8.0

        def shift_token(t):
            t1, t2 = jnp.split(t, 2, axis=-1)
            t2 = jnp.pad(t2, ((0, 0), (1, 0), (0, 0)))[:, :-1]
            return jnp.concatenate([t1, t2], axis=-1)

        def l2norm(t):
            return t / jnp.clip(jnp.linalg.norm(t, axis=-1, keepdims=True), 1e-12)

        def rotate_half(x):
            x1, x2 = jnp.split(x, 2, axis=-1)
            return jnp.concatenate([-x2, x1], axis=-1)

        def rotary_xpos(q, k):
            n = q.shape[-2]
            half_idx = jnp.arange(0, DIM_HEAD, 2, dtype=jnp.float32)
            inv_freq = 1.0 / 10000.0 ** (half_idx / DIM_HEAD)
            t = jnp.arange(n, dtype=jnp.float32)
            freqs = t[:, None] * inv_freq[None, :]
            freqs = jnp.concatenate([freqs, freqs], axis=-1)
            base = (half_idx + 0.4 * DIM_HEAD) / (1.4 * DIM_HEAD)
            power = (t - n // 2) / float(WINDOW // 2)
            scale = base[None, :] ** power[:, None]
            scale = jnp.concatenate([scale, scale], axis=-1)
            cos, sin = (jnp.cos(freqs), jnp.sin(freqs))
            q = q * cos * scale + rotate_half(q) * sin * scale
            k = k * cos / scale + rotate_half(k) * sin / scale
            return (q, k)

        def local_attention(q, k, v):
            b, h, n, d = q.shape
            w = n // WINDOW
            bq = q.reshape(b, h, w, WINDOW, d) * QK_SCALE
            bk = k.reshape(b, h, w, WINDOW, d)
            bv = v.reshape(b, h, w, WINDOW, d)

            def look_around(t):
                p = jnp.pad(t, ((0, 0), (0, 0), (1, 0), (0, 0), (0, 0)))
                return jnp.concatenate([p[:, :, :w], p[:, :, 1:]], axis=3)
            bk, bv = (look_around(bk), look_around(bv))
            bt = jnp.arange(n).reshape(w, WINDOW)
            btp = jnp.pad(bt, ((1, 0), (0, 0)), constant_values=-1)
            btk = jnp.concatenate([btp[:w], btp[1:]], axis=1)
            sim = jnp.einsum('bhwid,bhwjd->bhwij', bq, bk)
            i = bt[:, :, None]
            j = btk[:, None, :]
            mask = (i < j) | (i > j + WINDOW) | (j == -1)
            sim = jnp.where(mask, -jnp.finfo(sim.dtype).max, sim)
            attn = jax.nn.softmax(sim, axis=-1)
            out = jnp.einsum('bhwij,bhwjd->bhwid', attn, bv)
            return out.reshape(b, h, n, d)

        def _layer(x, wqkv, qs, ksc, wo, lg, lb, w1, b1, w2, b2):
            b, n, _ = x.shape
            h = shift_token(x)
            qkv = h @ wqkv
            q, k, v = jnp.split(qkv, 3, axis=-1)
            to_heads = lambda t: t.reshape(b, n, HEADS, DIM_HEAD).transpose(0, 2, 1, 3)
            q, k, v = (to_heads(q), to_heads(k), to_heads(v))
            q = l2norm(q) * qs
            k = l2norm(k) * ksc
            q, k = rotary_xpos(q, k)
            o = local_attention(q, k, v)
            o = o.transpose(0, 2, 1, 3).reshape(b, n, INNER)
            x = x + o @ wo
            h = shift_token(x)
            mu = h.mean(-1, keepdims=True)
            var = h.var(-1, keepdims=True)
            h = (h - mu) / jnp.sqrt(var + 1e-05) * lg + lb
            h = h @ w1 + b1
            a, g = jnp.split(h, 2, axis=-1)
            h = a * jax.nn.gelu(g, approximate=False)
            x = x + h @ w2 + b2
            return x
        key = jax.random.key(seed)
        ks = jax.random.split(key, 6)
        return {'x': jax.random.normal(ks[0], (B, N, DIM), jnp.float32), 'wqkv': jax.random.normal(ks[1], (DEPTH, DIM, 3 * INNER), jnp.float32) * 0.02, 'q_scale': jnp.ones((DEPTH, DIM_HEAD), jnp.float32), 'k_scale': jnp.ones((DEPTH, DIM_HEAD), jnp.float32), 'wo': jax.random.normal(ks[2], (DEPTH, INNER, DIM), jnp.float32) * 0.02, 'ln_g': jnp.ones((DEPTH, DIM), jnp.float32), 'ln_b': jnp.zeros((DEPTH, DIM), jnp.float32), 'w1': jax.random.normal(ks[3], (DEPTH, DIM, 2 * HID), jnp.float32) * 0.02, 'b1': jnp.zeros((DEPTH, 2 * HID), jnp.float32), 'w2': jax.random.normal(ks[4], (DEPTH, HID, DIM), jnp.float32) * 0.02, 'b2': jnp.zeros((DEPTH, DIM), jnp.float32)}
    _L0_ffn_all = _L0_ffn_setup()
    _L0_ffn_in = {k: v for k, v in _L0_ffn_all.items() if k in ('wqkv', 'q_scale', 'k_scale', 'wo', 'ln_g', 'ln_b', 'w1', 'b1', 'w2', 'b2')}
    del _L0_ffn_all
    return {'x': x, 'ctx_1024': ctx_1024, 'L0_attn_Wq': _L0_attn_in['Wq'], 'L0_attn_bq': _L0_attn_in['bq'], 'L0_attn_Wk': _L0_attn_in['Wk'], 'L0_attn_bk': _L0_attn_in['bk'], 'L0_attn_Wv': _L0_attn_in['Wv'], 'L0_attn_bv': _L0_attn_in['bv'], 'L0_attn_Wo': _L0_attn_in['Wo'], 'L0_attn_bo': _L0_attn_in['bo'], 'L0_xattn_igate_kernel': _L0_xattn_in['igate_kernel'], 'L0_xattn_igate_bias': _L0_xattn_in['igate_bias'], 'L0_xattn_fgate_kernel': _L0_xattn_in['fgate_kernel'], 'L0_xattn_fgate_bias': _L0_xattn_in['fgate_bias'], 'L0_xattn_rms_scale': _L0_xattn_in['rms_scale'], 'L0_ffn_wqkv': _L0_ffn_in['wqkv'], 'L0_ffn_q_scale': _L0_ffn_in['q_scale'], 'L0_ffn_k_scale': _L0_ffn_in['k_scale'], 'L0_ffn_wo': _L0_ffn_in['wo'], 'L0_ffn_ln_g': _L0_ffn_in['ln_g'], 'L0_ffn_ln_b': _L0_ffn_in['ln_b'], 'L0_ffn_w1': _L0_ffn_in['w1'], 'L0_ffn_b1': _L0_ffn_in['b1'], 'L0_ffn_w2': _L0_ffn_in['w2'], 'L0_ffn_b2': _L0_ffn_in['b2']}

def reference(x, ctx_1024, L0_attn_Wq, L0_attn_bq, L0_attn_Wk, L0_attn_bk, L0_attn_Wv, L0_attn_bv, L0_attn_Wo, L0_attn_bo, L0_xattn_igate_kernel, L0_xattn_igate_bias, L0_xattn_fgate_kernel, L0_xattn_fgate_bias, L0_xattn_rms_scale, L0_ffn_wqkv, L0_ffn_q_scale, L0_ffn_k_scale, L0_ffn_wo, L0_ffn_ln_g, L0_ffn_ln_b, L0_ffn_w1, L0_ffn_b1, L0_ffn_w2, L0_ffn_b2):
    import jax
    import jax.numpy as jnp

    def _L0_attn_ref(x, Wq, bq, Wk, bk, Wv, bv, Wo, bo):
        import jax, jax.numpy as jnp
        import numpy as np
        import math
        D_MODEL = 128
        NUM_HEADS = 16
        HEAD_DIM = D_MODEL // NUM_HEADS
        WINDOW = 5
        B, S, D = x.shape
        H, hd = (NUM_HEADS, HEAD_DIM)
        half = WINDOW // 2

        def proj(W, b):
            return (jnp.einsum('bsd,ed->bse', x, W) + b).reshape(B, S, H, hd).transpose(0, 2, 1, 3)
        q = proj(Wq, bq)
        k = proj(Wk, bk)
        v = proj(Wv, bv)
        scores = jnp.einsum('bhqd,bhkd->bhqk', q, k) / jnp.sqrt(jnp.asarray(hd, x.dtype))
        i = jnp.arange(S)[:, None]
        j = jnp.arange(S)[None, :]
        band = (j >= i - half) & (j <= i + half)
        scores = jnp.where(band, scores, jnp.asarray(-1000000000.0, x.dtype))
        attn = jax.nn.softmax(scores, axis=-1)
        out = jnp.einsum('bhqk,bhkd->bhqd', attn, v)
        out = out.transpose(0, 2, 1, 3).reshape(B, S, D)
        return jnp.einsum('bsd,ed->bse', out, Wo) + bo

    def _L0_xattn_ref(q, k, v, igate_kernel, igate_bias, fgate_kernel, fgate_bias, rms_scale):
        import jax, jax.numpy as jnp
        import numpy as np
        B, S, E, NH = (2, 256, 128, 4)
        HD = E // NH

        def _mlstm_head(q, k, v, ig, fg, eps=1e-06):
            s, dh = q.shape
            log_f = jax.nn.log_sigmoid(fg)
            cs = jnp.concatenate([jnp.zeros((1, 1), log_f.dtype), jnp.cumsum(log_f, axis=0)], axis=0)
            neg = jnp.asarray(-0.7 * jnp.finfo(cs.dtype).max, cs.dtype)
            log_d = jnp.where(jnp.tri(s, dtype=bool), (cs - cs.T)[1:, 1:] + ig.T, neg)
            m = jnp.max(log_d, axis=-1, keepdims=True)
            d = jnp.exp(log_d - m)
            c = q @ (k.T / jnp.sqrt(dh)) * d
            n = jnp.maximum(jnp.sum(c, axis=-1, keepdims=True), jnp.exp(-m))
            return c / (n + eps) @ v
        b, s, e = q.shape
        nh = igate_kernel.shape[1]
        hd = e // nh
        gate_in = jnp.concatenate((q, k, v), axis=-1)
        ig = (gate_in @ igate_kernel + igate_bias).swapaxes(-1, -2)[..., None]
        fg = (gate_in @ fgate_kernel + fgate_bias).swapaxes(-1, -2)[..., None]
        qh = q.reshape(b, s, nh, hd).swapaxes(1, 2)
        kh = k.reshape(b, s, nh, hd).swapaxes(1, 2)
        vh = v.reshape(b, s, nh, hd).swapaxes(1, 2)
        h = jax.vmap(jax.vmap(_mlstm_head))(qh, kh, vh, ig, fg)
        var = jnp.mean(jnp.square(h.astype(jnp.float32)), axis=-1, keepdims=True)
        h = (h * jax.lax.rsqrt(var + 1e-06)).astype(h.dtype) * (1.0 + rms_scale)
        return h.swapaxes(1, 2).reshape(b, s, e)

    def _L0_ffn_ref(x, wqkv, q_scale, k_scale, wo, ln_g, ln_b, w1, b1, w2, b2):
        import jax, jax.numpy as jnp
        import numpy as np
        DIM = 128
        DEPTH = 2
        HEADS = 8
        DIM_HEAD = 64
        WINDOW = 64
        INNER = HEADS * DIM_HEAD
        HID = int(DIM * 4 * 2 / 3)
        B, N = (2, 1024)
        QK_SCALE = 8.0

        def shift_token(t):
            t1, t2 = jnp.split(t, 2, axis=-1)
            t2 = jnp.pad(t2, ((0, 0), (1, 0), (0, 0)))[:, :-1]
            return jnp.concatenate([t1, t2], axis=-1)

        def l2norm(t):
            return t / jnp.clip(jnp.linalg.norm(t, axis=-1, keepdims=True), 1e-12)

        def rotate_half(x):
            x1, x2 = jnp.split(x, 2, axis=-1)
            return jnp.concatenate([-x2, x1], axis=-1)

        def rotary_xpos(q, k):
            n = q.shape[-2]
            half_idx = jnp.arange(0, DIM_HEAD, 2, dtype=jnp.float32)
            inv_freq = 1.0 / 10000.0 ** (half_idx / DIM_HEAD)
            t = jnp.arange(n, dtype=jnp.float32)
            freqs = t[:, None] * inv_freq[None, :]
            freqs = jnp.concatenate([freqs, freqs], axis=-1)
            base = (half_idx + 0.4 * DIM_HEAD) / (1.4 * DIM_HEAD)
            power = (t - n // 2) / float(WINDOW // 2)
            scale = base[None, :] ** power[:, None]
            scale = jnp.concatenate([scale, scale], axis=-1)
            cos, sin = (jnp.cos(freqs), jnp.sin(freqs))
            q = q * cos * scale + rotate_half(q) * sin * scale
            k = k * cos / scale + rotate_half(k) * sin / scale
            return (q, k)

        def local_attention(q, k, v):
            b, h, n, d = q.shape
            w = n // WINDOW
            bq = q.reshape(b, h, w, WINDOW, d) * QK_SCALE
            bk = k.reshape(b, h, w, WINDOW, d)
            bv = v.reshape(b, h, w, WINDOW, d)

            def look_around(t):
                p = jnp.pad(t, ((0, 0), (0, 0), (1, 0), (0, 0), (0, 0)))
                return jnp.concatenate([p[:, :, :w], p[:, :, 1:]], axis=3)
            bk, bv = (look_around(bk), look_around(bv))
            bt = jnp.arange(n).reshape(w, WINDOW)
            btp = jnp.pad(bt, ((1, 0), (0, 0)), constant_values=-1)
            btk = jnp.concatenate([btp[:w], btp[1:]], axis=1)
            sim = jnp.einsum('bhwid,bhwjd->bhwij', bq, bk)
            i = bt[:, :, None]
            j = btk[:, None, :]
            mask = (i < j) | (i > j + WINDOW) | (j == -1)
            sim = jnp.where(mask, -jnp.finfo(sim.dtype).max, sim)
            attn = jax.nn.softmax(sim, axis=-1)
            out = jnp.einsum('bhwij,bhwjd->bhwid', attn, bv)
            return out.reshape(b, h, n, d)

        def _layer(x, wqkv, qs, ksc, wo, lg, lb, w1, b1, w2, b2):
            b, n, _ = x.shape
            h = shift_token(x)
            qkv = h @ wqkv
            q, k, v = jnp.split(qkv, 3, axis=-1)
            to_heads = lambda t: t.reshape(b, n, HEADS, DIM_HEAD).transpose(0, 2, 1, 3)
            q, k, v = (to_heads(q), to_heads(k), to_heads(v))
            q = l2norm(q) * qs
            k = l2norm(k) * ksc
            q, k = rotary_xpos(q, k)
            o = local_attention(q, k, v)
            o = o.transpose(0, 2, 1, 3).reshape(b, n, INNER)
            x = x + o @ wo
            h = shift_token(x)
            mu = h.mean(-1, keepdims=True)
            var = h.var(-1, keepdims=True)
            h = (h - mu) / jnp.sqrt(var + 1e-05) * lg + lb
            h = h @ w1 + b1
            a, g = jnp.split(h, 2, axis=-1)
            h = a * jax.nn.gelu(g, approximate=False)
            x = x + h @ w2 + b2
            return x
        for l in range(DEPTH):
            x = _layer(x, wqkv[l], q_scale[l], k_scale[l], wo[l], ln_g[l], ln_b[l], w1[l], b1[l], w2[l], b2[l])
        return x
    x = x + _L0_attn_ref(_layernorm(x, axis=-1), L0_attn_Wq, L0_attn_bq, L0_attn_Wk, L0_attn_bk, L0_attn_Wv, L0_attn_bv, L0_attn_Wo, L0_attn_bo)
    x = x + _L0_xattn_ref(_layernorm(x, axis=-1), ctx_1024, ctx_1024, L0_xattn_igate_kernel, L0_xattn_igate_bias, L0_xattn_fgate_kernel, L0_xattn_fgate_bias, L0_xattn_rms_scale)
    x = x + _L0_ffn_ref(_layernorm(x, axis=-1), L0_ffn_wqkv, L0_ffn_q_scale, L0_ffn_k_scale, L0_ffn_wo, L0_ffn_ln_g, L0_ffn_ln_b, L0_ffn_w1, L0_ffn_b1, L0_ffn_w2, L0_ffn_b2)
    return x

_drawn_inputs = setup_inputs


def setup_inputs(seed=0):
    import zlib

    import numpy as np

    out = dict(_drawn_inputs(seed))
    spreads = {'L0_attn_bq': (0.0, 0.1),
     'L0_attn_bk': (0.0, 2.0),
     'L0_attn_bv': (0.0, 0.1),
     'L0_attn_bo': (0.0, 0.1),
     'L0_ffn_q_scale': (1.0, 0.6),
     'L0_ffn_k_scale': (1.0, 0.6),
     'L0_ffn_ln_g': (1.0, 0.6),
     'L0_ffn_ln_b': (0.0, 0.8),
     'L0_ffn_b1': (0.0, 0.8),
     'L0_ffn_b2': (0.0, 0.8)}
    factors = {'L0_xattn_igate_bias': 64.0,
     'L0_xattn_fgate_kernel': 5.144,
     'L0_xattn_rms_scale': 4.323,
     'L0_ffn_wqkv': 2.941,
     'L0_ffn_wo': 2.938,
     'L0_ffn_w1': 8.0,
     'L0_ffn_w2': 8.0}
    for name, (base, spread) in spreads.items():
        noise = np.random.default_rng([zlib.crc32(name.encode()), seed]).standard_normal(out[name].shape)
        drawn = base * np.exp(spread * noise) if base else spread * noise
        out[name] = jnp.asarray(drawn.astype(out[name].dtype))
    for name, factor in factors.items():
        out[name] = (out[name] * factor).astype(out[name].dtype)
    return out
```

```python
from contextlib import ExitStack

import numpy as np
import concourse.bass as bass
from concourse import mybir

F32 = mybir.dt.float32
F32R = mybir.dt.float32r
BF16 = mybir.dt.bfloat16
ALU = mybir.AluOpType
ACT = mybir.ActivationFunctionType
X_AXIS = mybir.AxisListType.X

P = 128
NSEQ, SEQ, D = 64, 64, 128
TOKENS = NSEQ * SEQ
TILES = TOKENS // P
GT = 4
GROUPS = TILES // GT
GN = GT * P
GS = GN // SEQ
AH, AHD, WIN = 16, 8, 5
HALF = WIN // 2
PADSEQ = SEQ + 2 * HALF
MH, MHD = 4, 32
LH, LHD = 8, 64
INNER = LH * LHD
HID = 341
HCH = (128, 128, 85)
DEPTH = 2
NEG = -1e30
LN_EPS = 1e-5

CONSTS = {}
_at = 0
for _name, _n in (("ident", 128), ("headsum", AH), ("winmask", WIN * AH), ("causal", SEQ), ("keyquery", SEQ),
                  ("tri", 128), ("negfold", SEQ), ("sameseq", 128), ("shift", 128), ("rot", 4 * LHD), ("eps", 4),
                  ("seqstart", 128)):
    CONSTS[_name] = (_at, _at + _n)
    _at += _n
NCONST = _at


def ahead(n):
    return not isinstance(n, int) or n > 0


def wait(eng, sem, n):
    if ahead(n):
        eng.wait_ge(sem, n)


def live(i, lag, n):
    return not isinstance(i, int) or 0 <= i - lag < n


def sweep(eng, n, lag, unroll, step):
    first = -(-(lag + 1) // unroll) * unroll
    for i in range(first):
        step(i, i % unroll)
    with eng.Fori(first // unroll, n // unroll) as u:
        for k in range(unroll):
            step(u * unroll + k if unroll > 1 else u, k)
    for i in range(n, n + lag):
        step(i, i % unroll)


def group_rows(x, g):
    return x[:, bass.ds(g * GT, GT), :]


class Semaphores:

    def __init__(self, nc):
        self.nc, self.all = nc, []

    def __call__(self, name):
        self.all.append(self.nc.alloc_semaphore(name))
        return self.all[-1]

    def clear(self):
        self.nc.clear_and_free_semaphores(self.all)
        self.nc.all_engine_barrier()


def apart(eng, sem):
    eng.sem_inc(sem, 1)


class Norm:

    def __init__(self, sb, sem, tag):
        self.stats = sb(f"{tag}_stats", [P, GT, 12])
        self.meanvar = sb(f"{tag}_meanvar", [P, GT, 2])
        self.logvar = sb(f"{tag}_logvar", [P, GT])
        self.rstd = sb(f"{tag}_rstd", [P, GT])
        self.s_stats = sem(f"{tag}_stats_done")
        self.s_meanvar = sem(f"{tag}_meanvar_done")
        self.s_logvar = sem(f"{tag}_logvar_done")
        self.s_rstd = sem(f"{tag}_rstd_done")
        self.s_apart = sem(f"{tag}_apart")


def norm_stats(dve, nm, x, g):
    for j in range(GT):
        dve.bn_stats(nm.stats[:, j, 0:6], x[:, g * GT + j, :]).then_inc(nm.s_stats, 1)
    dve.wait_ge(nm.s_stats, (g + 1) * GT)
    apart(dve, nm.s_apart)
    for j in range(GT):
        dve.bn_aggr(nm.meanvar[:, j, :], nm.stats[:, j, 0:6]).then_inc(nm.s_meanvar, 1)


def norm_rstd(act, nm, eps, g):
    act.wait_ge(nm.s_meanvar, (g + 1) * GT)
    act.activation(nm.logvar[:, :], nm.meanvar[:, :, 1], ACT.Ln, bias=eps).then_inc(nm.s_logvar, 1)
    act.wait_ge(nm.s_logvar, g + 1)
    act.activation(nm.rstd[:, :], nm.logvar[:, :], ACT.Exp, scale=-0.5).then_inc(nm.s_rstd, 1)


def norm_apply(dve, nm, out, x, g, s_out):
    dve.wait_ge(nm.s_rstd, g + 1)
    for j in range(GT):
        dve.tensor_scalar(out(j), x[:, g * GT + j, :], nm.meanvar[:, j, 0:1], nm.rstd[:, j:j + 1],
                          ALU.subtract, ALU.mult).then_inc(s_out, 1)


def load_phase(nc, t, dram):
    with ExitStack() as ctx:
        sem = Semaphores(nc)
        ctx.callback(sem.clear)

        s_const, s_x, s_zero, s_cast = sem("const_loaded"), sem("x_loaded"), sem("pads_zeroed"), sem("masks_cast")
        s_w, s_kv, s_tab = sem("weights_loaded"), sem("kv_gates_summed"), sem("ctx_ones_set")
        block = ctx.enter_context(nc.Block())

        @block.sync
        def _(sp):
            sp.dma_start(t["const"][:], dram["const"]).then_inc(s_const, 16)
            for g in range(GROUPS):
                src = dram["x"].rearrange("(t p) f -> p t f", p=P)[:, g * GT:(g + 1) * GT, :]
                sp.dma_start(t["X"][:, g * GT:(g + 1) * GT, :], src).then_inc(s_x, 16)
            sp.wait_ge(s_x, 16 * GROUPS)

        @block.scalar
        def _(act):
            n = 0
            for name in ("wq", "wk", "wv", "wo", "abias", "bo", "gate_q", "gate_k", "gate_v", "gate_bias",
                         "rms", "winspread"):
                act.dma_start(t[name][:], dram[name]).then_inc(s_w, 16)
                n += 16
            act.wait_ge(s_w, n)
            n = 0
            for name in ("wqkv", "lwo", "qks", "w1", "w2", "ffncols", "b2"):
                for layer in range(DEPTH):
                    act.dma_start(t[name][layer][:], dram[f"{name}{layer}"]).then_inc(t["s_layers"], 16)
                    n += 16
            t["layers_loaded"] = n

        @block.gpsimd
        def _(pool):
            pool.memset(t["kpad"][:], 0.0).then_inc(s_zero, 1)
            pool.memset(t["vpad"][:], 0.0).then_inc(s_zero, 1)
            pool.memset(t["ctxpad"][:], 1.0).then_inc(s_zero, 1)
            pool.memset(t["qdiag"][:], 0.0).then_inc(s_zero, 1)

        @block.vector
        def _(dve):
            c = t["c"]
            dve.wait_ge(s_const, 16)
            dve.tensor_copy(t["ident16"][:], c("ident")).then_inc(s_cast, 1)
            dve.tensor_copy(t["causal16"][:],
                            c("causal").unsqueeze(1).broadcast_to([P, 8, SEQ])).then_inc(s_cast, 1)
            dve.tensor_copy(t["keyquery16"][:],
                            c("keyquery").unsqueeze(1).broadcast_to([P, 8, SEQ])).then_inc(s_cast, 1)
            dve.wait_ge(s_w, 16 * 12)
            dve.tensor_tensor(t["gate_kv"][:], t["gate_k"][:], t["gate_v"][:], ALU.add).then_inc(s_kv, 1)
            dve.tensor_scalar(t["rms1"][:], t["rms"][:], 1.0, None, ALU.add).then_inc(s_kv, 1)


def window_attention(nc, t):
    with ExitStack() as ctx:
        def sb(name, shape, dt=F32):
            return ctx.enter_context(nc.sbuf_tensor(name, shape, dt))

        def ps(name, shape):
            return ctx.enter_context(nc.psum_tensor(name, shape, F32))

        sem = Semaphores(nc)
        ctx.callback(sem.clear)

        X, c = t["X"], t["c"]
        kpad, vpad = t["kpad"], t["vpad"]
        nm = Norm(sb, sem, "an")
        h = sb("a_h", [P, GT, D])
        hT = sb("a_hT", [P, GN])
        q = sb("a_q", [P, GS, SEQ])
        prod = sb("a_prod", [P, WIN, GN])
        score = sb("a_score", [P, GT, WIN, AH])
        prob = sb("a_prob", [P, GT, WIN, AH])
        pnorm = sb("a_pnorm", [P, GT, WIN, AH])
        smax = sb("a_smax", [P, GT, AH])
        ssum = sb("a_ssum", [P, GT, AH])
        sinv = sb("a_sinv", [P, GT, AH])
        pT = sb("a_pT", [WIN * AH, GN])
        pv = sb("a_pv", [P, WIN, GN])
        acc = sb("a_acc", [P, WIN - 2, GN])
        attnT = sb("a_attnT", [P, GN])

        ps_turn = ps("a_ps_turn", [P, GN])
        ps_qkv = ps("a_ps_qkv", [P, 3, GN])
        ps_score = ps("a_ps_score", [P, 512])
        ps_spread = ps("a_ps_spread", [P, 2, GN])
        ps_out = ps("a_ps_out", [P, GT, D])

        s_h, s_turned, s_hT = sem("a_h_ready"), sem("a_h_turned"), sem("a_hT_ready")
        s_qkv, s_q, s_k, s_v = sem("a_qkv_done"), sem("a_q_ready"), sem("a_k_ready"), sem("a_v_ready")
        s_prod_d, s_prod_p = sem("a_prod_vector"), sem("a_prod_pool")
        s_sc, s_masked, s_max, s_sub = sem("a_scores_done"), sem("a_masked"), sem("a_max_done"), sem("a_shifted")
        s_exp, s_sum, s_inv, s_pn = sem("a_exp_done"), sem("a_sum_done"), sem("a_inverse_done"), sem("a_probs_ready")
        s_pturned, s_pT = sem("a_probs_turned"), sem("a_pT_ready")
        s_spread, s_pv, s_acc = sem("a_probs_spread"), sem("a_pv_ready"), sem("a_sum_of_pv")
        s_out, s_res, s_bias = sem("a_out_done"), sem("a_residual_done"), sem("a_bias_added")

        eps = c("eps")[:, 0:1]
        maskb = c("winmask").unsqueeze(1).broadcast_to([P, GT, WIN * AH])
        N = GROUPS
        LAG = 3
        block = ctx.enter_context(nc.Block())

        @block.tensor
        def _(pe):
            def step(i, _):
                if live(i, 2, N):
                    g = i - 2
                    pe.wait_ge(s_prod_d, 3 * (g + 1))
                    pe.wait_ge(s_prod_p, 2 * (g + 1))
                    wait(pe, s_masked, g)
                    for j in range(GT):
                        for w in range(WIN):
                            at = (j * WIN + w) * AH
                            mm = pe.matmul(ps_score[:, at:at + AH], prod[:, w, j * P:(j + 1) * P], c("headsum"),
                                           start=True, stop=True)
                    mm.then_inc(s_sc, 1)
                if live(i, 3, N):
                    g = i - 3
                    pe.wait_ge(s_acc, 4 * (g + 1))
                    wait(pe, s_res, g)
                    for j in range(GT):
                        mm = pe.matmul(ps_out[:, j, :], attnT[:, j * P:(j + 1) * P], t["wo"][:, :],
                                       start=True, stop=True)
                    mm.then_inc(s_out, 1)
                if live(i, 1, N):
                    g = i - 1
                    pe.wait_ge(s_h, GT * (g + 1))
                    wait(pe, s_pT, g - 1)
                    for j in range(GT):
                        mm = pe.transpose(ps_turn[:, j * P:(j + 1) * P], h[:, j, :], c("ident"))
                    mm.then_inc(s_turned, 1)
                    pe.wait_ge(s_hT, g + 1)
                    wait(pe, s_v, g)
                    for n, w in enumerate(("wq", "wk", "wv")):
                        pe.matmul(ps_qkv[:, n, :], t[w][:, :], hT[:, :], start=True, stop=True).then_inc(s_qkv, 1)
                if live(i, 2, N):
                    g = i - 2
                    pe.wait_ge(s_pn, g + 1)
                    if live(i, 1, N):
                        pe.wait_ge(s_hT, g + 2)
                    for j in range(GT):
                        mm = pe.transpose(ps_turn[0:WIN * AH, j * P:(j + 1) * P],
                                          pnorm[:, j, :, :].rearrange("p w h -> p (w h)"), c("ident"))
                    mm.then_inc(s_pturned, 1)
                    pe.wait_ge(s_pT, g + 1)
                    for w in range(WIN):
                        wait(pe, s_pv, WIN * g + w - 1)
                        pe.matmul(ps_spread[:, w % 2, :], t["winspread"][:, w, :], pT[:, :],
                                  start=True, stop=True).then_inc(s_spread, 1)
            sweep(pe, N, LAG, 1, step)

        @block.scalar
        def _(act):
            act.preload_act_table_set("natural_log_exp_and_others")
            def step(i, _):
                if live(i, 2, N):
                    g = i - 2
                    act.wait_ge(s_sub, g + 1)
                    act.activation(prob[:], score[:], ACT.Exp, scale=float(AHD) ** -0.5).then_inc(s_exp, 1)
                if live(i, 1, N):
                    g = i - 1
                    act.wait_ge(s_turned, g + 1)
                    act.activation(hT[:], ps_turn[:], ACT.Copy).then_inc(s_hT, 1)
                    act.wait_ge(s_qkv, 3 * g + 1)
                    wait(act, s_prod_d, 3 * g)
                    wait(act, s_prod_p, 2 * g)
                    act.activation(q[:], ps_qkv[:, 0, :].rearrange("p (s t) -> p s t", t=SEQ), ACT.Identity,
                                   bias=t["abias"][:, 0:1]).then_inc(s_q, 1)
                    act.wait_ge(s_qkv, 3 * g + 2)
                    act.activation(kpad[:, :, HALF:HALF + SEQ],
                                   ps_qkv[:, 1, :].rearrange("p (s t) -> p s t", t=SEQ), ACT.Identity,
                                   bias=t["abias"][:, 1:2]).then_inc(s_k, 1)
                    act.wait_ge(s_qkv, 3 * g + 3)
                    act.activation(vpad[:, bass.ds(g * GS, GS), HALF:HALF + SEQ],
                                   ps_qkv[:, 2, :].rearrange("p (s t) -> p s t", t=SEQ), ACT.Identity,
                                   bias=t["abias"][:, 2:3]).then_inc(s_v, 1)
                if live(i, 2, N):
                    g = i - 2
                    act.wait_ge(s_pturned, g + 1)
                    act.activation(pT[:], ps_turn[0:WIN * AH, :], ACT.Copy).then_inc(s_pT, 1)
                if live(i, 0, N):
                    norm_rstd(act, nm, eps, i)
            sweep(act, N, LAG, 1, step)

        def window_product(eng, w, s):
            eng.tensor_tensor(prod[:, w, :].rearrange("p (s t) -> p s t", t=SEQ), q[:], kpad[:, :, w:w + SEQ],
                              ALU.mult).then_inc(s, 1)

        @block.vector
        def _(dve):
            def step(i, _):
                if live(i, 2, N):
                    g = i - 2
                    dve.wait_ge(s_sc, g + 1)
                    wait(dve, s_exp, g)
                    flat = score[:].rearrange("p j w h -> p j (w h)")
                    dve.tensor_tensor(flat, ps_score[:, 0:GT * WIN * AH].rearrange("p (j x) -> p j x", j=GT), maskb,
                                      ALU.add).then_inc(s_masked, 1)
                    dve.wait_ge(s_masked, g + 1)
                    dve.tensor_reduce(smax[:], score[:].rearrange("p j w h -> p j h w"), X_AXIS,
                                      ALU.max).then_inc(s_max, 1)
                    dve.wait_ge(s_max, g + 1)
                    dve.tensor_tensor(score[:], score[:], smax[:].unsqueeze(2).broadcast_to([P, GT, WIN, AH]),
                                      ALU.subtract).then_inc(s_sub, 1)
                if live(i, 3, N):
                    g = i - 3
                    dve.wait_ge(s_out, g + 1)
                    dve.wait_ge(s_bias, g + 1)
                    dve.tensor_tensor(group_rows(X, g), ps_out[:], group_rows(X, g), ALU.add).then_inc(s_res, 1)
                if live(i, 2, N):
                    g = i - 2
                    dve.wait_ge(s_exp, g + 1)
                    dve.tensor_reduce(ssum[:], prob[:].rearrange("p j w h -> p j h w"), X_AXIS,
                                      ALU.add).then_inc(s_sum, 1)
                    dve.wait_ge(s_sum, g + 1)
                    dve.reciprocal(sinv[:], ssum[:]).then_inc(s_inv, 1)
                    dve.wait_ge(s_inv, g + 1)
                    wait(dve, s_pturned, g)
                    dve.tensor_tensor(pnorm[:], prob[:], sinv[:].unsqueeze(2).broadcast_to([P, GT, WIN, AH]),
                                      ALU.mult).then_inc(s_pn, 1)
                if live(i, 1, N):
                    g = i - 1
                    dve.wait_ge(s_q, g + 1)
                    dve.wait_ge(s_k, g + 1)
                    wait(dve, s_sc, g)
                    for w in range(3):
                        window_product(dve, w, s_prod_d)
                if live(i, 0, N):
                    wait(dve, s_h, GT * i)
                    norm_stats(dve, nm, X, i)
                if live(i, 2, N):
                    g = i - 2
                    wait(dve, s_acc, 4 * g)
                    for w in range(WIN):
                        dve.wait_ge(s_spread, WIN * g + w + 1)
                        dve.tensor_tensor(pv[:, w, :].rearrange("p (s t) -> p s t", t=SEQ),
                                          ps_spread[:, w % 2, :].rearrange("p (s t) -> p s t", t=SEQ),
                                          vpad[:, bass.ds(g * GS, GS), w:w + SEQ], ALU.mult).then_inc(s_pv, 1)
                if live(i, 0, N):
                    wait(dve, s_turned, i)
                    norm_apply(dve, nm, lambda j: h[:, j, :], X, i, s_h)
            sweep(dve, N, LAG, 1, step)

        @block.gpsimd
        def _(pool):
            def step(i, _):
                if live(i, 1, N):
                    g = i - 1
                    pool.wait_ge(s_q, g + 1)
                    pool.wait_ge(s_k, g + 1)
                    wait(pool, s_sc, g)
                    for w in range(3, WIN):
                        window_product(pool, w, s_prod_p)
                    pool.wait_ge(s_h, GT * (g + 1))
                    pool.tensor_tensor(group_rows(X, g), group_rows(X, g),
                                       t["bo"][:].unsqueeze(1).broadcast_to([P, GT, D]), ALU.add).then_inc(s_bias, 1)
                if live(i, 2, N):
                    g = i - 2
                    wait(pool, s_out, g)
                    sums = [acc[:, 0, :], acc[:, 1, :], acc[:, 2, :], attnT[:, :]]
                    for w in range(1, WIN):
                        pool.wait_ge(s_pv, WIN * g + w + 1)
                        if w > 1:
                            pool.wait_ge(s_acc, 4 * g + w - 1)
                        pool.tensor_tensor(sums[w - 1], pv[:, 0, :] if w == 1 else sums[w - 2], pv[:, w, :],
                                           ALU.add).then_inc(s_acc, 1)
            sweep(pool, N, LAG, 1, step)


def mlstm(nc, t, dram):
    with ExitStack() as ctx:
        def sb(name, shape, dt=F32):
            return ctx.enter_context(nc.sbuf_tensor(name, shape, dt))

        def ps(name, shape):
            return ctx.enter_context(nc.psum_tensor(name, shape, F32))

        sem = Semaphores(nc)
        ctx.callback(sem.clear)

        X, Y, c = t["X"], t["Y"], t["c"]
        ctxpad, qdiag = t["ctxpad"], t["qdiag"]
        GH = GT * MH
        nm, ny = Norm(sb, sem, "bn"), Norm(sb, sem, "yn")
        h = sb("b_h", [P, GT, D])
        ctx_in = sb("b_ctx", [P, 2, GT, D])
        qT = sb("b_qT", [P, GN])
        cT = sb("b_cT", [P, 2, GN])
        gate = sb("b_gate", [P, GT, 2 * MH])
        fabs, fexp, fln = sb("b_fabs", [P, GT, MH]), sb("b_fexp", [P, GT, MH]), sb("b_fln", [P, GT, MH])
        logf = sb("b_logf", [P, GH])
        csum = sb("b_csum", [P, GH])
        u = sb("b_u", [P, 2, GH])
        umaxT = sb("b_umaxT", [GH, P])
        umax = sb("b_umax", [P, GH])
        negm = sb("b_negm", [P, GH])
        floor = sb("b_floor", [P, 2, GH])
        spread = sb("b_spread", [P, GH, SEQ])
        decay_log = sb("b_decay_log", [P, GH, SEQ])
        decay = sb("b_decay", [P, GH, SEQ])
        weight = sb("b_weight", [P, GH, SEQ])
        norm, norm_eps, inv = sb("b_norm", [P, GH]), sb("b_norm_eps", [P, GH]), sb("b_inv", [P, GH])
        ho, hsq, hn, hr = (sb(f"b_{n}", [P, GH, MHD]) for n in ("ho", "hsq", "hn", "hr"))
        ms, lms, rms = sb("b_ms", [P, GH]), sb("b_lms", [P, GH]), sb("b_rms", [P, GH])

        ps_turn = ps("b_ps_turn", [P, 2, GN])
        ps_small = ps("b_ps_small", [P, 512])
        ps_decay = ps("b_ps_decay", [P, 2, 512])
        ps_score = ps("b_ps_score", [P, 2, 512])
        G0, C0, U0, M0 = 0, 64, 128, 256

        s_ctx, s_pad = [sem("b_ctx_loaded0"), sem("b_ctx_loaded1")], sem("b_ctxpad_ready")
        s_h, s_turned, s_qT, s_cT, s_qdiag = (sem(f"b_{n}") for n in
                                              ("h_ready", "turned", "qT_ready", "cT_ready", "qdiag_ready"))
        s_gate, s_gsb, s_fabs, s_fexp, s_fln, s_logf = (sem(f"b_{n}") for n in
                                                        ("gates_done", "gates_ready", "fabs", "fexp", "fln", "logf"))
        s_cs, s_u, s_csum, s_uT, s_scan, s_mT, s_umax, s_negm, s_floor = (
            sem(f"b_{n}") for n in ("cs_done", "u_ready", "csum_ready", "uT_done", "scan_done", "umax_turned",
                                    "umax_ready", "negm_ready", "floor_ready"))
        s_spread, s_mbc, s_dlog, s_decay, s_st, s_weight, s_av = (
            sem(f"b_{n}") for n in ("spread_ready", "decay_log_done", "decay_log_ready", "decay_ready",
                                    "scores_done", "weights_ready", "output_done"))
        s_norm, s_neps, s_inv, s_ho, s_hsq, s_ms, s_lms, s_rms, s_hn, s_hr, s_x, s_y = (
            sem(f"b_{n}") for n in ("norm", "norm_eps", "inverse", "ho", "ho_squared", "meansquare", "log_ms",
                                    "rms", "hn_ready", "hr_ready", "x_updated", "y_ready"))
        s_apart, s_apart_pool = sem("b_apart"), sem("b_apart_pool")
        N, LAG = GROUPS, 3
        block = ctx.enter_context(nc.Block())

        @block.sync
        def _(sp):
            def step(i, par):
                if live(i, 0, N):
                    wait(sp, s_turned, i - 1)
                    wait(sp, s_pad, i - 1)
                    sp.dma_start(ctx_in[:, par, :, :], dram["ctx"].rearrange("(t p) f -> p t f", p=P)[
                        :, bass.ds(i * GT, GT), :]).then_inc(s_ctx[par], 16)
            sweep(sp, N, LAG, 2, step)

        def ctx_count(g, par):
            return 16 * (g // 2 + 1) if isinstance(g, int) else (g - par + 2) * 8

        @block.tensor
        def _(pe):
            def step(i, par):
                if live(i, 2, N):
                    g = i - 2
                    pe.wait_ge(s_spread, g + 1)
                    wait(pe, s_ho, g)
                    for b in range(2):
                        pe.matmul(ps_decay[:, b, :], c("sameseq"), spread[:, b * 8:(b + 1) * 8, :],
                                  start=True, stop=False)
                        mm = pe.matmul(ps_decay[:, b, :], t["ident16"][:], t["keyquery16"][:],
                                       start=False, stop=True)
                    mm.then_inc(s_mbc, 1)
                if live(i, 1, N):
                    g = i - 1
                    pe.wait_ge(s_h, GT * (g + 1))
                    pe.wait_ge(s_ctx[1 - par], ctx_count(g, 1 - par))
                    wait(pe, s_qdiag, 4 * g)
                    wait(pe, s_cT, g)
                    for j in range(GT):
                        pe.transpose(ps_turn[:, 0, j * P:(j + 1) * P], h[:, j, :], c("ident"))
                    for j in range(GT):
                        mm = pe.transpose(ps_turn[:, 1, j * P:(j + 1) * P], ctx_in[:, 1 - par, j, :], c("ident"))
                    mm.then_inc(s_turned, 1)
                if live(i, 2, N):
                    g = i - 2
                    wait(pe, s_weight, 2 * g)
                    for j in range(GT):
                        for s in range(2):
                            mm = pe.matmul(ps_score[s * SEQ:(s + 1) * SEQ, j // 2, (j % 2) * 256:(j % 2) * 256 + 256],
                                           cT[:, par, j * P + s * SEQ:j * P + (s + 1) * SEQ],
                                           qdiag[:, par, 2 * j + s, :, :], start=True, stop=True)
                        if j % 2:
                            mm.then_inc(s_st, 1)
                if live(i, 1, N):
                    g = i - 1
                    pe.wait_ge(s_qT, g + 1)
                    pe.wait_ge(s_cT, g + 1)
                    wait(pe, s_negm, g)
                    for j in range(GT):
                        at = G0 + j * 2 * MH
                        pe.matmul(ps_small[:, at:at + 2 * MH], qT[:, j * P:(j + 1) * P], t["gate_q"][:],
                                  start=True, stop=False)
                        mm = pe.matmul(ps_small[:, at:at + 2 * MH], cT[:, 1 - par, j * P:(j + 1) * P],
                                       t["gate_kv"][:], start=False, stop=True)
                    mm.then_inc(s_gate, 1)

                def output(tiles):
                    for j in tiles:
                        for hd in range(MH):
                            for s in range(2):
                                at = (j % 2) * MH * (MHD + 1) + hd * (MHD + 1)
                                mm = pe.matmul(ps_decay[s * SEQ:(s + 1) * SEQ, j // 2, at:at + MHD + 1],
                                               weight[s * SEQ:(s + 1) * SEQ, j * MH + hd, :],
                                               ctxpad[s * SEQ:(s + 1) * SEQ, par, j, hd, :], start=True, stop=True)
                    mm.then_inc(s_av, 1)

                if live(i, 2, N):
                    g = i - 2
                    pe.wait_ge(s_weight, 2 * (g + 1))
                    pe.wait_ge(s_pad, g + 1)
                    apart(pe, s_apart)
                    output((0, 1))
                if live(i, 1, N):
                    g = i - 1
                    pe.wait_ge(s_logf, g + 1)
                    pe.matmul(ps_small[:, C0:C0 + GH], c("tri"), logf[:], start=True, stop=True).then_inc(s_cs, 1)
                if live(i, 2, N):
                    output((2, 3))
                if live(i, 1, N):
                    g = i - 1
                    pe.wait_ge(s_u, g + 1)
                    pe.wait_ge(s_csum, g + 1)
                    pe.transpose(ps_small[0:GH, U0:U0 + P], u[:, 1 - par, :], c("ident")).then_inc(s_uT, 1)
                    pe.wait_ge(s_scan, g + 1)
                    apart(pe, s_apart)
                    pe.transpose(ps_small[:, M0:M0 + GH], umaxT[:], c("ident")[0:GH, 0:GH]).then_inc(s_mT, 1)
            sweep(pe, N, LAG, 2, step)

        @block.scalar
        def _(act):
            act.preload_act_table_set("natural_log_exp_and_others")
            eps, one = c("eps")[:, 0:1], c("eps")[:, 2:3]
            small_eps = c("eps")[:, 1:2]

            def step(i, par):
                if live(i, 2, N):
                    g = i - 2
                    act.wait_ge(s_dlog, 2 * (g + 1))
                    wait(act, s_weight, 2 * g)
                    act.activation(decay[:], decay_log[:], ACT.Exp).then_inc(s_decay, 1)
                if live(i, 1, N):
                    g = i - 1
                    act.wait_ge(s_turned, g + 1)
                    wait(act, s_gate, g)
                    act.activation(qT[:], ps_turn[:, 0, :], ACT.Copy).then_inc(s_qT, 1)
                    wait(act, s_st, 2 * (g - 1))
                    act.activation(cT[:, 1 - par, :], ps_turn[:, 1, :], ACT.Copy).then_inc(s_cT, 1)
                    for hd in range(MH):
                        rows = slice(hd * MHD, (hd + 1) * MHD)
                        act.activation(qdiag[rows, 1 - par, :, hd, :],
                                       ps_turn[rows, 0, :].rearrange("p (s t) -> p s t", t=SEQ),
                                       ACT.Copy).then_inc(s_qdiag, 1)
                    act.wait_ge(s_gsb, g + 1)
                    wait(act, s_logf, g)
                    act.activation(fabs[:], gate[:, :, MH:2 * MH], ACT.Abs).then_inc(s_fabs, 1)
                    act.wait_ge(s_fabs, g + 1)
                    act.activation(fexp[:], fabs[:], ACT.Exp, scale=-1.0).then_inc(s_fexp, 1)
                    act.wait_ge(s_fexp, g + 1)
                    act.activation(fln[:], fexp[:], ACT.Ln, bias=one).then_inc(s_fln, 1)
                if live(i, 0, N):
                    norm_rstd(act, nm, eps, i)
                if live(i, 2, N):
                    g = i - 2
                    act.wait_ge(s_ho, g + 1)
                    wait(act, s_ms, g)
                    act.activation(hsq[:], ho[:], ACT.Square).then_inc(s_hsq, 1)
                    act.wait_ge(s_ms, g + 1)
                    act.activation(lms[:], ms[:], ACT.Ln, bias=small_eps, scale=1.0 / MHD).then_inc(s_lms, 1)
                    act.wait_ge(s_lms, g + 1)
                    wait(act, s_hn, g)
                    act.activation(rms[:], lms[:], ACT.Exp, scale=-0.5).then_inc(s_rms, 1)
                if live(i, 1, N):
                    g = i - 1
                    act.wait_ge(s_negm, g + 1)
                    wait(act, s_norm, g - 1)
                    act.activation(floor[:, 1 - par, :], negm[:], ACT.Exp).then_inc(s_floor, 1)
                if live(i, 3, N):
                    norm_rstd(act, ny, eps, i - 3)
            sweep(act, N, LAG, 2, step)

        @block.vector
        def _(dve):
            def step(i, par):
                if live(i, 2, N):
                    g = i - 2
                    dve.wait_ge(s_mbc, g + 1)
                    wait(dve, s_decay, g)
                    for b in range(2):
                        dve.tensor_tensor(decay_log[:, b * 8:(b + 1) * 8, :],
                                          ps_decay[:, b, :].rearrange("p (x t) -> p x t", t=SEQ),
                                          u[:, par, b * 8:(b + 1) * 8].unsqueeze(2).broadcast_to([P, 8, SEQ]),
                                          ALU.add).then_inc(s_dlog, 1)
                if live(i, 0, N):
                    wait(dve, s_h, GT * i)
                    norm_stats(dve, nm, X, i)
                if live(i, 2, N):
                    g = i - 2
                    dve.wait_ge(s_decay, g + 1)
                    wait(dve, s_av, 2 * g)
                    for b in range(2):
                        dve.wait_ge(s_st, 2 * g + b + 1)
                        dve.scalar_tensor_tensor(out=weight[:, b * 8:(b + 1) * 8, :].rearrange("p x t -> p (x t)"),
                                                 in0=ps_score[:, b, :], scalar=float(MHD) ** -0.5,
                                                 in1=decay[:, b * 8:(b + 1) * 8, :].rearrange("p x t -> p (x t)"),
                                                 op0=ALU.mult, op1=ALU.mult).then_inc(s_weight, 1)
                if live(i, 1, N):
                    g = i - 1
                    dve.wait_ge(s_gate, g + 1)
                    wait(dve, s_u, g)
                    dve.tensor_tensor(gate[:], ps_small[:, G0:G0 + GT * 2 * MH].rearrange("p (j x) -> p j x", j=GT),
                                      t["gate_bias"][:].unsqueeze(1).broadcast_to([P, GT, 2 * MH]),
                                      ALU.add).then_inc(s_gsb, 1)
                    dve.wait_ge(s_fln, g + 1)
                    dve.wait_ge(s_gsb, g + 1)
                    wait(dve, s_cs, g)
                    dve.scalar_tensor_tensor(out=logf[:].rearrange("p (j x) -> p j x", j=GT),
                                             in0=gate[:, :, MH:2 * MH], scalar=0.0, in1=fln[:],
                                             op0=ALU.min, op1=ALU.subtract).then_inc(s_logf, 1)
                    dve.wait_ge(s_cs, g + 1)
                    dve.tensor_tensor(u[:, 1 - par, :].rearrange("p (j x) -> p j x", j=GT), gate[:, :, 0:MH],
                                      ps_small[:, C0:C0 + GH].rearrange("p (j x) -> p j x", j=GT),
                                      ALU.subtract).then_inc(s_u, 1)
                    wait(dve, s_negm, g)
                    dve.tensor_copy(csum[:], ps_small[:, C0:C0 + GH]).then_inc(s_csum, 1)
                    dve.wait_ge(s_uT, g + 1)
                    wait(dve, s_mT, g)
                    dve.tensor_tensor_scan(umaxT[:], c("seqstart")[0:GH, :], ps_small[0:GH, U0:U0 + P], 0.0,
                                           ALU.add, ALU.max).then_inc(s_scan, 1)
                    dve.wait_ge(s_mT, g + 1)
                    wait(dve, s_spread, g)
                    dve.tensor_copy(umax[:], ps_small[:, M0:M0 + GH]).then_inc(s_umax, 1)
                    dve.wait_ge(s_csum, g + 1)
                    wait(dve, s_floor, g)
                    dve.scalar_tensor_tensor(out=negm[:], in0=csum[:], scalar=-1.0, in1=ps_small[:, M0:M0 + GH],
                                             op0=ALU.mult, op1=ALU.subtract).then_inc(s_negm, 1)
                if live(i, 2, N):
                    g = i - 2
                    dve.wait_ge(s_av, 2 * (g + 1))
                    dve.wait_ge(s_floor, g + 1)
                    out = ps_decay[:, :, 0:2 * MH * (MHD + 1)].rearrange("p b (x d) -> p b x d", d=MHD + 1)
                    dve.tensor_tensor(norm[:].rearrange("p (b x) -> p b x", b=2), out[:, :, :, MHD],
                                      floor[:, par, :].rearrange("p (b x) -> p b x", b=2), ALU.max).then_inc(s_norm, 1)
                    dve.wait_ge(s_norm, g + 1)
                    dve.tensor_scalar(norm_eps[:], norm[:], 1e-6, None, ALU.add).then_inc(s_neps, 1)
                    dve.wait_ge(s_neps, g + 1)
                    dve.reciprocal(inv[:], norm_eps[:]).then_inc(s_inv, 1)
                    dve.wait_ge(s_inv, g + 1)
                    wait(dve, s_hn, g)
                    wait(dve, s_hsq, g)
                    dve.tensor_tensor(ho[:].rearrange("p (b x) d -> p b x d", b=2), out[:, :, :, 0:MHD],
                                      inv[:].rearrange("p (b x) -> p b x", b=2).unsqueeze(3).broadcast_to(
                                          [P, 2, 8, MHD]), ALU.mult).then_inc(s_ho, 1)
                if live(i, 0, N):
                    wait(dve, s_turned, i)
                    norm_apply(dve, nm, lambda j: h[:, j, :], X, i, s_h)
                if live(i, 2, N):
                    g = i - 2
                    dve.wait_ge(s_hsq, g + 1)
                    wait(dve, s_lms, g)
                    dve.tensor_reduce(ms[:], hsq[:], X_AXIS, ALU.add).then_inc(s_ms, 1)
                if live(i, 3, N):
                    g = i - 3
                    dve.wait_ge(s_x, g + 1)
                    wait(dve, s_y, GT * g)
                    norm_stats(dve, ny, X, g)
                if live(i, 2, N):
                    g = i - 2
                    dve.wait_ge(s_rms, g + 1)
                    wait(dve, s_hr, g)
                    dve.tensor_tensor(hn[:], ho[:], rms[:].unsqueeze(2).broadcast_to([P, GH, MHD]),
                                      ALU.mult).then_inc(s_hn, 1)
                if live(i, 3, N):
                    g = i - 3
                    norm_apply(dve, ny, lambda j: Y[:, g * GT + j, :], X, g, s_y)
            sweep(dve, N, LAG, 2, step)

        @block.gpsimd
        def _(pool):
            def step(i, par):
                if live(i, 1, N):
                    g = i - 1
                    pool.wait_ge(s_ctx[1 - par], ctx_count(g, 1 - par))
                    wait(pool, s_av, 2 * (g - 1))
                    apart(pool, s_apart_pool)
                    pool.tensor_scalar(ctxpad[:, 1 - par, :, :, 0:MHD],
                                       ctx_in[:, 1 - par, :, :].rearrange("p j (h d) -> p j h d", d=MHD),
                                       1.0, None, ALU.mult).then_inc(s_pad, 1)
                    pool.wait_ge(s_umax, g + 1)
                    wait(pool, s_mbc, g)
                    pool.tensor_tensor(spread[:], c("negfold").unsqueeze(1).broadcast_to([P, GH, SEQ]),
                                       umax[:].unsqueeze(2).broadcast_to([P, GH, SEQ]), ALU.mult).then_inc(s_spread, 1)
                if live(i, 2, N):
                    g = i - 2
                    pool.wait_ge(s_hn, g + 1)
                    wait(pool, s_x, g)
                    pool.tensor_tensor(hr[:], hn[:], t["rms1"][:].unsqueeze(1).broadcast_to([P, GH, MHD]),
                                       ALU.mult).then_inc(s_hr, 1)
                    pool.wait_ge(s_hr, g + 1)
                    pool.tensor_tensor(group_rows(X, g), group_rows(X, g),
                                       hr[:].rearrange("p (j h) d -> p j (h d)", j=GT), ALU.add).then_inc(s_x, 1)
            sweep(pool, N, LAG, 2, step)


def causal_attention(nc, t, layer):
    with ExitStack() as ctx:
        def sb(name, shape, dt=F32):
            return ctx.enter_context(nc.sbuf_tensor(f"c{layer}_{name}", shape, dt))

        def ps(name, shape):
            return ctx.enter_context(nc.psum_tensor(f"c{layer}_{name}", shape, F32))

        phase_sems = Semaphores(nc)
        ctx.callback(phase_sems.clear)

        def sem(name):
            return phase_sems(f"c{layer}_{name}")

        Y, c = t["Y"], t["c"]
        wqkv, wo, qks = t["wqkv"][layer], t["lwo"][layer], t["qks"][layer]
        HT = LHD // 2
        w_hi, w_lo = sb("w_hi", [P, 3 * INNER], F32R), sb("w_lo", [P, 3 * INNER], F32R)
        costab, sintab = sb("costab", [P, 2, LHD]), sb("sintab", [P, 2, LHD])
        xin = sb("xin", [P, D])
        xT = sb("xT", [P, P])
        x_hi, x_lo = sb("x_hi", [P, P], F32R), sb("x_lo", [P, P], F32R)
        qk = sb("qk", [P, 2 * LH, LHD])
        sq = sb("sq", [P, 2 * LH, LHD])
        rcos, rsin = sb("rcos", [P, 2 * LH, LHD]), sb("rsin", [P, 2 * LH, LHD])
        rsum, rot = sb("rsum", [P, 2 * LH, LHD]), sb("rot", [P, 2 * LH, LHD])
        ss, ssc, lss, inv = (sb(n, [P, 2 * LH]) for n in ("ss", "ssc", "lss", "inv"))
        v = sb("v", [P, 2, INNER])
        qkT = sb("qkT", [P, 2 * LH // 2, P])
        smax, ssum, sinv = (sb(n, [P, LH]) for n in ("smax", "ssum", "sinv"))
        score, prob, pnorm = (sb(n, [P, LH, SEQ]) for n in ("score", "prob", "pnorm"))
        pT = sb("pT", [P, INNER])
        oT = sb("oT", [P, LH // 2, P])

        ps_qkv = ps("ps_qkv", [P, 3, INNER])
        ps_qkT = ps("ps_qkT", [P, 2, 512])
        ps_score = ps("ps_score", [P, 512])
        ps_o0 = ps("ps_o0", [P, 512])
        ps_o1 = ps("ps_o1", [P, 512])
        ps_y, ps_xT = ps_o0[:, 384:512], ps_o1[:, 384:512]

        s_tab, s_whi, s_wlo, s_zero = sem("tables_ready"), sem("w_hi_ready"), sem("w_lo_ready"), sem("xT_zeroed")
        s_xin, s_xturned, s_xT, s_xhi, s_xlo = (sem(n) for n in ("xin_ready", "x_turned", "xT_ready", "x_hi_ready",
                                                                 "x_lo_ready"))
        s_qkv, s_qk, s_v, s_sq, s_rcos, s_rsin = (sem(n) for n in ("qkv_done", "qk_ready", "v_ready", "sq_ready",
                                                                   "rcos_ready", "rsin_ready"))
        s_ss, s_ssc, s_lss, s_inv, s_rsum, s_rot = (sem(n) for n in ("ss_ready", "ss_clipped", "log_ss", "inv_ready",
                                                                     "rsum_ready", "rot_ready"))
        s_rturned, s_qkT, s_sc, s_max, s_sub, s_exp = (sem(n) for n in ("rot_turned", "qkT_ready", "scores_done",
                                                                        "max_ready", "shifted", "exp_ready"))
        s_sum, s_sinv, s_pn, s_pturned, s_pT, s_av, s_oT, s_y, s_res = (
            sem(n) for n in ("sum_ready", "sum_inverse", "probs_ready", "probs_turned", "pT_ready", "output_done",
                             "oT_ready", "y_done", "residual_done"))
        s_apart = sem("apart")
        N, LAG = TILES, 3
        block = ctx.enter_context(nc.Block())

        @block.tensor
        def _(pe):
            pe.wait_ge(s_whi, 1)
            pe.wait_ge(s_wlo, 1)

            def step(i, par):
                if live(i, 1, N):
                    g = i - 1
                    pe.wait_ge(s_xlo, g + 1)
                    for n in range(3):
                        wait(pe, s_qk if n < 2 else s_v, 2 * (g - 1) + n + 1 if n < 2 else g)
                        cols = slice(n * INNER, (n + 1) * INNER)
                        pe.matmul(ps_qkv[:, n, :], x_hi[:], w_hi[:, cols], start=True, stop=False)
                        pe.matmul(ps_qkv[:, n, :], x_hi[:], w_lo[:, cols], start=False, stop=False)
                        pe.matmul(ps_qkv[:, n, :], x_lo[:], w_hi[:, cols], start=False,
                                  stop=True).then_inc(s_qkv, 1)
                if live(i, 3, N):
                    g = i - 3
                    pe.wait_ge(s_pn, g + 1)
                    for x in range(LH // 2):
                        mm = pe.transpose(ps_score[:, x * P:(x + 1) * P],
                                          pnorm[:, 2 * x:2 * x + 2, :].rearrange("p s k -> p (s k)"), c("ident"))
                    mm.then_inc(s_pturned, 1)
                if live(i, 2, N):
                    g = i - 2
                    pe.wait_ge(s_rot, g + 1)
                    wait(pe, s_qkT, 2 * g)
                    for x in range(LH):
                        mm = pe.transpose(ps_qkT[:, x // 4, (x % 4) * P:(x % 4 + 1) * P],
                                          rot[:, 2 * x:2 * x + 2, :].rearrange("p s k -> p (s k)"), c("ident"))
                        if x % 4 == 3:
                            mm.then_inc(s_rturned, 1)
                if live(i, 3, N):
                    g = i - 3
                    pe.wait_ge(s_pT, g + 1)
                    pe.wait_ge(s_v, g + 1)
                    wait(pe, s_res, g)
                    apart(pe, s_apart)
                    for x in range(LH // 2):
                        for s, bank in ((0, ps_o0), (1, ps_o1)):
                            for e in range(2):
                                mm = pe.matmul(bank[e * LHD:(e + 1) * LHD, x * SEQ:(x + 1) * SEQ],
                                               v[s * SEQ:(s + 1) * SEQ, (1 - par),
                                                 (2 * x + e) * LHD:(2 * x + e + 1) * LHD],
                                               pT[s * SEQ:(s + 1) * SEQ, x * P + e * SEQ:x * P + (e + 1) * SEQ],
                                               start=True, stop=True)
                    mm.then_inc(s_av, 1)
                if live(i, 2, N):
                    g = i - 2
                    pe.wait_ge(s_qkT, 2 * (g + 1))
                    if live(i, 3, N):
                        pe.wait_ge(s_pT, g)
                    elif not isinstance(i, int) or i < 3:
                        pass
                    pe.matmul(ps_score[:], t["ident16"][:], t["causal16"][:], start=True, stop=False,
                              skip_group_check=True)
                    for x in range(LH // 2):
                        for s in range(2):
                            for e in range(2):
                                mm = pe.matmul(ps_score[e * SEQ:(e + 1) * SEQ, x * P + s * SEQ:x * P + (s + 1) * SEQ],
                                               qkT[e * LHD:(e + 1) * LHD, x, s * SEQ:(s + 1) * SEQ],
                                               qkT[e * LHD:(e + 1) * LHD, LH // 2 + x, s * SEQ:(s + 1) * SEQ],
                                               start=False, stop=True, skip_group_check=True)
                    mm.then_inc(s_sc, 1)
                if live(i, 0, N):
                    pe.wait_ge(s_xin, i + 1)
                    if live(i, 3, N):
                        pe.wait_ge(s_oT, 2 * (i - 2))
                    pe.transpose(ps_xT, xin[:], c("ident")).then_inc(s_xturned, 1)
                if live(i, 3, N):
                    g = i - 3
                    pe.wait_ge(s_oT, 2 * (g + 1))
                    for x in range(LH // 2):
                        mm = pe.matmul(ps_y, oT[:, x, :], wo[:, x, :], start=(x == 0), stop=(x == LH // 2 - 1))
                    mm.then_inc(s_y, 1)
            sweep(pe, N, LAG, 2, step)

        @block.scalar
        def _(act):
            act.preload_act_table_set("natural_log_exp_and_others")
            act.wait_ge(s_zero, 1)

            def step(i, par):
                if live(i, 1, N):
                    g = i - 1
                    wait(act, s_rcos, g)
                    wait(act, s_rsin, 2 * g)
                    for n in range(2):
                        act.wait_ge(s_qkv, 3 * g + n + 1)
                        act.activation(qk[:, n * LH:(n + 1) * LH, :].rearrange("p h d -> p (h d)"), ps_qkv[:, n, :],
                                       ACT.Copy).then_inc(s_qk, 1)
                    act.wait_ge(s_qk, 2 * (g + 1))
                    wait(act, s_ss, g)
                    act.activation(sq[:], qk[:], ACT.Square).then_inc(s_sq, 1)
                if live(i, 3, N):
                    g = i - 3
                    act.wait_ge(s_pturned, g + 1)
                    act.activation(pT[:], ps_score[:], ACT.Copy).then_inc(s_pT, 1)
                if live(i, 2, N):
                    g = i - 2
                    wait(act, s_sc, g)
                    for n in range(2):
                        act.wait_ge(s_rturned, 2 * g + n + 1)
                        act.activation(qkT[:, 4 * n:4 * n + 4, :].rearrange("p x t -> p (x t)"), ps_qkT[:, n, :],
                                       ACT.Copy).then_inc(s_qkT, 1)
                if live(i, 3, N):
                    g = i - 3
                    act.wait_ge(s_av, g + 1)
                    wait(act, s_y, g)
                    for s, bank in ((0, ps_o0), (1, ps_o1)):
                        act.activation(oT[:, :, s * SEQ:(s + 1) * SEQ],
                                       bank[:, 0:LH // 2 * SEQ].rearrange("p (x t) -> p x t", t=SEQ),
                                       ACT.Copy).then_inc(s_oT, 1)
                if live(i, 1, N):
                    g = i - 1
                    act.wait_ge(s_qkv, 3 * (g + 1))
                    act.activation(v[:, 1 - par, :], ps_qkv[:, 2, :], ACT.Copy).then_inc(s_v, 1)
                if live(i, 0, N):
                    act.wait_ge(s_xturned, i + 1)
                    wait(act, s_xlo, i)
                    act.activation(xT[0:D // 2, :], ps_xT[0:D // 2, :], ACT.Copy).then_inc(s_xT, 1)
                    act.activation(xT[D // 2:D, :].rearrange("p (s t) -> p s t", t=SEQ)[:, :, 1:SEQ],
                                   ps_xT[D // 2:D, :].rearrange("p (s t) -> p s t", t=SEQ)[:, :, 0:SEQ - 1],
                                   ACT.Copy).then_inc(s_xT, 1)
                if live(i, 1, N):
                    g = i - 1
                    act.wait_ge(s_ssc, g + 1)
                    act.activation(lss[:], ssc[:], ACT.Ln).then_inc(s_lss, 1)
                    act.wait_ge(s_lss, g + 1)
                    wait(act, s_rot, g)
                    act.activation(inv[:], lss[:], ACT.Exp, scale=-0.5).then_inc(s_inv, 1)
                if live(i, 2, N):
                    g = i - 2
                    act.wait_ge(s_sub, g + 1)
                    wait(act, s_pn, g)
                    act.activation(prob[:], score[:], ACT.Exp, scale=8.0).then_inc(s_exp, 1)
            sweep(act, N, LAG, 2, step)

        @block.vector
        def _(dve):
            cos, sin = c("rot")[:, 0:2 * LHD], c("rot")[:, 2 * LHD:4 * LHD]
            two = lambda a: a.rearrange("p (n d) -> p n d", d=LHD)
            dve.wait_ge(t["s_layers"], t["layers_loaded"])
            dve.tensor_tensor(costab[:], two(cos), qks[:], ALU.mult).then_inc(s_tab, 1)
            dve.tensor_tensor(sintab[:, :, 0:HT], two(sin)[:, :, 0:HT], qks[:, :, HT:LHD], ALU.mult).then_inc(s_tab, 1)
            dve.tensor_tensor(sintab[:, :, HT:LHD], two(sin)[:, :, HT:LHD], qks[:, :, 0:HT],
                              ALU.mult).then_inc(s_tab, 1)
            dve.memset(xT[:], 0.0).then_inc(s_zero, 1)
            dve.tensor_copy(w_hi[:], wqkv[:]).then_inc(s_whi, 1)
            dve.wait_ge(s_whi, 1)
            dve.tensor_tensor(w_lo[:], wqkv[:], w_hi[:].bitcast(F32), ALU.subtract).then_inc(s_wlo, 1)
            dve.wait_ge(s_tab, 3)

            def step(i, par):
                if live(i, 3, N):
                    g = i - 3
                    dve.wait_ge(s_exp, g + 1)
                    dve.tensor_reduce(ssum[:], prob[:], X_AXIS, ALU.add).then_inc(s_sum, 1)
                    dve.wait_ge(s_sum, g + 1)
                    wait(dve, s_pn, g)
                    dve.reciprocal(sinv[:], ssum[:]).then_inc(s_sinv, 1)
                if live(i, 1, N):
                    g = i - 1
                    dve.wait_ge(s_qk, 2 * (g + 1))
                    wait(dve, s_rsum, g)
                    heads = lambda a: a.rearrange("p (n h) d -> p n h d", n=2)
                    tab = lambda a: a.unsqueeze(2).broadcast_to([P, 2, LH, a.shape[-1]])
                    dve.tensor_tensor(heads(rcos[:]), heads(qk[:]), tab(costab[:]), ALU.mult).then_inc(s_rcos, 1)
                    for lo, hi in ((0, HT), (HT, 0)):
                        dve.tensor_tensor(heads(rsin[:])[:, :, :, lo:lo + HT], heads(qk[:])[:, :, :, hi:hi + HT],
                                          tab(sintab[:, :, lo:lo + HT]), ALU.mult).then_inc(s_rsin, 1)
                    dve.wait_ge(s_sq, g + 1)
                    dve.tensor_reduce(ss[:], sq[:], X_AXIS, ALU.add).then_inc(s_ss, 1)
                    dve.wait_ge(s_ss, g + 1)
                    wait(dve, s_lss, g)
                    dve.tensor_scalar(ssc[:], ss[:], 1e-24, None, ALU.max).then_inc(s_ssc, 1)
                if live(i, 2, N):
                    g = i - 2
                    dve.wait_ge(s_sc, g + 1)
                    flat = ps_score[:].rearrange("p (h k) -> p h k", k=SEQ)
                    dve.tensor_reduce(smax[:], flat, X_AXIS, ALU.max).then_inc(s_max, 1)
                    dve.wait_ge(s_max, g + 1)
                    wait(dve, s_exp, g)
                    dve.tensor_tensor(score[:], flat, smax[:].unsqueeze(2).broadcast_to([P, LH, SEQ]),
                                      ALU.subtract).then_inc(s_sub, 1)
                if live(i, 0, N):
                    dve.wait_ge(s_xT, 2 * (i + 1))
                    wait(dve, s_qkv, 3 * i)
                    dve.tensor_copy(x_hi[:], xT[:]).then_inc(s_xhi, 1)
                    dve.wait_ge(s_xhi, i + 1)
                    dve.tensor_tensor(x_lo[:], xT[:], x_hi[:].bitcast(F32), ALU.subtract).then_inc(s_xlo, 1)
                if live(i, 3, N):
                    g = i - 3
                    dve.wait_ge(s_y, g + 1)
                    dve.tensor_tensor(Y[:, g, :], ps_y, Y[:, g, :], ALU.add).then_inc(s_res, 1)
            sweep(dve, N, LAG, 2, step)

        @block.gpsimd
        def _(pool):
            def step(i, par):
                if live(i, 3, N):
                    g = i - 3
                    pool.wait_ge(s_sinv, g + 1)
                    wait(pool, s_pturned, g)
                    pool.tensor_tensor(pnorm[:], prob[:], sinv[:].unsqueeze(2).broadcast_to([P, LH, SEQ]),
                                       ALU.mult).then_inc(s_pn, 1)
                if live(i, 0, N):
                    wait(pool, s_xturned, i)
                    pool.tensor_copy(xin[:], Y[:, i, :]).then_inc(s_xin, 1)
                if live(i, 1, N):
                    g = i - 1
                    pool.wait_ge(s_rcos, g + 1)
                    pool.wait_ge(s_rsin, 2 * (g + 1))
                    wait(pool, s_rot, g)
                    pool.tensor_tensor(rsum[:], rcos[:], rsin[:], ALU.add).then_inc(s_rsum, 1)
                    pool.wait_ge(s_rsum, g + 1)
                    pool.wait_ge(s_inv, g + 1)
                    wait(pool, s_rturned, 2 * g)
                    pool.tensor_tensor(rot[:], rsum[:], inv[:].unsqueeze(2).broadcast_to([P, 2 * LH, LHD]),
                                       ALU.mult).then_inc(s_rot, 1)
            sweep(pool, N, LAG, 2, step)


def gated_ffn(nc, t, dram, layer):
    last = layer == DEPTH - 1
    with ExitStack() as ctx:
        def sb(name, shape, dt=F32):
            return ctx.enter_context(nc.sbuf_tensor(f"f{layer}_{name}", shape, dt))

        def ps(name, shape):
            return ctx.enter_context(nc.psum_tensor(f"f{layer}_{name}", shape, F32))

        phase_sems = Semaphores(nc)
        ctx.callback(phase_sems.clear)

        def sem(name):
            return phase_sems(f"f{layer}_{name}")

        X, Y, c = t["X"], t["Y"], t["c"]
        w1, w2, cols, b2 = t["w1"][layer], t["w2"][layer], t["ffncols"][layer], t["b2"][layer]
        H2 = D // 2
        nm = Norm(sb, sem, "n")
        w_hi, w_lo = sb("w_hi", [P, 2 * HID], F32R), sb("w_lo", [P, 2 * HID], F32R)
        h = sb("h", [P, GT, D])
        hT = sb("hT", [P, GN])
        h_hi, h_lo = sb("h_hi", [P, GN], F32R), sb("h_lo", [P, GN], F32R)
        gelu = sb("gelu", [P, 2, GN])
        act_in = sb("gated", [P, 3, GN])

        ps_shift = ps("ps_shift", [P, 512])
        ps_turn = ps("ps_turn", [P, GN])
        ps_a = ps("ps_a", [P, 2, GN])
        ps_g = ps("ps_g", [P, 2, GN])
        ps_out = ps("ps_out", [P, GT, D])

        s_whi, s_wlo = sem("w_hi_ready"), sem("w_lo_ready")
        s_shift, s_h, s_turned, s_hT, s_hhi, s_hlo = (sem(n) for n in ("shifted", "h_ready", "h_turned", "hT_ready",
                                                                       "h_hi_ready", "h_lo_ready"))
        s_a, s_g, s_gelu, s_gated, s_out, s_bias, s_bias2, s_res = (
            sem(n) for n in ("a_done", "g_done", "gelu_ready", "gated_ready", "out_done", "bias_added", "x_added",
                             "residual_done"))
        s_store = sem("stored")
        N, LAG = GROUPS, 2
        NCH = len(HCH)
        block = ctx.enter_context(nc.Block())

        if last:
            @block.sync
            def _(sp):
                def step(i, _):
                    if live(i, 2, N):
                        g = i - 2
                        sp.wait_ge(s_res, g + 1)
                        dst = dram["out"].rearrange("(t p) f -> p t f", p=P)
                        sp.dma_start(dst[:, bass.ds(g * GT, GT), :], group_rows(Y, g)).then_inc(s_store, 16)
                sweep(sp, N, LAG, 1, step)
                sp.wait_ge(s_store, 16 * N)

        @block.tensor
        def _(pe):
            pe.wait_ge(s_whi, 1)
            pe.wait_ge(s_wlo, 1)

            def step(i, _):
                if live(i, 1, N):
                    g = i - 1
                    pe.wait_ge(s_h, 2 * GT * (g + 1))
                    wait(pe, s_hT, g)
                    for j in range(GT):
                        mm = pe.transpose(ps_turn[:, j * P:(j + 1) * P], h[:, j, :], c("ident"))
                    mm.then_inc(s_turned, 1)
                if live(i, 2, N):
                    g = i - 2
                    pe.wait_ge(s_gated, NCH * (g + 1))
                    wait(pe, s_res, g)
                    for j in range(GT):
                        for n, m in enumerate(HCH):
                            mm = pe.matmul(ps_out[:, j, :], act_in[0:m, n, j * P:(j + 1) * P], w2[0:m, n, :],
                                           start=(n == 0), stop=(n == NCH - 1))
                    mm.then_inc(s_out, 1)
                if live(i, 1, N):
                    g = i - 1
                    pe.wait_ge(s_hlo, g + 1)
                    for n, m in enumerate(HCH):
                        for bank, at, done, used in ((ps_g, HID, s_g, s_gelu), (ps_a, 0, s_a, s_gated)):
                            wait(pe, used, NCH * g + max(n - 1, 0))
                            part = slice(at + n * P, at + n * P + m)
                            out = bank[0:m, n % 2, :]
                            pe.matmul(out, w_hi[:, part], h_hi[:], start=True, stop=False)
                            pe.matmul(out, w_hi[:, part], h_lo[:], start=False, stop=False)
                            pe.matmul(out, w_lo[:, part], h_hi[:], start=False, stop=True).then_inc(done, 1)
                if live(i, 0, N):
                    wait(pe, s_h, 2 * GT * i)
                    pe.matmul(ps_shift[:, 0:GT * H2], c("shift"), Y[:, bass.ds(i * GT, GT), H2:D],
                              start=True, stop=True).then_inc(s_shift, 1)
            sweep(pe, N, LAG, 1, step)

        @block.scalar
        def _(act):
            def step(i, _):
                if live(i, 1, N):
                    g = i - 1
                    act.wait_ge(s_turned, g + 1)
                    wait(act, s_hlo, g)
                    act.activation(hT[:], ps_turn[:], ACT.Identity, bias=cols[:, 7:8],
                                   scale=cols[:, 6:7]).then_inc(s_hT, 1)
                    for n, m in enumerate(HCH):
                        act.wait_ge(s_g, NCH * g + n + 1)
                        wait(act, s_gated, NCH * g + max(n - 1, 0))
                        act.activation(gelu[0:m, n % 2, :], ps_g[0:m, n % 2, :], ACT.Gelu,
                                       bias=cols[0:m, 3 + n:4 + n]).then_inc(s_gelu, 1)
                if live(i, 0, N):
                    act.preload_act_table_set("natural_log_exp_and_others")
                    norm_rstd(act, nm, c("eps")[:, 0:1], i)
            sweep(act, N, LAG, 1, step)

        @block.vector
        def _(dve):
            dve.tensor_copy(w_hi[:], w1[:]).then_inc(s_whi, 1)
            dve.wait_ge(s_whi, 1)
            dve.tensor_tensor(w_lo[:], w1[:], w_hi[:].bitcast(F32), ALU.subtract).then_inc(s_wlo, 1)

            def step(i, _):
                if live(i, 1, N):
                    g = i - 1
                    dve.wait_ge(s_hT, g + 1)
                    wait(dve, s_a, NCH * g)
                    dve.tensor_copy(h_hi[:], hT[:]).then_inc(s_hhi, 1)
                    dve.wait_ge(s_hhi, g + 1)
                    dve.tensor_tensor(h_lo[:], hT[:], h_hi[:].bitcast(F32), ALU.subtract).then_inc(s_hlo, 1)
                if live(i, 2, N):
                    g = i - 2
                    dve.wait_ge(s_out, g + 1)
                    dve.wait_ge(s_bias2 if last else s_bias, g + 1)
                    dve.tensor_tensor(group_rows(Y, g), ps_out[:], group_rows(Y, g), ALU.add).then_inc(s_res, 1)
                if live(i, 1, N):
                    g = i - 1
                    wait(dve, s_out, g)
                    for n, m in enumerate(HCH):
                        dve.wait_ge(s_a, NCH * g + n + 1)
                        dve.wait_ge(s_gelu, NCH * g + n + 1)
                        dve.scalar_tensor_tensor(out=act_in[0:m, n, :], in0=ps_a[0:m, n % 2, :],
                                                 scalar=cols[0:m, n:n + 1], in1=gelu[0:m, n % 2, :],
                                                 op0=ALU.add, op1=ALU.mult).then_inc(s_gated, 1)
                if live(i, 0, N):
                    wait(dve, s_h, 2 * GT * i)
                    dve.wait_ge(s_shift, i + 1)
                    for j in range(GT):
                        dve.bn_stats(nm.stats[:, j, 0:6], Y[:, i * GT + j, 0:H2]).then_inc(nm.s_stats, 1)
                        dve.bn_stats(nm.stats[:, j, 6:12], ps_shift[:, j * H2:(j + 1) * H2]).then_inc(nm.s_stats, 1)
                    dve.wait_ge(nm.s_stats, 2 * GT * (i + 1))
                    apart(dve, nm.s_apart)
                    for j in range(GT):
                        dve.bn_aggr(nm.meanvar[:, j, :], nm.stats[:, j, :]).then_inc(nm.s_meanvar, 1)
                    dve.wait_ge(nm.s_rstd, i + 1)
                    wait(dve, s_turned, i)
                    for j in range(GT):
                        for half, src in ((0, Y[:, i * GT + j, 0:H2]), (1, ps_shift[:, j * H2:(j + 1) * H2])):
                            dve.tensor_scalar(h[:, j, half * H2:(half + 1) * H2], src, nm.meanvar[:, j, 0:1],
                                              nm.rstd[:, j:j + 1], ALU.subtract, ALU.mult).then_inc(s_h, 1)
            sweep(dve, N, LAG, 1, step)

        @block.gpsimd
        def _(pool):
            def step(i, _):
                if live(i, 1, N):
                    g = i - 1
                    pool.wait_ge(s_h, 2 * GT * (g + 1))
                    pool.tensor_tensor(group_rows(Y, g), group_rows(Y, g),
                                       b2[:].unsqueeze(1).broadcast_to([P, GT, D]), ALU.add).then_inc(s_bias, 1)
                    if last:
                        pool.wait_ge(s_bias, g + 1)
                        pool.tensor_tensor(group_rows(Y, g), group_rows(Y, g), group_rows(X, g),
                                           ALU.add).then_inc(s_bias2, 1)
            sweep(pool, N, LAG, 1, step)


def build(nc, dram):
    with ExitStack() as ctx:
        def sb(name, shape, dt=F32):
            return ctx.enter_context(nc.sbuf_tensor(name, shape, dt))

        t = {"const": sb("const", [P, NCONST]), "X": sb("X", [P, TILES, D])}
        t["c"] = lambda name: t["const"][:, CONSTS[name][0]:CONSTS[name][1]]
        for name in ("wq", "wk", "wv", "wo"):
            t[name] = sb(name, [P, D])
        t["abias"] = sb("abias", [P, 3])
        t["bo"] = sb("bo", [P, D])
        t["winspread"] = sb("winspread", [WIN * AH, WIN, P])
        for name in ("gate_q", "gate_k", "gate_v", "gate_kv", "gate_bias"):
            t[name] = sb(name, [P, 2 * MH])
        t["rms"] = sb("rms", [P, MHD])
        t["kpad"] = sb("kpad", [P, GS, PADSEQ])
        t["vpad"] = sb("vpad", [P, NSEQ, PADSEQ])
        t["ctxpad"] = sb("ctxpad", [P, 2, GT, MH, MHD + 1])
        t["qdiag"] = sb("qdiag", [P, 2, GS, MH, SEQ])
        t["ident16"] = sb("ident16", [P, P], BF16)
        t["causal16"] = sb("causal16", [P, 8, SEQ], BF16)
        t["keyquery16"] = sb("keyquery16", [P, 8, SEQ], BF16)
        t["Y"] = sb("Y", [P, TILES, D])
        t["rms1"] = sb("rms1", [P, MHD])
        for name, shape in (("wqkv", [P, 3 * INNER]), ("lwo", [P, LH // 2, D]), ("qks", [P, 2, LHD]),
                            ("w1", [P, 2 * HID]), ("w2", [P, len(HCH), D]), ("ffncols", [P, 8]), ("b2", [P, D])):
            t[name] = [sb(f"{name}{layer}", shape) for layer in range(DEPTH)]
        t["s_layers"] = ctx.enter_context(nc.semaphore("layer_weights_loaded"))
        load_phase(nc, t, dram)
        window_attention(nc, t)
        mlstm(nc, t, dram)
        for layer in range(DEPTH):
            causal_attention(nc, t, layer)
            gated_ffn(nc, t, dram, layer)


def shape_constants():
    p = np.arange(P)
    tok = p % SEQ
    out = np.zeros((P, NCONST), np.float32)

    def put(name, a):
        out[:, CONSTS[name][0]:CONSTS[name][1]] = a
    same = (p[:, None] // SEQ) == (p[None, :] // SEQ)
    put("ident", np.eye(P))
    put("headsum", p[:, None] // AHD == np.arange(AH)[None, :])
    place = tok[:, None] + np.arange(WIN)[None, :] - HALF
    put("winmask", np.repeat(np.where((place >= 0) & (place < SEQ), 0.0, NEG), AH, axis=1))
    put("causal", np.where(np.arange(SEQ)[None, :] > tok[:, None], NEG, 0.0))
    put("keyquery", np.where(np.arange(SEQ)[None, :] < tok[:, None], NEG, 0.0))
    put("tri", same & (p[:, None] <= p[None, :]))
    put("negfold", -(tok[:, None] == np.arange(SEQ)[None, :]).astype(np.float32))
    put("sameseq", same)
    put("shift", same & (p[:, None] + 1 == p[None, :]))
    put("eps", np.tile(np.array([LN_EPS, 1e-6, 1.0, 0.0], np.float32), (P, 1)))
    put("seqstart", np.where(p[None, :] % SEQ == 0, NEG, 0.0) * np.ones((P, 1)))
    half = np.arange(0, LHD, 2, dtype=np.float32)
    freq = np.arange(SEQ, dtype=np.float32)[:, None] * (np.float32(1.0) / np.float32(10000.0) ** (half / LHD))[None, :]
    freq = np.concatenate([freq, freq], -1)
    base = (half + np.float32(0.4 * LHD)) / np.float32(1.4 * LHD)
    power = (np.arange(SEQ, dtype=np.float32) - SEQ // 2) / np.float32(32.0)
    scale = base[None, :] ** power[:, None]
    scale = np.concatenate([scale, scale], -1)
    sign = np.where(np.arange(LHD) < LHD // 2, -1.0, 1.0).astype(np.float32)
    cos, sin = np.cos(freq), np.sin(freq) * sign
    put("rot", np.tile(np.concatenate([cos * scale, cos / scale, sin * scale, sin / scale], 1), (2, 1)))
    spread = np.zeros((WIN, AH, WIN, P), np.float32)
    for w in range(WIN):
        spread[w, :, w, :] = np.arange(AH)[:, None] == p[None, :] // AHD
    return out, spread.reshape(WIN * AH, WIN, P)


def kernel(**inputs):
    import concourse.bacc as bacc
    from concourse.bass_utils import run_bass_kernel_spmd

    def arr(name):
        return np.asarray(inputs[name])

    def rows(a):
        return np.ascontiguousarray(np.broadcast_to(np.asarray(a).reshape(1, -1), (P, np.asarray(a).size)))

    const, spread = shape_constants()
    ins = {
        "x": arr("x").reshape(TOKENS, D), "ctx": arr("ctx_1024").reshape(TOKENS, D), "const": const,
        "winspread": spread,
        "wq": arr("L0_attn_Wq").T, "wk": arr("L0_attn_Wk").T, "wv": arr("L0_attn_Wv").T, "wo": arr("L0_attn_Wo").T,
        "abias": np.stack([arr("L0_attn_bq"), arr("L0_attn_bk"), arr("L0_attn_bv")], 1),
        "bo": rows(arr("L0_attn_bo")),
    }
    gates = np.concatenate([arr("L0_xattn_igate_kernel"), arr("L0_xattn_fgate_kernel")], 1)
    ins["gate_q"], ins["gate_k"], ins["gate_v"] = gates[:D], gates[D:2 * D], gates[2 * D:]
    ins["gate_bias"] = rows(np.concatenate([arr("L0_xattn_igate_bias"), arr("L0_xattn_fgate_bias")]))
    ins["rms"] = rows(arr("L0_xattn_rms_scale"))

    pad = np.zeros(P - HCH[-1], np.float32)
    for layer in range(DEPTH):
        w1b = arr("L0_ffn_b1")[layer]
        chunks = []
        for at in (0, HID):
            for n, m in enumerate(HCH):
                col = w1b[at + n * P:at + n * P + m]
                chunks.append(col if m == P else np.concatenate([col, pad]))
        w2 = arr("L0_ffn_w2")[layer]
        ins[f"wqkv{layer}"] = arr("L0_ffn_wqkv")[layer]
        ins[f"lwo{layer}"] = arr("L0_ffn_wo")[layer].reshape(LH // 2, P, D).transpose(1, 0, 2)
        ins[f"qks{layer}"] = rows(np.stack([arr("L0_ffn_q_scale")[layer], arr("L0_ffn_k_scale")[layer]])).reshape(
            P, 2, LHD)
        ins[f"w1{layer}"] = arr("L0_ffn_w1")[layer]
        ins[f"w2{layer}"] = np.concatenate([w2, np.zeros((len(HCH) * P - HID, D), np.float32)]).reshape(
            len(HCH), P, D).transpose(1, 0, 2)
        ins[f"ffncols{layer}"] = np.stack(chunks + [arr("L0_ffn_ln_g")[layer], arr("L0_ffn_ln_b")[layer]], 1)
        ins[f"b2{layer}"] = rows(arr("L0_ffn_b2")[layer])

    nc = bacc.Bacc("TRN2", target_bir_lowering=False, num_devices=1)
    arrays, dram = {}, {}
    for name, a in ins.items():
        a = np.ascontiguousarray(a)
        arrays[f"in_{name}"] = a
        dram[name] = nc.dram_tensor(f"in_{name}", list(a.shape), mybir.dt.from_np(a.dtype), kind="ExternalInput").ap()
    dram["out"] = nc.dram_tensor("out", [TOKENS, D], F32, kind="ExternalOutput").ap()
    build(nc, dram)
    r = run_bass_kernel_spmd(nc, [arrays], core_ids=[0])
    return np.asarray(r.results[0]["out"]).reshape(NSEQ, SEQ, D)
```

```python
from contextlib import ExitStack

import numpy as np
import concourse.bass as bass
from concourse import mybir

F32 = mybir.dt.float32
F32R = mybir.dt.float32r
BF16 = mybir.dt.bfloat16
ALU = mybir.AluOpType
ACT = mybir.ActivationFunctionType
X_AXIS = mybir.AxisListType.X

P = 128
NSEQ, SEQ, D = 64, 64, 128
TOKENS = NSEQ * SEQ
TILES = TOKENS // P
GT = 4
GROUPS = TILES // GT
GN = GT * P
GS = GN // SEQ
AH, AHD, WIN = 16, 8, 5
HALF = WIN // 2
PADSEQ = SEQ + 2 * HALF
MH, MHD = 4, 32
LH, LHD = 8, 64
INNER = LH * LHD
HID = 341
HCH = (128, 128, 85)
DEPTH = 2
NEG = -1e30
LN_EPS = 1e-5

CONSTS = {}
_at = 0
for _name, _n in (("ident", 128), ("winmask", WIN * AH), ("causal", SEQ), ("keyquery", SEQ),
                  ("tri", 128), ("negfold", SEQ), ("sameseq", 128), ("shift", 128), ("rot", 4 * LHD), ("eps", 4),
                  ("seqstart", 128)):
    CONSTS[_name] = (_at, _at + _n)
    _at += _n
NCONST = _at


def ahead(n):
    return not isinstance(n, int) or n > 0


def wait(eng, sem, n):
    if ahead(n):
        eng.wait_ge(sem, n)


def live(i, lag, n):
    return not isinstance(i, int) or 0 <= i - lag < n


def sweep(eng, n, lag, unroll, step):
    first = -(-(lag + 1) // unroll) * unroll
    for i in range(first):
        step(i, i % unroll)
    with eng.Fori(first // unroll, n // unroll) as u:
        for k in range(unroll):
            step(u * unroll + k if unroll > 1 else u, k)
    for i in range(n, n + lag):
        step(i, i % unroll)


def group_rows(x, g):
    return x[:, bass.ds(g * GT, GT), :]


class Semaphores:

    def __init__(self, nc):
        self.nc, self.all = nc, []

    def __call__(self, name):
        self.all.append(self.nc.alloc_semaphore(name))
        return self.all[-1]

    def clear(self):
        self.nc.clear_and_free_semaphores(self.all)
        self.nc.all_engine_barrier()


def apart(eng, sem):
    eng.sem_inc(sem, 1)


class Norm:

    def __init__(self, sb, sem, tag):
        self.stats = sb(f"{tag}_stats", [P, GT, 12])
        self.meanvar = sb(f"{tag}_meanvar", [P, GT, 2])
        self.logvar = sb(f"{tag}_logvar", [P, GT])
        self.rstd = sb(f"{tag}_rstd", [P, GT])
        self.s_stats = sem(f"{tag}_stats_done")
        self.s_meanvar = sem(f"{tag}_meanvar_done")
        self.s_logvar = sem(f"{tag}_logvar_done")
        self.s_rstd = sem(f"{tag}_rstd_done")
        self.s_apart = sem(f"{tag}_apart")


def norm_stats(dve, nm, x, g):
    for j in range(GT):
        dve.bn_stats(nm.stats[:, j, 0:6], x[:, g * GT + j, :]).then_inc(nm.s_stats, 1)
    dve.wait_ge(nm.s_stats, (g + 1) * GT)
    apart(dve, nm.s_apart)
    for j in range(GT):
        dve.bn_aggr(nm.meanvar[:, j, :], nm.stats[:, j, 0:6]).then_inc(nm.s_meanvar, 1)


def norm_rstd(act, nm, eps, g):
    act.wait_ge(nm.s_meanvar, (g + 1) * GT)
    act.activation(nm.logvar[:, :], nm.meanvar[:, :, 1], ACT.Ln, bias=eps).then_inc(nm.s_logvar, 1)
    act.wait_ge(nm.s_logvar, g + 1)
    act.activation(nm.rstd[:, :], nm.logvar[:, :], ACT.Exp, scale=-0.5).then_inc(nm.s_rstd, 1)


def norm_apply(dve, nm, out, x, g, s_out):
    dve.wait_ge(nm.s_rstd, g + 1)
    for j in range(GT):
        dve.tensor_scalar(out(j), x[:, g * GT + j, :], nm.meanvar[:, j, 0:1], nm.rstd[:, j:j + 1],
                          ALU.subtract, ALU.mult).then_inc(s_out, 1)


def load_phase(nc, t, dram):
    with ExitStack() as ctx:
        sem = Semaphores(nc)
        ctx.callback(sem.clear)

        s_const, s_x, s_zero, s_cast = sem("const_loaded"), sem("x_loaded"), sem("pads_zeroed"), sem("masks_cast")
        s_w, s_kv, s_tab = sem("weights_loaded"), sem("kv_gates_summed"), sem("ctx_ones_set")
        block = ctx.enter_context(nc.Block())

        @block.sync
        def _(sp):
            sp.dma_start(t["const"][:], dram["const"]).then_inc(s_const, 16)
            for g in range(GROUPS):
                src = dram["x"].rearrange("(t p) f -> p t f", p=P)[:, g * GT:(g + 1) * GT, :]
                sp.dma_start(t["X"][:, g * GT:(g + 1) * GT, :], src).then_inc(s_x, 16)
            sp.wait_ge(s_x, 16 * GROUPS)

        @block.scalar
        def _(act):
            n = 0
            for name in ("wq", "wk", "wv", "wo", "abias", "bo", "gate_q", "gate_k", "gate_v", "gate_bias",
                         "rms", "winfold", "winspread"):
                act.dma_start(t[name][:], dram[name]).then_inc(s_w, 16)
                n += 16
            act.wait_ge(s_w, n)
            n = 0
            for name in ("wqkv", "lwo", "qks", "w1", "w2", "ffncols", "b2"):
                for layer in range(DEPTH):
                    act.dma_start(t[name][layer][:], dram[f"{name}{layer}"]).then_inc(t["s_layers"], 16)
                    n += 16
            t["layers_loaded"] = n

        @block.gpsimd
        def _(pool):
            pool.memset(t["kpad"][:], 0.0).then_inc(s_zero, 1)
            pool.memset(t["vpad"][:], 0.0).then_inc(s_zero, 1)
            pool.memset(t["ctxpad"][:], 1.0).then_inc(s_zero, 1)
            pool.memset(t["qdiag"][:], 0.0).then_inc(s_zero, 1)

        @block.vector
        def _(dve):
            c = t["c"]
            dve.wait_ge(s_const, 16)
            dve.tensor_copy(t["ident16"][:], c("ident")).then_inc(s_cast, 1)
            dve.tensor_copy(t["causal16"][:],
                            c("causal").unsqueeze(1).broadcast_to([P, 8, SEQ])).then_inc(s_cast, 1)
            dve.tensor_copy(t["keyquery16"][:],
                            c("keyquery").unsqueeze(1).broadcast_to([P, 8, SEQ])).then_inc(s_cast, 1)
            dve.wait_ge(s_w, 16 * 13)
            dve.tensor_copy(t["winspread_r"][:], t["winspread"][:]).then_inc(s_cast, 1)
            dve.tensor_tensor(t["gate_kv"][:], t["gate_k"][:], t["gate_v"][:], ALU.add).then_inc(s_kv, 1)
            dve.tensor_scalar(t["rms1"][:], t["rms"][:], 1.0, None, ALU.add).then_inc(s_kv, 1)


def window_attention(nc, t):
    with ExitStack() as ctx:
        def sb(name, shape, dt=F32):
            return ctx.enter_context(nc.sbuf_tensor(name, shape, dt))

        def ps(name, shape):
            return ctx.enter_context(nc.psum_tensor(name, shape, F32))

        sem = Semaphores(nc)
        ctx.callback(sem.clear)

        X, c = t["X"], t["c"]
        kpad, vpad = t["kpad"], t["vpad"]
        nm = Norm(sb, sem, "an")
        shift = sb("a_shift", [P, GT])
        h = sb("a_h", [P, GT, D])
        hT = sb("a_hT", [P, GN])
        q = sb("a_q", [P, GS, SEQ])
        prod = sb("a_prod", [P, WIN, GN])
        scT = sb("a_scT", [WIN * AH, GN])
        score = sb("a_score", [P, GT, WIN, AH])
        prob = sb("a_prob", [P, GT, WIN, AH])
        pnorm = sb("a_pnorm", [P, GT, WIN, AH])
        smax = sb("a_smax", [P, GT, AH])
        ssum = sb("a_ssum", [P, GT, AH])
        sinv = sb("a_sinv", [P, GT, AH])
        p_hi, p_lo = sb("a_p_hi", [WIN * AH, GN], F32R), sb("a_p_lo", [WIN * AH, GN], F32R)
        pv = sb("a_pv", [P, WIN, GN])
        acc = sb("a_acc", [P, WIN - 2, GN])
        attnT = sb("a_attnT", [P, GN])

        ps_turn = ps("a_ps_turn", [P, GN])
        ps_qkv = ps("a_ps_qkv", [P, 3, GN])
        ps_score = ps("a_ps_score", [P, 512])
        ps_spread = ps("a_ps_spread", [P, 2, GN])
        ps_out = ps("a_ps_out", [P, GT, D])
        ps_pT = ps_out[0:WIN * AH, :, :].rearrange("p j d -> p (j d)")

        s_shift, s_h, s_turned, s_hT = sem("a_shift_ready"), sem("a_h_ready"), sem("a_h_turned"), sem("a_hT_ready")
        s_qkv, s_q, s_k, s_v = sem("a_qkv_done"), sem("a_q_ready"), sem("a_k_ready"), sem("a_v_ready")
        s_prod_d, s_prod_p = sem("a_prod_vector"), sem("a_prod_pool")
        s_sc, s_masked, s_max, s_sub = sem("a_scores_done"), sem("a_masked"), sem("a_max_done"), sem("a_shifted")
        s_exp, s_sum, s_inv, s_pn = sem("a_exp_done"), sem("a_sum_done"), sem("a_inverse_done"), sem("a_probs_ready")
        s_pturned, s_phi, s_plo = sem("a_probs_turned"), sem("a_p_hi_ready"), sem("a_p_lo_ready")
        s_folded, s_scT, s_apart = sem("a_scores_folded"), sem("a_scT_ready"), sem("a_apart")
        s_spread, s_pv, s_acc = sem("a_probs_spread"), sem("a_pv_ready"), sem("a_sum_of_pv")
        s_out, s_res, s_bias = sem("a_out_done"), sem("a_residual_done"), sem("a_bias_added")

        eps = c("eps")[:, 0:1]
        maskb = c("winmask").unsqueeze(1).broadcast_to([P, GT, WIN * AH])
        N = GROUPS
        LAG = 4
        block = ctx.enter_context(nc.Block())

        @block.tensor
        def _(pe):
            def project(g, names):
                for n, w in names:
                    wait(pe, (s_q, s_k, s_v)[n], g)
                    pe.matmul(ps_qkv[:, n, :], t[w][:, :], hT[:, :], start=True, stop=True).then_inc(s_qkv, 1)

            def spread(g, places):
                for w in places:
                    wait(pe, s_pv, WIN * g + max(w - 1, 0))
                    pe.matmul(ps_spread[:, w % 2, :], t["winspread_r"][:, w, :], p_hi[:, :], start=True, stop=False)
                    pe.matmul(ps_spread[:, w % 2, :], t["winspread_r"][:, w, :], p_lo[:, :],
                              start=False, stop=True).then_inc(s_spread, 1)

            def fold(places):
                for w in places:
                    mm = pe.matmul(ps_turn[0:WIN * AH, :], t["winfold"][:, w, :], prod[:, w, :],
                                   start=(w == 0), stop=(w == WIN - 1), skip_group_check=True)
                return mm

            def step(i, _):
                if live(i, 1, N):
                    g = i - 1
                    pe.wait_ge(s_h, GT * (g + 1))
                    wait(pe, s_scT, g - 1)
                    for j in range(GT):
                        mm = pe.transpose(ps_turn[:, j * P:(j + 1) * P], h[:, j, :], c("ident"))
                    mm.then_inc(s_turned, 1)
                if live(i, 4, N):
                    spread(i - 4, (3,))
                if live(i, 4, N):
                    spread(i - 4, (4,))
                if live(i, 2, N):
                    g = i - 2
                    pe.wait_ge(s_prod_d, 3 * (g + 1))
                    pe.wait_ge(s_prod_p, 2 * (g + 1))
                    pe.wait_ge(s_hT, g + 2 if live(i, 1, N) else N)
                    fold((0, 1))
                if live(i, 2, N):
                    fold((2, 3, 4)).then_inc(s_folded, 1)
                if live(i, 1, N):
                    pe.wait_ge(s_hT, i)
                    project(i - 1, ((0, "wq"),))
                if live(i, 4, N):
                    g = i - 4
                    pe.wait_ge(s_acc, 4 * (g + 1))
                    pe.wait_ge(s_plo, g + 1)
                    for j in range(GT):
                        mm = pe.matmul(ps_out[:, j, :], attnT[:, j * P:(j + 1) * P], t["wo"][:, :],
                                       start=True, stop=True)
                    mm.then_inc(s_out, 1)
                if live(i, 2, N):
                    g = i - 2
                    pe.wait_ge(s_scT, g + 1)
                    wait(pe, s_masked, g)
                    apart(pe, s_apart)
                    for j in range(GT):
                        mm = pe.transpose(ps_score[:, j * WIN * AH:(j + 1) * WIN * AH], scT[:, j * P:(j + 1) * P],
                                          c("ident")[0:WIN * AH, 0:WIN * AH])
                    mm.then_inc(s_sc, 1)
                if live(i, 1, N):
                    project(i - 1, ((1, "wk"),))
                if live(i, 3, N):
                    g = i - 3
                    pe.wait_ge(s_pn, g + 1)
                    wait(pe, s_res, g)
                    for j in range(GT):
                        mm = pe.transpose(ps_pT[:, j * P:(j + 1) * P],
                                          pnorm[:, j, :, :].rearrange("p w h -> p (w h)"), c("ident"))
                    mm.then_inc(s_pturned, 1)
                if live(i, 1, N):
                    project(i - 1, ((2, "wv"),))
                if live(i, 3, N):
                    pe.wait_ge(s_plo, i - 2)
                    spread(i - 3, (0, 1))
                if live(i, 3, N):
                    spread(i - 3, (2,))
            sweep(pe, N, LAG, 1, step)

        @block.scalar
        def _(act):
            act.preload_act_table_set("natural_log_exp_and_others")

            def step(i, _):
                if live(i, 1, N):
                    g = i - 1
                    act.wait_ge(s_turned, g + 1)
                    wait(act, s_qkv, 3 * g)
                    act.activation(hT[:], ps_turn[:], ACT.Copy).then_inc(s_hT, 1)
                if live(i, 0, N):
                    norm_rstd(act, nm, eps, i)
                if live(i, 2, N):
                    g = i - 2
                    act.wait_ge(s_folded, g + 1)
                    wait(act, s_sc, g)
                    act.activation(scT[:], ps_turn[0:WIN * AH, :], ACT.Copy).then_inc(s_scT, 1)
                if live(i, 1, N):
                    g = i - 1
                    act.wait_ge(s_qkv, 3 * g + 1)
                    wait(act, s_prod_d, 3 * g)
                    wait(act, s_prod_p, 2 * g)
                    act.activation(q[:], ps_qkv[:, 0, :].rearrange("p (s t) -> p s t", t=SEQ), ACT.Identity,
                                   bias=t["abias"][:, 0:1]).then_inc(s_q, 1)
                if live(i, 1, N):
                    g = i - 1
                    act.wait_ge(s_qkv, 3 * g + 2)
                    act.activation(kpad[:, :, HALF:HALF + SEQ],
                                   ps_qkv[:, 1, :].rearrange("p (s t) -> p s t", t=SEQ), ACT.Identity,
                                   bias=t["abias"][:, 1:2]).then_inc(s_k, 1)
                if live(i, 3, N):
                    g = i - 3
                    act.wait_ge(s_pturned, g + 1)
                    wait(act, s_spread, WIN * g)
                    act.activation(p_hi[:], ps_pT, ACT.Copy).then_inc(s_phi, 1)
                if live(i, 0, N):
                    act.wait_ge(s_shift, i + 1)
                    wait(act, s_turned, i)
                    for j in range(GT):
                        act.activation(h[:, j, :], X[:, i * GT + j, :], ACT.Identity, bias=shift[:, j:j + 1],
                                       scale=nm.rstd[:, j:j + 1]).then_inc(s_h, 1)
                if live(i, 2, N):
                    g = i - 2
                    act.wait_ge(s_sub, g + 1)
                    wait(act, s_pn, g)
                    act.activation(prob[:], score[:], ACT.Exp, scale=float(AHD) ** -0.5).then_inc(s_exp, 1)
                if live(i, 1, N):
                    g = i - 1
                    act.wait_ge(s_qkv, 3 * g + 3)
                    act.activation(vpad[:, bass.ds(g * GS, GS), HALF:HALF + SEQ],
                                   ps_qkv[:, 2, :].rearrange("p (s t) -> p s t", t=SEQ), ACT.Identity,
                                   bias=t["abias"][:, 2:3]).then_inc(s_v, 1)
            sweep(act, N, LAG, 1, step)

        def window_product(eng, w, s):
            eng.tensor_tensor(prod[:, w, :].rearrange("p (s t) -> p s t", t=SEQ), q[:], kpad[:, :, w:w + SEQ],
                              ALU.mult).then_inc(s, 1)

        @block.vector
        def _(dve):
            def weighted(g, w):
                dve.wait_ge(s_spread, WIN * g + w + 1)
                dve.tensor_tensor(pv[:, w, :].rearrange("p (s t) -> p s t", t=SEQ),
                                  ps_spread[:, w % 2, :].rearrange("p (s t) -> p s t", t=SEQ),
                                  vpad[:, bass.ds(g * GS, GS), w:w + SEQ], ALU.mult).then_inc(s_pv, 1)

            def step(i, _):
                if live(i, 4, N):
                    weighted(i - 4, 3)
                if live(i, 4, N):
                    weighted(i - 4, 4)
                if live(i, 3, N):
                    g = i - 3
                    dve.wait_ge(s_exp, g + 1)
                    dve.tensor_reduce(ssum[:], prob[:].rearrange("p j w h -> p j h w"), X_AXIS,
                                      ALU.add).then_inc(s_sum, 1)
                if live(i, 3, N):
                    g = i - 3
                    dve.wait_ge(s_sum, g + 1)
                    dve.reciprocal(sinv[:], ssum[:]).then_inc(s_inv, 1)
                if live(i, 3, N):
                    g = i - 3
                    dve.wait_ge(s_inv, g + 1)
                    wait(dve, s_pturned, g)
                    dve.tensor_tensor(pnorm[:], prob[:], sinv[:].unsqueeze(2).broadcast_to([P, GT, WIN, AH]),
                                      ALU.mult).then_inc(s_pn, 1)
                if live(i, 0, N):
                    wait(dve, s_h, GT * i)
                    norm_stats(dve, nm, X, i)
                if live(i, 0, N):
                    dve.wait_ge(nm.s_rstd, i + 1)
                    dve.scalar_tensor_tensor(out=shift[:], in0=nm.meanvar[:, :, 0], scalar=-1.0, in1=nm.rstd[:],
                                             op0=ALU.mult, op1=ALU.mult).then_inc(s_shift, 1)
                if live(i, 4, N):
                    g = i - 4
                    dve.wait_ge(s_out, g + 1)
                    dve.wait_ge(s_bias, g + 1)
                    dve.tensor_tensor(group_rows(X, g), ps_out[:], group_rows(X, g), ALU.add).then_inc(s_res, 1)
                if live(i, 2, N):
                    g = i - 2
                    dve.wait_ge(s_sc, g + 1)
                    wait(dve, s_exp, g)
                    flat = score[:].rearrange("p j w h -> p j (w h)")
                    dve.tensor_tensor(flat, ps_score[:, 0:GT * WIN * AH].rearrange("p (j x) -> p j x", j=GT), maskb,
                                      ALU.add).then_inc(s_masked, 1)
                    dve.wait_ge(s_masked, g + 1)
                    dve.tensor_reduce(smax[:], score[:].rearrange("p j w h -> p j h w"), X_AXIS,
                                      ALU.max).then_inc(s_max, 1)
                    dve.wait_ge(s_max, g + 1)
                    dve.tensor_tensor(score[:], score[:], smax[:].unsqueeze(2).broadcast_to([P, GT, WIN, AH]),
                                      ALU.subtract).then_inc(s_sub, 1)
                if live(i, 3, N):
                    g = i - 3
                    dve.wait_ge(s_phi, g + 1)
                    dve.tensor_tensor(p_lo[:], ps_pT, p_hi[:].bitcast(F32), ALU.subtract).then_inc(s_plo, 1)
                if live(i, 1, N):
                    g = i - 1
                    dve.wait_ge(s_q, g + 1)
                    dve.wait_ge(s_k, g + 1)
                    wait(dve, s_folded, g)
                    window_product(dve, 0, s_prod_d)
                    window_product(dve, 1, s_prod_d)
                if live(i, 3, N):
                    wait(dve, s_acc, 4 * (i - 3))
                    weighted(i - 3, 0)
                if live(i, 1, N):
                    window_product(dve, 2, s_prod_d)
                if live(i, 3, N):
                    weighted(i - 3, 1)
                if live(i, 3, N):
                    weighted(i - 3, 2)
            sweep(dve, N, LAG, 1, step)

        @block.gpsimd
        def _(pool):
            def step(i, _):
                if live(i, 4, N):
                    g = i - 4
                    wait(pool, s_out, g)
                    sums = [acc[:, 0, :], acc[:, 1, :], acc[:, 2, :], attnT[:, :]]
                    for w in range(1, WIN):
                        pool.wait_ge(s_pv, WIN * g + w + 1)
                        if w > 1:
                            pool.wait_ge(s_acc, 4 * g + w - 1)
                        pool.tensor_tensor(sums[w - 1], pv[:, 0, :] if w == 1 else sums[w - 2], pv[:, w, :],
                                           ALU.add).then_inc(s_acc, 1)
                if live(i, 1, N):
                    g = i - 1
                    pool.wait_ge(s_h, GT * (g + 1))
                    pool.tensor_tensor(group_rows(X, g), group_rows(X, g),
                                       t["bo"][:].unsqueeze(1).broadcast_to([P, GT, D]), ALU.add).then_inc(s_bias, 1)
                    pool.wait_ge(s_q, g + 1)
                    pool.wait_ge(s_k, g + 1)
                    wait(pool, s_folded, g)
                    for w in range(3, WIN):
                        window_product(pool, w, s_prod_p)
            sweep(pool, N, LAG, 1, step)


def mlstm(nc, t, dram):
    with ExitStack() as ctx:
        def sb(name, shape, dt=F32):
            return ctx.enter_context(nc.sbuf_tensor(name, shape, dt))

        def ps(name, shape):
            return ctx.enter_context(nc.psum_tensor(name, shape, F32))

        sem = Semaphores(nc)
        ctx.callback(sem.clear)

        X, Y, c = t["X"], t["Y"], t["c"]
        ctxpad, qdiag = t["ctxpad"], t["qdiag"]
        GH = GT * MH
        nm, ny = Norm(sb, sem, "bn"), Norm(sb, sem, "yn")
        h = sb("b_h", [P, GT, D])
        ctx_in = sb("b_ctx", [P, 2, GT, D])
        qT = sb("b_qT", [P, GN])
        cT = sb("b_cT", [P, 2, GN])
        gate = sb("b_gate", [P, GT, 2 * MH])
        fabs, fexp, fln = sb("b_fabs", [P, GT, MH]), sb("b_fexp", [P, GT, MH]), sb("b_fln", [P, GT, MH])
        logf = sb("b_logf", [P, GH])
        csum = sb("b_csum", [P, GH])
        u = sb("b_u", [P, 2, GH])
        umaxT = sb("b_umaxT", [GH, P])
        umax = sb("b_umax", [P, GH])
        negm = sb("b_negm", [P, GH])
        floor = sb("b_floor", [P, 2, GH])
        spread = sb("b_spread", [P, GH, SEQ])
        decay_log = sb("b_decay_log", [P, GH, SEQ])
        decay = sb("b_decay", [P, GH, SEQ])
        weight = sb("b_weight", [P, GH, SEQ])
        norm, norm_eps, inv = sb("b_norm", [P, GH]), sb("b_norm_eps", [P, GH]), sb("b_inv", [P, GH])
        ho, hsq, hn, hr = (sb(f"b_{n}", [P, GH, MHD]) for n in ("ho", "hsq", "hn", "hr"))
        ms, lms, rms = sb("b_ms", [P, GH]), sb("b_lms", [P, GH]), sb("b_rms", [P, GH])

        ps_turn = ps("b_ps_turn", [P, 2, GN])
        ps_small = ps("b_ps_small", [P, 512])
        ps_decay = ps("b_ps_decay", [P, 2, 512])
        ps_score = ps("b_ps_score", [P, 2, 512])
        G0, C0, U0, M0 = 0, 64, 128, 256

        s_ctx, s_pad = [sem("b_ctx_loaded0"), sem("b_ctx_loaded1")], sem("b_ctxpad_ready")
        s_h, s_turned, s_qT, s_cT, s_qdiag = (sem(f"b_{n}") for n in
                                              ("h_ready", "turned", "qT_ready", "cT_ready", "qdiag_ready"))
        s_gate, s_gsb, s_fabs, s_fexp, s_fln, s_logf = (sem(f"b_{n}") for n in
                                                        ("gates_done", "gates_ready", "fabs", "fexp", "fln", "logf"))
        s_cs, s_u, s_csum, s_uT, s_scan, s_mT, s_umax, s_negm, s_floor = (
            sem(f"b_{n}") for n in ("cs_done", "u_ready", "csum_ready", "uT_done", "scan_done", "umax_turned",
                                    "umax_ready", "negm_ready", "floor_ready"))
        s_spread, s_mbc, s_dlog, s_decay, s_st, s_weight, s_av = (
            sem(f"b_{n}") for n in ("spread_ready", "decay_log_done", "decay_log_ready", "decay_ready",
                                    "scores_done", "weights_ready", "output_done"))
        s_norm, s_neps, s_inv, s_ho, s_hsq, s_ms, s_lms, s_rms, s_hn, s_hr, s_x, s_y = (
            sem(f"b_{n}") for n in ("norm", "norm_eps", "inverse", "ho", "ho_squared", "meansquare", "log_ms",
                                    "rms", "hn_ready", "hr_ready", "x_updated", "y_ready"))
        s_apart, s_apart_pool = sem("b_apart"), sem("b_apart_pool")
        N, LAG = GROUPS, 3
        block = ctx.enter_context(nc.Block())

        @block.sync
        def _(sp):
            def step(i, par):
                if live(i, 0, N):
                    wait(sp, s_turned, i - 1)
                    wait(sp, s_pad, i - 1)
                    sp.dma_start(ctx_in[:, par, :, :], dram["ctx"].rearrange("(t p) f -> p t f", p=P)[
                        :, bass.ds(i * GT, GT), :]).then_inc(s_ctx[par], 16)
            sweep(sp, N, LAG, 2, step)

        def ctx_count(g, par):
            return 16 * (g // 2 + 1) if isinstance(g, int) else (g - par + 2) * 8

        @block.tensor
        def _(pe):
            def step(i, par):
                if live(i, 2, N):
                    g = i - 2
                    pe.wait_ge(s_spread, g + 1)
                    wait(pe, s_ho, g)
                    for b in range(2):
                        pe.matmul(ps_decay[:, b, :], c("sameseq"), spread[:, b * 8:(b + 1) * 8, :],
                                  start=True, stop=False)
                        mm = pe.matmul(ps_decay[:, b, :], t["ident16"][:], t["keyquery16"][:],
                                       start=False, stop=True)
                    mm.then_inc(s_mbc, 1)
                if live(i, 1, N):
                    g = i - 1
                    pe.wait_ge(s_h, GT * (g + 1))
                    pe.wait_ge(s_ctx[1 - par], ctx_count(g, 1 - par))
                    wait(pe, s_qdiag, 4 * g)
                    wait(pe, s_cT, g)
                    for j in range(GT):
                        pe.transpose(ps_turn[:, 0, j * P:(j + 1) * P], h[:, j, :], c("ident"))
                    for j in range(GT):
                        mm = pe.transpose(ps_turn[:, 1, j * P:(j + 1) * P], ctx_in[:, 1 - par, j, :], c("ident"))
                    mm.then_inc(s_turned, 1)
                if live(i, 2, N):
                    g = i - 2
                    wait(pe, s_weight, 2 * g)
                    for j in range(GT):
                        for s in range(2):
                            mm = pe.matmul(ps_score[s * SEQ:(s + 1) * SEQ, j // 2, (j % 2) * 256:(j % 2) * 256 + 256],
                                           cT[:, par, j * P + s * SEQ:j * P + (s + 1) * SEQ],
                                           qdiag[:, par, 2 * j + s, :, :], start=True, stop=True)
                        if j % 2:
                            mm.then_inc(s_st, 1)
                if live(i, 1, N):
                    g = i - 1
                    pe.wait_ge(s_qT, g + 1)
                    pe.wait_ge(s_cT, g + 1)
                    wait(pe, s_negm, g)
                    for j in range(GT):
                        at = G0 + j * 2 * MH
                        pe.matmul(ps_small[:, at:at + 2 * MH], qT[:, j * P:(j + 1) * P], t["gate_q"][:],
                                  start=True, stop=False)
                        mm = pe.matmul(ps_small[:, at:at + 2 * MH], cT[:, 1 - par, j * P:(j + 1) * P],
                                       t["gate_kv"][:], start=False, stop=True)
                    mm.then_inc(s_gate, 1)

                def output(tiles):
                    for j in tiles:
                        for hd in range(MH):
                            for s in range(2):
                                at = (j % 2) * MH * (MHD + 1) + hd * (MHD + 1)
                                mm = pe.matmul(ps_decay[s * SEQ:(s + 1) * SEQ, j // 2, at:at + MHD + 1],
                                               weight[s * SEQ:(s + 1) * SEQ, j * MH + hd, :],
                                               ctxpad[s * SEQ:(s + 1) * SEQ, par, j, hd, :], start=True, stop=True)
                    mm.then_inc(s_av, 1)

                if live(i, 2, N):
                    g = i - 2
                    pe.wait_ge(s_weight, 2 * (g + 1))
                    pe.wait_ge(s_pad, g + 1)
                    apart(pe, s_apart)
                    output((0, 1))
                if live(i, 1, N):
                    g = i - 1
                    pe.wait_ge(s_logf, g + 1)
                    pe.matmul(ps_small[:, C0:C0 + GH], c("tri"), logf[:], start=True, stop=True).then_inc(s_cs, 1)
                if live(i, 2, N):
                    output((2, 3))
                if live(i, 1, N):
                    g = i - 1
                    pe.wait_ge(s_u, g + 1)
                    pe.wait_ge(s_csum, g + 1)
                    pe.transpose(ps_small[0:GH, U0:U0 + P], u[:, 1 - par, :], c("ident")).then_inc(s_uT, 1)
                    pe.wait_ge(s_scan, g + 1)
                    apart(pe, s_apart)
                    pe.transpose(ps_small[:, M0:M0 + GH], umaxT[:], c("ident")[0:GH, 0:GH]).then_inc(s_mT, 1)
            sweep(pe, N, LAG, 2, step)

        @block.scalar
        def _(act):
            act.preload_act_table_set("natural_log_exp_and_others")
            eps, one = c("eps")[:, 0:1], c("eps")[:, 2:3]
            small_eps = c("eps")[:, 1:2]

            def step(i, par):
                if live(i, 2, N):
                    g = i - 2
                    act.wait_ge(s_dlog, 2 * (g + 1))
                    wait(act, s_weight, 2 * g)
                    act.activation(decay[:], decay_log[:], ACT.Exp).then_inc(s_decay, 1)
                if live(i, 1, N):
                    g = i - 1
                    act.wait_ge(s_turned, g + 1)
                    wait(act, s_gate, g)
                    act.activation(qT[:], ps_turn[:, 0, :], ACT.Copy).then_inc(s_qT, 1)
                    wait(act, s_st, 2 * (g - 1))
                    act.activation(cT[:, 1 - par, :], ps_turn[:, 1, :], ACT.Copy).then_inc(s_cT, 1)
                    for hd in range(MH):
                        rows = slice(hd * MHD, (hd + 1) * MHD)
                        act.activation(qdiag[rows, 1 - par, :, hd, :],
                                       ps_turn[rows, 0, :].rearrange("p (s t) -> p s t", t=SEQ),
                                       ACT.Copy).then_inc(s_qdiag, 1)
                    act.wait_ge(s_gsb, g + 1)
                    wait(act, s_logf, g)
                    act.activation(fabs[:], gate[:, :, MH:2 * MH], ACT.Abs).then_inc(s_fabs, 1)
                    act.wait_ge(s_fabs, g + 1)
                    act.activation(fexp[:], fabs[:], ACT.Exp, scale=-1.0).then_inc(s_fexp, 1)
                    act.wait_ge(s_fexp, g + 1)
                    act.activation(fln[:], fexp[:], ACT.Ln, bias=one).then_inc(s_fln, 1)
                if live(i, 0, N):
                    norm_rstd(act, nm, eps, i)
                if live(i, 2, N):
                    g = i - 2
                    act.wait_ge(s_ho, g + 1)
                    wait(act, s_ms, g)
                    act.activation(hsq[:], ho[:], ACT.Square).then_inc(s_hsq, 1)
                    act.wait_ge(s_ms, g + 1)
                    act.activation(lms[:], ms[:], ACT.Ln, bias=small_eps, scale=1.0 / MHD).then_inc(s_lms, 1)
                    act.wait_ge(s_lms, g + 1)
                    wait(act, s_hn, g)
                    act.activation(rms[:], lms[:], ACT.Exp, scale=-0.5).then_inc(s_rms, 1)
                if live(i, 1, N):
                    g = i - 1
                    act.wait_ge(s_negm, g + 1)
                    wait(act, s_norm, g - 1)
                    act.activation(floor[:, 1 - par, :], negm[:], ACT.Exp).then_inc(s_floor, 1)
                if live(i, 3, N):
                    norm_rstd(act, ny, eps, i - 3)
            sweep(act, N, LAG, 2, step)

        @block.vector
        def _(dve):
            def step(i, par):
                if live(i, 2, N):
                    g = i - 2
                    dve.wait_ge(s_mbc, g + 1)
                    wait(dve, s_decay, g)
                    for b in range(2):
                        dve.tensor_tensor(decay_log[:, b * 8:(b + 1) * 8, :],
                                          ps_decay[:, b, :].rearrange("p (x t) -> p x t", t=SEQ),
                                          u[:, par, b * 8:(b + 1) * 8].unsqueeze(2).broadcast_to([P, 8, SEQ]),
                                          ALU.add).then_inc(s_dlog, 1)
                if live(i, 0, N):
                    wait(dve, s_h, GT * i)
                    norm_stats(dve, nm, X, i)
                if live(i, 2, N):
                    g = i - 2
                    dve.wait_ge(s_decay, g + 1)
                    wait(dve, s_av, 2 * g)
                    for b in range(2):
                        dve.wait_ge(s_st, 2 * g + b + 1)
                        dve.scalar_tensor_tensor(out=weight[:, b * 8:(b + 1) * 8, :].rearrange("p x t -> p (x t)"),
                                                 in0=ps_score[:, b, :], scalar=float(MHD) ** -0.5,
                                                 in1=decay[:, b * 8:(b + 1) * 8, :].rearrange("p x t -> p (x t)"),
                                                 op0=ALU.mult, op1=ALU.mult).then_inc(s_weight, 1)
                if live(i, 1, N):
                    g = i - 1
                    dve.wait_ge(s_gate, g + 1)
                    wait(dve, s_u, g)
                    dve.tensor_tensor(gate[:], ps_small[:, G0:G0 + GT * 2 * MH].rearrange("p (j x) -> p j x", j=GT),
                                      t["gate_bias"][:].unsqueeze(1).broadcast_to([P, GT, 2 * MH]),
                                      ALU.add).then_inc(s_gsb, 1)
                    dve.wait_ge(s_fln, g + 1)
                    dve.wait_ge(s_gsb, g + 1)
                    wait(dve, s_cs, g)
                    dve.scalar_tensor_tensor(out=logf[:].rearrange("p (j x) -> p j x", j=GT),
                                             in0=gate[:, :, MH:2 * MH], scalar=0.0, in1=fln[:],
                                             op0=ALU.min, op1=ALU.subtract).then_inc(s_logf, 1)
                    dve.wait_ge(s_cs, g + 1)
                    dve.tensor_tensor(u[:, 1 - par, :].rearrange("p (j x) -> p j x", j=GT), gate[:, :, 0:MH],
                                      ps_small[:, C0:C0 + GH].rearrange("p (j x) -> p j x", j=GT),
                                      ALU.subtract).then_inc(s_u, 1)
                    wait(dve, s_negm, g)
                    dve.tensor_copy(csum[:], ps_small[:, C0:C0 + GH]).then_inc(s_csum, 1)
                    dve.wait_ge(s_uT, g + 1)
                    wait(dve, s_mT, g)
                    dve.tensor_tensor_scan(umaxT[:], c("seqstart")[0:GH, :], ps_small[0:GH, U0:U0 + P], 0.0,
                                           ALU.add, ALU.max).then_inc(s_scan, 1)
                    dve.wait_ge(s_mT, g + 1)
                    wait(dve, s_spread, g)
                    dve.tensor_copy(umax[:], ps_small[:, M0:M0 + GH]).then_inc(s_umax, 1)
                    dve.wait_ge(s_csum, g + 1)
                    wait(dve, s_floor, g)
                    dve.scalar_tensor_tensor(out=negm[:], in0=csum[:], scalar=-1.0, in1=ps_small[:, M0:M0 + GH],
                                             op0=ALU.mult, op1=ALU.subtract).then_inc(s_negm, 1)
                if live(i, 2, N):
                    g = i - 2
                    dve.wait_ge(s_av, 2 * (g + 1))
                    dve.wait_ge(s_floor, g + 1)
                    out = ps_decay[:, :, 0:2 * MH * (MHD + 1)].rearrange("p b (x d) -> p b x d", d=MHD + 1)
                    dve.tensor_tensor(norm[:].rearrange("p (b x) -> p b x", b=2), out[:, :, :, MHD],
                                      floor[:, par, :].rearrange("p (b x) -> p b x", b=2), ALU.max).then_inc(s_norm, 1)
                    dve.wait_ge(s_norm, g + 1)
                    dve.tensor_scalar(norm_eps[:], norm[:], 1e-6, None, ALU.add).then_inc(s_neps, 1)
                    dve.wait_ge(s_neps, g + 1)
                    dve.reciprocal(inv[:], norm_eps[:]).then_inc(s_inv, 1)
                    dve.wait_ge(s_inv, g + 1)
                    wait(dve, s_hn, g)
                    wait(dve, s_hsq, g)
                    dve.tensor_tensor(ho[:].rearrange("p (b x) d -> p b x d", b=2), out[:, :, :, 0:MHD],
                                      inv[:].rearrange("p (b x) -> p b x", b=2).unsqueeze(3).broadcast_to(
                                          [P, 2, 8, MHD]), ALU.mult).then_inc(s_ho, 1)
                if live(i, 0, N):
                    wait(dve, s_turned, i)
                    norm_apply(dve, nm, lambda j: h[:, j, :], X, i, s_h)
                if live(i, 2, N):
                    g = i - 2
                    dve.wait_ge(s_hsq, g + 1)
                    wait(dve, s_lms, g)
                    dve.tensor_reduce(ms[:], hsq[:], X_AXIS, ALU.add).then_inc(s_ms, 1)
                if live(i, 3, N):
                    g = i - 3
                    dve.wait_ge(s_x, g + 1)
                    wait(dve, s_y, GT * g)
                    norm_stats(dve, ny, X, g)
                if live(i, 2, N):
                    g = i - 2
                    dve.wait_ge(s_rms, g + 1)
                    wait(dve, s_hr, g)
                    dve.tensor_tensor(hn[:], ho[:], rms[:].unsqueeze(2).broadcast_to([P, GH, MHD]),
                                      ALU.mult).then_inc(s_hn, 1)
                if live(i, 3, N):
                    g = i - 3
                    norm_apply(dve, ny, lambda j: Y[:, g * GT + j, :], X, g, s_y)
            sweep(dve, N, LAG, 2, step)

        @block.gpsimd
        def _(pool):
            def step(i, par):
                if live(i, 1, N):
                    g = i - 1
                    pool.wait_ge(s_ctx[1 - par], ctx_count(g, 1 - par))
                    wait(pool, s_av, 2 * (g - 1))
                    apart(pool, s_apart_pool)
                    pool.tensor_scalar(ctxpad[:, 1 - par, :, :, 0:MHD],
                                       ctx_in[:, 1 - par, :, :].rearrange("p j (h d) -> p j h d", d=MHD),
                                       1.0, None, ALU.mult).then_inc(s_pad, 1)
                    pool.wait_ge(s_umax, g + 1)
                    wait(pool, s_mbc, g)
                    pool.tensor_tensor(spread[:], c("negfold").unsqueeze(1).broadcast_to([P, GH, SEQ]),
                                       umax[:].unsqueeze(2).broadcast_to([P, GH, SEQ]), ALU.mult).then_inc(s_spread, 1)
                if live(i, 2, N):
                    g = i - 2
                    pool.wait_ge(s_hn, g + 1)
                    wait(pool, s_x, g)
                    pool.tensor_tensor(hr[:], hn[:], t["rms1"][:].unsqueeze(1).broadcast_to([P, GH, MHD]),
                                       ALU.mult).then_inc(s_hr, 1)
                    pool.wait_ge(s_hr, g + 1)
                    pool.tensor_tensor(group_rows(X, g), group_rows(X, g),
                                       hr[:].rearrange("p (j h) d -> p j (h d)", j=GT), ALU.add).then_inc(s_x, 1)
            sweep(pool, N, LAG, 2, step)


def causal_attention(nc, t, layer):
    with ExitStack() as ctx:
        def sb(name, shape, dt=F32):
            return ctx.enter_context(nc.sbuf_tensor(f"c{layer}_{name}", shape, dt))

        def ps(name, shape):
            return ctx.enter_context(nc.psum_tensor(f"c{layer}_{name}", shape, F32))

        phase_sems = Semaphores(nc)
        ctx.callback(phase_sems.clear)

        def sem(name):
            return phase_sems(f"c{layer}_{name}")

        Y, c = t["Y"], t["c"]
        wqkv, wo, qks = t["wqkv"][layer], t["lwo"][layer], t["qks"][layer]
        HT = LHD // 2
        w_hi, w_lo = sb("w_hi", [P, 3 * INNER], F32R), sb("w_lo", [P, 3 * INNER], F32R)
        costab, sintab = sb("costab", [P, 2, LHD]), sb("sintab", [P, 2, LHD])
        xin = sb("xin", [P, D])
        xT = sb("xT", [P, P])
        x_hi, x_lo = sb("x_hi", [P, P], F32R), sb("x_lo", [P, P], F32R)
        qk = sb("qk", [P, 2 * LH, LHD])
        sq = sb("sq", [P, 2 * LH, LHD])
        rcos, rsin = sb("rcos", [P, 2 * LH, LHD]), sb("rsin", [P, 2 * LH, LHD])
        rsum, rot = sb("rsum", [P, 2 * LH, LHD]), sb("rot", [P, 2 * LH, LHD])
        ss, ssc, lss, inv = (sb(n, [P, 2 * LH]) for n in ("ss", "ssc", "lss", "inv"))
        v = sb("v", [P, 4, INNER])
        qkT = sb("qkT", [P, 2 * LH // 2, P])
        smax, ssum, sinv = (sb(n, [P, LH]) for n in ("smax", "ssum", "sinv"))
        score, prob, pnorm = (sb(n, [P, LH, SEQ]) for n in ("score", "prob", "pnorm"))
        pT = sb("pT", [P, INNER])
        oT = sb("oT", [P, LH // 2, P])

        ps_qkv = ps("ps_qkv", [P, 3, INNER])
        ps_qkT = ps("ps_qkT", [P, 2, 512])
        ps_score = ps("ps_score", [P, 512])
        ps_o0 = ps("ps_o0", [P, 512])
        ps_o1 = ps("ps_o1", [P, 512])
        ps_y, ps_xT = ps_qkv[:, 2, 0:D], ps_o1[:, 384:512]

        s_tab, s_whi, s_wlo, s_zero = sem("tables_ready"), sem("w_hi_ready"), sem("w_lo_ready"), sem("xT_zeroed")
        s_xin, s_xturned, s_xT, s_xhi, s_xlo = (sem(n) for n in ("xin_ready", "x_turned", "xT_ready", "x_hi_ready",
                                                                 "x_lo_ready"))
        s_qkv, s_qk, s_v, s_sq, s_rcos, s_rsin = (sem(n) for n in ("qkv_done", "qk_ready", "v_ready", "sq_ready",
                                                                   "rcos_ready", "rsin_ready"))
        s_ss, s_ssc, s_lss, s_inv, s_rsum, s_rot = (sem(n) for n in ("ss_ready", "ss_clipped", "log_ss", "inv_ready",
                                                                     "rsum_ready", "rot_ready"))
        s_rturned, s_qkT, s_sc, s_max, s_sub, s_exp = (sem(n) for n in ("rot_turned", "qkT_ready", "scores_done",
                                                                        "max_ready", "shifted", "exp_ready"))
        s_sum, s_sinv, s_pn, s_pturned, s_pT, s_av, s_oT, s_y, s_res = (
            sem(n) for n in ("sum_ready", "sum_inverse", "probs_ready", "probs_turned", "pT_ready", "output_done",
                             "oT_ready", "y_done", "residual_done"))
        s_apart = sem("apart")
        N, LAG = TILES, 5
        block = ctx.enter_context(nc.Block())

        @block.tensor
        def _(pe):
            pe.wait_ge(s_whi, 1)
            pe.wait_ge(s_wlo, 1)

            def step(i, par):
                if live(i, 1, N):
                    g = i - 1
                    pe.wait_ge(s_xlo, g + 1)
                    for n in range(3):
                        if n < 2:
                            wait(pe, s_qk, 2 * (g - 1) + n + 1)
                        else:
                            wait(pe, s_v, g)
                            wait(pe, s_pT, g - 3)
                            wait(pe, s_res, g - 4)
                        cols = slice(n * INNER, (n + 1) * INNER)
                        pe.matmul(ps_qkv[:, n, :], x_hi[:], w_hi[:, cols], start=True, stop=False)
                        pe.matmul(ps_qkv[:, n, :], x_hi[:], w_lo[:, cols], start=False, stop=False)
                        pe.matmul(ps_qkv[:, n, :], x_lo[:], w_hi[:, cols], start=False,
                                  stop=True).then_inc(s_qkv, 1)
                if live(i, 0, N):
                    pe.wait_ge(s_xin, i + 1)
                    wait(pe, s_oT, 2 * (i - 4))
                    pe.transpose(ps_xT, xin[:], c("ident")).then_inc(s_xturned, 1)
                if live(i, 3, N):
                    g = i - 3
                    wait(pe, s_sub, g)
                    pe.wait_ge(s_qkT, 2 * (g + 1))
                    pe.matmul(ps_score[:], t["ident16"][:], t["causal16"][:], start=True, stop=False,
                              skip_group_check=True)
                    for x in range(LH // 2):
                        for s in range(2):
                            for e in range(2):
                                mm = pe.matmul(ps_score[e * SEQ:(e + 1) * SEQ, x * P + s * SEQ:x * P + (s + 1) * SEQ],
                                               qkT[e * LHD:(e + 1) * LHD, x, s * SEQ:(s + 1) * SEQ],
                                               qkT[e * LHD:(e + 1) * LHD, LH // 2 + x, s * SEQ:(s + 1) * SEQ],
                                               start=False, stop=True, skip_group_check=True)
                    mm.then_inc(s_sc, 1)
                if live(i, 4, N):
                    g = i - 4
                    pe.wait_ge(s_pn, g + 1)
                    pe.wait_ge(s_v, g + 4 if live(i, 1, N) else N)
                    wait(pe, s_res, g - 1)
                    for x in range(LH // 2):
                        mm = pe.transpose(ps_qkv[:, 2, x * P:(x + 1) * P],
                                          pnorm[:, 2 * x:2 * x + 2, :].rearrange("p s k -> p (s k)"), c("ident"))
                    mm.then_inc(s_pturned, 1)
                if live(i, 2, N):
                    g = i - 2
                    pe.wait_ge(s_rot, g + 1)
                    wait(pe, s_qkT, 2 * g)
                    for x in range(LH):
                        mm = pe.transpose(ps_qkT[:, x // 4, (x % 4) * P:(x % 4 + 1) * P],
                                          rot[:, 2 * x:2 * x + 2, :].rearrange("p s k -> p (s k)"), c("ident"))
                        if x % 4 == 3:
                            mm.then_inc(s_rturned, 1)
                if live(i, 5, N):
                    g = i - 5
                    pe.wait_ge(s_oT, 2 * (g + 1))
                    pe.wait_ge(s_pT, g + 2 if live(i, 4, N) else N)
                    wait(pe, s_res, g)
                    for x in range(LH // 2):
                        mm = pe.matmul(ps_y, oT[:, x, :], wo[:, x, :], start=(x == 0), stop=(x == LH // 2 - 1))
                    mm.then_inc(s_y, 1)
                if live(i, 4, N):
                    g = i - 4
                    pe.wait_ge(s_pT, g + 1)
                    if live(i, 0, N):
                        pe.wait_ge(s_xT, 2 * (i + 1))
                    apart(pe, s_apart)
                    for x in range(LH // 2):
                        for s, bank in ((0, ps_o0), (1, ps_o1)):
                            for e in range(2):
                                mm = pe.matmul(bank[e * LHD:(e + 1) * LHD, x * SEQ:(x + 1) * SEQ],
                                               v[s * SEQ:(s + 1) * SEQ, (par - 4) % 4,
                                                 (2 * x + e) * LHD:(2 * x + e + 1) * LHD],
                                               pT[s * SEQ:(s + 1) * SEQ, x * P + e * SEQ:x * P + (e + 1) * SEQ],
                                               start=True, stop=True)
                    mm.then_inc(s_av, 1)
            sweep(pe, N, LAG, 4, step)

        @block.scalar
        def _(act):
            act.preload_act_table_set("natural_log_exp_and_others")
            act.wait_ge(s_zero, 1)

            def step(i, par):
                if live(i, 1, N):
                    g = i - 1
                    wait(act, s_rcos, g)
                    wait(act, s_rsin, 2 * g)
                    act.wait_ge(s_qkv, 3 * g + 1)
                    act.activation(qk[:, 0:LH, :].rearrange("p h d -> p (h d)"), ps_qkv[:, 0, :],
                                   ACT.Copy).then_inc(s_qk, 1)
                if live(i, 1, N):
                    g = i - 1
                    act.wait_ge(s_qkv, 3 * g + 2)
                    act.activation(qk[:, LH:2 * LH, :].rearrange("p h d -> p (h d)"), ps_qkv[:, 1, :],
                                   ACT.Copy).then_inc(s_qk, 1)
                if live(i, 1, N):
                    g = i - 1
                    act.wait_ge(s_qkv, 3 * (g + 1))
                    wait(act, s_av, g - 3)
                    act.activation(v[:, (par - 1) % 4, :], ps_qkv[:, 2, :], ACT.Copy).then_inc(s_v, 1)
                if live(i, 0, N):
                    act.wait_ge(s_xturned, i + 1)
                    wait(act, s_xlo, i)
                    act.activation(xT[0:D // 2, :], ps_xT[0:D // 2, :], ACT.Copy).then_inc(s_xT, 1)
                    act.activation(xT[D // 2:D, :].rearrange("p (s t) -> p s t", t=SEQ)[:, :, 1:SEQ],
                                   ps_xT[D // 2:D, :].rearrange("p (s t) -> p s t", t=SEQ)[:, :, 0:SEQ - 1],
                                   ACT.Copy).then_inc(s_xT, 1)
                if live(i, 1, N):
                    g = i - 1
                    act.wait_ge(s_qk, 2 * (g + 1))
                    wait(act, s_ss, g)
                    act.activation(sq[:], qk[:], ACT.Square).then_inc(s_sq, 1)
                if live(i, 4, N):
                    g = i - 4
                    act.wait_ge(s_pturned, g + 1)
                    wait(act, s_av, g)
                    act.activation(pT[:], ps_qkv[:, 2, :], ACT.Copy).then_inc(s_pT, 1)
                if live(i, 2, N):
                    g = i - 2
                    wait(act, s_sc, g)
                    for n in range(2):
                        act.wait_ge(s_rturned, 2 * g + n + 1)
                        act.activation(qkT[:, 4 * n:4 * n + 4, :].rearrange("p x t -> p (x t)"), ps_qkT[:, n, :],
                                       ACT.Copy).then_inc(s_qkT, 1)
                if live(i, 3, N):
                    g = i - 3
                    act.wait_ge(s_sub, g + 1)
                    wait(act, s_pn, g)
                    act.activation(prob[:], score[:], ACT.Exp, scale=8.0).then_inc(s_exp, 1)
                if live(i, 1, N):
                    g = i - 1
                    act.wait_ge(s_ssc, g + 1)
                    act.activation(lss[:], ssc[:], ACT.Ln).then_inc(s_lss, 1)
                    act.wait_ge(s_lss, g + 1)
                    wait(act, s_rot, g)
                    act.activation(inv[:], lss[:], ACT.Exp, scale=-0.5).then_inc(s_inv, 1)
                if live(i, 4, N):
                    g = i - 4
                    act.wait_ge(s_av, g + 1)
                    wait(act, s_y, g)
                    for s, bank in ((0, ps_o0), (1, ps_o1)):
                        act.activation(oT[:, :, s * SEQ:(s + 1) * SEQ],
                                       bank[:, 0:LH // 2 * SEQ].rearrange("p (x t) -> p x t", t=SEQ),
                                       ACT.Copy).then_inc(s_oT, 1)
            sweep(act, N, LAG, 4, step)

        @block.vector
        def _(dve):
            cos, sin = c("rot")[:, 0:2 * LHD], c("rot")[:, 2 * LHD:4 * LHD]
            two = lambda a: a.rearrange("p (n d) -> p n d", d=LHD)
            heads = lambda a: a.rearrange("p (n h) d -> p n h d", n=2)
            tab = lambda a: a.unsqueeze(2).broadcast_to([P, 2, LH, a.shape[-1]])
            flat = ps_score[:].rearrange("p (h k) -> p h k", k=SEQ)
            dve.wait_ge(t["s_layers"], t["layers_loaded"])
            dve.tensor_tensor(costab[:], two(cos), qks[:], ALU.mult).then_inc(s_tab, 1)
            dve.tensor_tensor(sintab[:, :, 0:HT], two(sin)[:, :, 0:HT], qks[:, :, HT:LHD], ALU.mult).then_inc(s_tab, 1)
            dve.tensor_tensor(sintab[:, :, HT:LHD], two(sin)[:, :, HT:LHD], qks[:, :, 0:HT],
                              ALU.mult).then_inc(s_tab, 1)
            dve.memset(xT[:], 0.0).then_inc(s_zero, 1)
            dve.tensor_copy(w_hi[:], wqkv[:]).then_inc(s_whi, 1)
            dve.wait_ge(s_whi, 1)
            dve.tensor_tensor(w_lo[:], wqkv[:], w_hi[:].bitcast(F32), ALU.subtract).then_inc(s_wlo, 1)
            dve.wait_ge(s_tab, 3)

            def step(i, par):
                if live(i, 0, N):
                    wait(dve, s_xturned, i)
                    dve.tensor_copy(xin[:], Y[:, i, :]).then_inc(s_xin, 1)
                if live(i, 1, N):
                    g = i - 1
                    dve.wait_ge(s_qk, 2 * (g + 1))
                    wait(dve, s_rsum, g)
                    dve.tensor_tensor(heads(rcos[:]), heads(qk[:]), tab(costab[:]), ALU.mult).then_inc(s_rcos, 1)
                if live(i, 1, N):
                    for lo, hi in ((0, HT), (HT, 0)):
                        dve.tensor_tensor(heads(rsin[:])[:, :, :, lo:lo + HT], heads(qk[:])[:, :, :, hi:hi + HT],
                                          tab(sintab[:, :, lo:lo + HT]), ALU.mult).then_inc(s_rsin, 1)
                if live(i, 3, N):
                    g = i - 3
                    dve.wait_ge(s_sc, g + 1)
                    dve.tensor_reduce(smax[:], flat, X_AXIS, ALU.max).then_inc(s_max, 1)
                if live(i, 0, N):
                    dve.wait_ge(s_xT, 2 * (i + 1))
                    wait(dve, s_qkv, 3 * i)
                    dve.tensor_copy(x_hi[:], xT[:]).then_inc(s_xhi, 1)
                    dve.wait_ge(s_xhi, i + 1)
                    dve.tensor_tensor(x_lo[:], xT[:], x_hi[:].bitcast(F32), ALU.subtract).then_inc(s_xlo, 1)
                if live(i, 3, N):
                    g = i - 3
                    dve.wait_ge(s_max, g + 1)
                    wait(dve, s_exp, g)
                    dve.tensor_tensor(score[:], flat, smax[:].unsqueeze(2).broadcast_to([P, LH, SEQ]),
                                      ALU.subtract).then_inc(s_sub, 1)
                if live(i, 1, N):
                    g = i - 1
                    dve.wait_ge(s_sq, g + 1)
                    dve.tensor_reduce(ss[:], sq[:], X_AXIS, ALU.add).then_inc(s_ss, 1)
                if live(i, 1, N):
                    g = i - 1
                    dve.wait_ge(s_ss, g + 1)
                    wait(dve, s_lss, g)
                    dve.tensor_scalar(ssc[:], ss[:], 1e-24, None, ALU.max).then_inc(s_ssc, 1)
                if live(i, 3, N):
                    g = i - 3
                    dve.wait_ge(s_exp, g + 1)
                    dve.tensor_reduce(ssum[:], prob[:], X_AXIS, ALU.add).then_inc(s_sum, 1)
                if live(i, 5, N):
                    g = i - 5
                    dve.wait_ge(s_y, g + 1)
                    dve.tensor_tensor(Y[:, g, :], ps_y, Y[:, g, :], ALU.add).then_inc(s_res, 1)
                if live(i, 3, N):
                    g = i - 3
                    dve.wait_ge(s_sum, g + 1)
                    wait(dve, s_pn, g)
                    dve.reciprocal(sinv[:], ssum[:]).then_inc(s_sinv, 1)
            sweep(dve, N, LAG, 4, step)

        @block.gpsimd
        def _(pool):
            def step(i, par):
                if live(i, 1, N):
                    g = i - 1
                    pool.wait_ge(s_rcos, g + 1)
                    pool.wait_ge(s_rsin, 2 * (g + 1))
                    wait(pool, s_rot, g)
                    pool.tensor_tensor(rsum[:], rcos[:], rsin[:], ALU.add).then_inc(s_rsum, 1)
                    pool.wait_ge(s_rsum, g + 1)
                    pool.wait_ge(s_inv, g + 1)
                    wait(pool, s_rturned, 2 * g)
                    pool.tensor_tensor(rot[:], rsum[:], inv[:].unsqueeze(2).broadcast_to([P, 2 * LH, LHD]),
                                       ALU.mult).then_inc(s_rot, 1)
                if live(i, 3, N):
                    g = i - 3
                    pool.wait_ge(s_sinv, g + 1)
                    wait(pool, s_pturned, g)
                    pool.tensor_tensor(pnorm[:], prob[:], sinv[:].unsqueeze(2).broadcast_to([P, LH, SEQ]),
                                       ALU.mult).then_inc(s_pn, 1)
            sweep(pool, N, LAG, 4, step)


def gated_ffn(nc, t, dram, layer):
    last = layer == DEPTH - 1
    with ExitStack() as ctx:
        def sb(name, shape, dt=F32):
            return ctx.enter_context(nc.sbuf_tensor(f"f{layer}_{name}", shape, dt))

        def ps(name, shape):
            return ctx.enter_context(nc.psum_tensor(f"f{layer}_{name}", shape, F32))

        phase_sems = Semaphores(nc)
        ctx.callback(phase_sems.clear)

        def sem(name):
            return phase_sems(f"f{layer}_{name}")

        X, Y, c = t["X"], t["Y"], t["c"]
        w1, w2, cols, b2 = t["w1"][layer], t["w2"][layer], t["ffncols"][layer], t["b2"][layer]
        H2 = D // 2
        NCH = len(HCH)
        w_hi, w_lo = sb("w_hi", [P, 2 * HID], F32R), sb("w_lo", [P, 2 * HID], F32R)
        x_in = sb("x_in", [P, 2, GT, D])
        stats, meanvar = sb("stats", [P, GT, 6]), sb("meanvar", [P, 2, GT, 2])
        vareps, rstd = sb("vareps", [P, GT]), sb("rstd", [P, GT])
        h = sb("h", [P, GT, D])
        hT = sb("hT", [P, GN])
        h_hi, h_lo = sb("h_hi", [P, 2, GN], F32R), sb("h_lo", [P, 2, GN], F32R)
        gelu = sb("gelu", [P, 2, GN])
        gated = sb("gated", [P, 2, NCH, GN])

        ps_shift = ps("ps_shift", [P, GT, P])
        ps_turn = ps("ps_turn", [P, GN])
        ps_a = ps("ps_a", [P, 2, GN])
        ps_g = ps("ps_g", [P, 2, GN])
        ps_out = ps("ps_out", [P, GT, D])

        s_whi, s_wlo = sem("w_hi_ready"), sem("w_lo_ready")
        s_shift, s_in, s_stats, s_meanvar, s_rstd = (sem(n) for n in ("shifted", "x_in_ready", "stats_done",
                                                                      "meanvar_done", "rstd_ready"))
        s_h, s_turned, s_hT, s_hhi, s_hlo = (sem(n) for n in ("h_ready", "h_turned", "hT_ready", "h_hi_ready",
                                                              "h_lo_ready"))
        s_a, s_g, s_gelu, s_gated, s_out, s_bias, s_bias2, s_res = (
            sem(n) for n in ("a_done", "g_done", "gelu_ready", "gated_ready", "out_done", "bias_added", "x_added",
                             "residual_done"))
        s_store, s_apart, s_vareps = sem("stored"), sem("apart"), sem("variance_ready")
        N, LAG = GROUPS, 3
        block = ctx.enter_context(nc.Block())

        if last:
            @block.sync
            def _(sp):
                def step(i, par):
                    if live(i, 3, N):
                        g = i - 3
                        sp.wait_ge(s_res, g + 1)
                        dst = dram["out"].rearrange("(t p) f -> p t f", p=P)
                        sp.dma_start(dst[:, bass.ds(g * GT, GT), :], group_rows(Y, g)).then_inc(s_store, 16)
                sweep(sp, N, LAG, 2, step)
                sp.wait_ge(s_store, 16 * N)

        @block.tensor
        def _(pe):
            pe.wait_ge(s_whi, 1)
            pe.wait_ge(s_wlo, 1)

            def hidden(g, par, chunks):
                for n in chunks:
                    m, b = HCH[n], (NCH * par + n) % 2
                    for bank, at, done, used in ((ps_g, HID, s_g, s_gelu), (ps_a, 0, s_a, s_gated)):
                        wait(pe, used, NCH * g + n - 1)
                        part = slice(at + n * P, at + n * P + m)
                        out = bank[0:m, b, :]
                        pe.matmul(out, w_hi[:, part], h_hi[:, par, :], start=True, stop=False)
                        pe.matmul(out, w_hi[:, part], h_lo[:, par, :], start=False, stop=False)
                        pe.matmul(out, w_lo[:, part], h_hi[:, par, :], start=False, stop=True).then_inc(done, 1)

            def step(i, par):
                if live(i, 2, N):
                    pe.wait_ge(s_hlo, i - 1)
                    hidden(i - 2, par, (0,))
                if live(i, 3, N):
                    g = i - 3
                    pe.wait_ge(s_gated, NCH * (g + 1))
                    wait(pe, s_res, g)
                    for j in range(GT):
                        for n, m in enumerate(HCH):
                            mm = pe.matmul(ps_out[:, j, :], gated[0:m, 1 - par, n, j * P:(j + 1) * P], w2[0:m, n, :],
                                           start=(n == 0), stop=(n == NCH - 1))
                    mm.then_inc(s_out, 1)
                if live(i, 1, N):
                    g = i - 1
                    pe.wait_ge(s_h, GT * (g + 1))
                    wait(pe, s_hT, g)
                    for j in range(GT):
                        mm = pe.transpose(ps_turn[:, j * P:(j + 1) * P], h[:, j, :], c("ident"))
                    mm.then_inc(s_turned, 1)
                if live(i, 0, N):
                    wait(pe, s_in, 2 * i)
                    pe.matmul(ps_shift[:, :, H2:D], c("shift"), Y[:, bass.ds(i * GT, GT), H2:D],
                              start=True, stop=True).then_inc(s_shift, 1)
                if live(i, 2, N):
                    hidden(i - 2, par, (1, 2))
            sweep(pe, N, LAG, 2, step)

        @block.scalar
        def _(act):
            act.preload_act_table_set("gelu_and_others")

            def gelus(g, par, chunks):
                for n in chunks:
                    m, b = HCH[n], (NCH * par + n) % 2
                    act.wait_ge(s_g, NCH * g + n + 1)
                    wait(act, s_gated, NCH * g + n - 1)
                    act.activation(gelu[0:m, b, :], ps_g[0:m, b, :], ACT.Gelu,
                                   bias=cols[0:m, 3 + n:4 + n]).then_inc(s_gelu, 1)

            def step(i, par):
                if live(i, 2, N):
                    gelus(i - 2, par, (0,))
                if live(i, 1, N):
                    g = i - 1
                    act.wait_ge(s_turned, g + 1)
                    wait(act, s_hlo, g)
                    act.activation(hT[:], ps_turn[:], ACT.Identity, bias=cols[:, 7:8],
                                   scale=cols[:, 6:7]).then_inc(s_hT, 1)
                if live(i, 0, N):
                    wait(act, s_h, GT * (i - 1))
                    act.activation(x_in[:, par, :, 0:H2], Y[:, bass.ds(i * GT, GT), 0:H2], ACT.Copy).then_inc(s_in, 1)
                    act.wait_ge(s_shift, i + 1)
                    act.activation(x_in[:, par, :, H2:D], ps_shift[:, :, H2:D], ACT.Copy).then_inc(s_in, 1)
                if live(i, 2, N):
                    gelus(i - 2, par, (1, 2))
            sweep(act, N, LAG, 2, step)

        @block.vector
        def _(dve):
            dve.tensor_copy(w_hi[:], w1[:]).then_inc(s_whi, 1)
            dve.wait_ge(s_whi, 1)
            dve.tensor_tensor(w_lo[:], w1[:], w_hi[:].bitcast(F32), ALU.subtract).then_inc(s_wlo, 1)

            def gate(g, par, n):
                m, b = HCH[n], (NCH * par + n) % 2
                wait(dve, s_out, g - 1)
                dve.wait_ge(s_a, NCH * g + n + 1)
                dve.wait_ge(s_gelu, NCH * g + n + 1)
                dve.scalar_tensor_tensor(out=gated[0:m, par, n, :], in0=ps_a[0:m, b, :],
                                         scalar=cols[0:m, n:n + 1], in1=gelu[0:m, b, :],
                                         op0=ALU.add, op1=ALU.mult).then_inc(s_gated, 1)

            def step(i, par):
                if live(i, 2, N):
                    gate(i - 2, par, 0)
                if live(i, 1, N):
                    g = i - 1
                    dve.wait_ge(s_rstd, g + 1)
                    wait(dve, s_turned, g)
                    for j in range(GT):
                        dve.tensor_scalar(h[:, j, :], x_in[:, 1 - par, j, :], meanvar[:, 1 - par, j, 0:1],
                                          rstd[:, j:j + 1], ALU.subtract, ALU.mult).then_inc(s_h, 1)
                if live(i, 3, N):
                    g = i - 3
                    dve.wait_ge(s_out, g + 1)
                    dve.wait_ge(s_bias2 if last else s_bias, g + 1)
                    dve.tensor_tensor(group_rows(Y, g), ps_out[:], group_rows(Y, g), ALU.add).then_inc(s_res, 1)
                if live(i, 1, N):
                    g = i - 1
                    dve.wait_ge(s_hT, g + 1)
                    wait(dve, s_a, NCH * (g - 1))
                    dve.tensor_copy(h_hi[:, 1 - par, :], hT[:]).then_inc(s_hhi, 1)
                    dve.wait_ge(s_hhi, g + 1)
                    dve.tensor_tensor(h_lo[:, 1 - par, :], hT[:], h_hi[:, 1 - par, :].bitcast(F32),
                                      ALU.subtract).then_inc(s_hlo, 1)
                if live(i, 2, N):
                    gate(i - 2, par, 1)
                if live(i, 0, N):
                    dve.wait_ge(s_in, 2 * (i + 1))
                    wait(dve, s_meanvar, GT * i)
                    for j in range(GT):
                        dve.bn_stats(stats[:, j, :], x_in[:, par, j, :]).then_inc(s_stats, 1)
                    dve.wait_ge(s_stats, GT * (i + 1))
                    apart(dve, s_apart)
                    for j in range(GT):
                        dve.bn_aggr(meanvar[:, par, j, :], stats[:, j, :]).then_inc(s_meanvar, 1)
                    dve.wait_ge(s_meanvar, GT * (i + 1))
                    wait(dve, s_rstd, i)
                    dve.tensor_scalar(vareps[:], meanvar[:, par, :, 1], LN_EPS, None, ALU.add).then_inc(s_vareps, 1)
                if live(i, 2, N):
                    gate(i - 2, par, 2)
            sweep(dve, N, LAG, 2, step)

        @block.gpsimd
        def _(pool):
            def step(i, par):
                if live(i, 1, N):
                    g = i - 1
                    pool.wait_ge(s_in, 2 * (g + 1))
                    pool.tensor_tensor(group_rows(Y, g), group_rows(Y, g),
                                       b2[:].unsqueeze(1).broadcast_to([P, GT, D]), ALU.add).then_inc(s_bias, 1)
                    if last:
                        pool.wait_ge(s_bias, g + 1)
                        pool.tensor_tensor(group_rows(Y, g), group_rows(Y, g), group_rows(X, g),
                                           ALU.add).then_inc(s_bias2, 1)
                if live(i, 0, N):
                    pool.wait_ge(s_vareps, i + 1)
                    wait(pool, s_h, GT * i)
                    pool.tensor_tensor(rstd[:], vareps[:], c("eps")[:, 3:4].broadcast_to([P, GT]),
                                       ALU.pow).then_inc(s_rstd, 1)
            sweep(pool, N, LAG, 2, step)


def build(nc, dram):
    with ExitStack() as ctx:
        def sb(name, shape, dt=F32):
            return ctx.enter_context(nc.sbuf_tensor(name, shape, dt))

        t = {"const": sb("const", [P, NCONST]), "X": sb("X", [P, TILES, D])}
        t["c"] = lambda name: t["const"][:, CONSTS[name][0]:CONSTS[name][1]]
        for name in ("wq", "wk", "wv", "wo"):
            t[name] = sb(name, [P, D])
        t["abias"] = sb("abias", [P, 3])
        t["bo"] = sb("bo", [P, D])
        t["winspread"] = sb("winspread", [WIN * AH, WIN, P])
        t["winfold"] = sb("winfold", [P, WIN, WIN * AH])
        t["winspread_r"] = sb("winspread_r", [WIN * AH, WIN, P], F32R)
        for name in ("gate_q", "gate_k", "gate_v", "gate_kv", "gate_bias"):
            t[name] = sb(name, [P, 2 * MH])
        t["rms"] = sb("rms", [P, MHD])
        t["kpad"] = sb("kpad", [P, GS, PADSEQ])
        t["vpad"] = sb("vpad", [P, NSEQ, PADSEQ])
        t["ctxpad"] = sb("ctxpad", [P, 2, GT, MH, MHD + 1])
        t["qdiag"] = sb("qdiag", [P, 2, GS, MH, SEQ])
        t["ident16"] = sb("ident16", [P, P], BF16)
        t["causal16"] = sb("causal16", [P, 8, SEQ], BF16)
        t["keyquery16"] = sb("keyquery16", [P, 8, SEQ], BF16)
        t["Y"] = sb("Y", [P, TILES, D])
        t["rms1"] = sb("rms1", [P, MHD])
        for name, shape in (("wqkv", [P, 3 * INNER]), ("lwo", [P, LH // 2, D]), ("qks", [P, 2, LHD]),
                            ("w1", [P, 2 * HID]), ("w2", [P, len(HCH), D]), ("ffncols", [P, 8]), ("b2", [P, D])):
            t[name] = [sb(f"{name}{layer}", shape) for layer in range(DEPTH)]
        t["s_layers"] = ctx.enter_context(nc.semaphore("layer_weights_loaded"))
        load_phase(nc, t, dram)
        window_attention(nc, t)
        mlstm(nc, t, dram)
        for layer in range(DEPTH):
            causal_attention(nc, t, layer)
            gated_ffn(nc, t, dram, layer)


def shape_constants():
    p = np.arange(P)
    tok = p % SEQ
    out = np.zeros((P, NCONST), np.float32)

    def put(name, a):
        out[:, CONSTS[name][0]:CONSTS[name][1]] = a
    same = (p[:, None] // SEQ) == (p[None, :] // SEQ)
    put("ident", np.eye(P))
    place = tok[:, None] + np.arange(WIN)[None, :] - HALF
    put("winmask", np.repeat(np.where((place >= 0) & (place < SEQ), 0.0, NEG), AH, axis=1))
    put("causal", np.where(np.arange(SEQ)[None, :] > tok[:, None], NEG, 0.0))
    put("keyquery", np.where(np.arange(SEQ)[None, :] < tok[:, None], NEG, 0.0))
    put("tri", same & (p[:, None] <= p[None, :]))
    put("negfold", -(tok[:, None] == np.arange(SEQ)[None, :]).astype(np.float32))
    put("sameseq", same)
    put("shift", same & (p[:, None] + 1 == p[None, :]))
    put("eps", np.tile(np.array([LN_EPS, 1e-6, 1.0, -0.5], np.float32), (P, 1)))
    put("seqstart", np.where(p[None, :] % SEQ == 0, NEG, 0.0) * np.ones((P, 1)))
    half = np.arange(0, LHD, 2, dtype=np.float32)
    freq = np.arange(SEQ, dtype=np.float32)[:, None] * (np.float32(1.0) / np.float32(10000.0) ** (half / LHD))[None, :]
    freq = np.concatenate([freq, freq], -1)
    base = (half + np.float32(0.4 * LHD)) / np.float32(1.4 * LHD)
    power = (np.arange(SEQ, dtype=np.float32) - SEQ // 2) / np.float32(32.0)
    scale = base[None, :] ** power[:, None]
    scale = np.concatenate([scale, scale], -1)
    sign = np.where(np.arange(LHD) < LHD // 2, -1.0, 1.0).astype(np.float32)
    cos, sin = np.cos(freq), np.sin(freq) * sign
    put("rot", np.tile(np.concatenate([cos * scale, cos / scale, sin * scale, sin / scale], 1), (2, 1)))
    spread = np.zeros((WIN, AH, WIN, P), np.float32)
    for w in range(WIN):
        spread[w, :, w, :] = np.arange(AH)[:, None] == p[None, :] // AHD
    spread = spread.reshape(WIN * AH, WIN, P)
    return out, spread, spread.transpose(2, 1, 0)


def kernel(**inputs):
    import concourse.bacc as bacc
    from concourse.bass_utils import run_bass_kernel_spmd

    def arr(name):
        return np.asarray(inputs[name])

    def rows(a):
        return np.ascontiguousarray(np.broadcast_to(np.asarray(a).reshape(1, -1), (P, np.asarray(a).size)))

    const, spread, fold = shape_constants()
    ins = {
        "x": arr("x").reshape(TOKENS, D), "ctx": arr("ctx_1024").reshape(TOKENS, D), "const": const,
        "winspread": spread, "winfold": fold,
        "wq": arr("L0_attn_Wq").T, "wk": arr("L0_attn_Wk").T, "wv": arr("L0_attn_Wv").T, "wo": arr("L0_attn_Wo").T,
        "abias": np.stack([arr("L0_attn_bq"), arr("L0_attn_bk"), arr("L0_attn_bv")], 1),
        "bo": rows(arr("L0_attn_bo")),
    }
    gates = np.concatenate([arr("L0_xattn_igate_kernel"), arr("L0_xattn_fgate_kernel")], 1)
    ins["gate_q"], ins["gate_k"], ins["gate_v"] = gates[:D], gates[D:2 * D], gates[2 * D:]
    ins["gate_bias"] = rows(np.concatenate([arr("L0_xattn_igate_bias"), arr("L0_xattn_fgate_bias")]))
    ins["rms"] = rows(arr("L0_xattn_rms_scale"))

    pad = np.zeros(P - HCH[-1], np.float32)
    for layer in range(DEPTH):
        w1b = arr("L0_ffn_b1")[layer]
        chunks = []
        for at in (0, HID):
            for n, m in enumerate(HCH):
                col = w1b[at + n * P:at + n * P + m]
                chunks.append(col if m == P else np.concatenate([col, pad]))
        w2 = arr("L0_ffn_w2")[layer]
        ins[f"wqkv{layer}"] = arr("L0_ffn_wqkv")[layer]
        ins[f"lwo{layer}"] = arr("L0_ffn_wo")[layer].reshape(LH // 2, P, D).transpose(1, 0, 2)
        ins[f"qks{layer}"] = rows(np.stack([arr("L0_ffn_q_scale")[layer], arr("L0_ffn_k_scale")[layer]])).reshape(
            P, 2, LHD)
        ins[f"w1{layer}"] = arr("L0_ffn_w1")[layer]
        ins[f"w2{layer}"] = np.concatenate([w2, np.zeros((len(HCH) * P - HID, D), np.float32)]).reshape(
            len(HCH), P, D).transpose(1, 0, 2)
        ins[f"ffncols{layer}"] = np.stack(chunks + [arr("L0_ffn_ln_g")[layer], arr("L0_ffn_ln_b")[layer]], 1)
        ins[f"b2{layer}"] = rows(arr("L0_ffn_b2")[layer])

    nc = bacc.Bacc("TRN2", target_bir_lowering=False, num_devices=1)
    arrays, dram = {}, {}
    for name, a in ins.items():
        a = np.ascontiguousarray(a)
        arrays[f"in_{name}"] = a
        dram[name] = nc.dram_tensor(f"in_{name}", list(a.shape), mybir.dt.from_np(a.dtype), kind="ExternalInput").ap()
    dram["out"] = nc.dram_tensor("out", [TOKENS, D], F32, kind="ExternalOutput").ap()
    build(nc, dram)
    r = run_bass_kernel_spmd(nc, [arrays], core_ids=[0])
    return np.asarray(r.results[0]["out"]).reshape(NSEQ, SEQ, D)
```

```python
from contextlib import ExitStack

import numpy as np
import concourse.bass as bass
from concourse import mybir

F32 = mybir.dt.float32
F32R = mybir.dt.float32r
BF16 = mybir.dt.bfloat16
ALU = mybir.AluOpType
ACT = mybir.ActivationFunctionType
X_AXIS = mybir.AxisListType.X

P = 128
NSEQ, SEQ, D = 64, 64, 128
TOKENS = NSEQ * SEQ
TILES = TOKENS // P
GT = 4
GROUPS = TILES // GT
GN = GT * P
GS = GN // SEQ
AH, AHD, WIN = 16, 8, 5
HALF = WIN // 2
PADSEQ = SEQ + 2 * HALF
MH, MHD = 4, 32
LH, LHD = 8, 64
INNER = LH * LHD
HID = 341
HCH = (128, 128, 85)
DEPTH = 2
NEG = -1e30
LN_EPS = 1e-5

CONSTS = {}
_at = 0
for _name, _n in (("ident", 128), ("winmask", WIN * AH), ("eps", 4),
                  ("causal", SEQ), ("keyquery", SEQ), ("tri", 128), ("negfold", SEQ), ("sameseq", 128),
                  ("shift", 128), ("rot", 4 * LHD), ("seqstart", 128)):
    CONSTS[_name] = (_at, _at + _n)
    _at += _n
NCONST = _at
EARLY = CONSTS["causal"][0]

SMALLS = {}
_at = 0
for _name, _n in (("abias", 3), ("bo", D), ("gate_q", 2 * MH), ("gate_k", 2 * MH), ("gate_v", 2 * MH),
                  ("gate_bias", 2 * MH), ("rms", MHD)):
    SMALLS[_name] = (_at, _at + _n)
    _at += _n
NSMALL = _at


def ahead(n):
    return not isinstance(n, int) or n > 0


def wait(eng, sem, n):
    if ahead(n):
        eng.wait_ge(sem, n)


def live(i, lag, n):
    return not isinstance(i, int) or 0 <= i - lag < n


def sweep(eng, n, lag, unroll, step):
    first = -(-(lag + 1) // unroll) * unroll
    for i in range(first):
        step(i, i % unroll)
    with eng.Fori(first // unroll, n // unroll) as u:
        for k in range(unroll):
            step(u * unroll + k if unroll > 1 else u, k)
    for i in range(n, n + lag):
        step(i, i % unroll)


def group_rows(x, g):
    return x[:, bass.ds(g * GT, GT), :]


LAYER_INPUTS = ("wqkv", "lwo", "qks", "w1", "w2", "ffncols", "b2")


class Semaphores:

    def __init__(self, nc):
        self.nc, self.all = nc, []

    def __call__(self, name):
        self.all.append(self.nc.alloc_semaphore(name))
        return self.all[-1]

    def clear(self):
        self.nc.clear_and_free_semaphores(self.all)
        self.nc.all_engine_barrier()


def apart(eng, sem):
    eng.sem_inc(sem, 1)


def split_weights(pool, w, hi, lo, s_split):
    pool.tensor_copy(hi[:], w[:]).then_inc(s_split, 1)
    pool.wait_ge(s_split, 1)
    pool.tensor_tensor(lo[:], w[:], hi[:].bitcast(F32), ALU.subtract).then_inc(s_split, 1)


class Norm:

    def __init__(self, sb, sem, tag):
        self.stats = sb(f"{tag}_stats", [P, GT, 6])
        self.meanvar = sb(f"{tag}_meanvar", [P, GT, 2])
        self.logvar = sb(f"{tag}_logvar", [P, GT])
        self.rstd = sb(f"{tag}_rstd", [P, GT])
        self.s_stats = sem(f"{tag}_stats_done")
        self.s_meanvar = sem(f"{tag}_meanvar_done")
        self.s_logvar = sem(f"{tag}_logvar_done")
        self.s_rstd = sem(f"{tag}_rstd_done")
        self.s_apart = sem(f"{tag}_apart")


def norm_stats(dve, nm, x, g):
    for j in range(GT):
        dve.bn_stats(nm.stats[:, j, :], x[:, g * GT + j, :]).then_inc(nm.s_stats, 1)
    dve.wait_ge(nm.s_stats, (g + 1) * GT)
    apart(dve, nm.s_apart)
    for j in range(GT):
        dve.bn_aggr(nm.meanvar[:, j, :], nm.stats[:, j, :]).then_inc(nm.s_meanvar, 1)


def norm_rstd(act, nm, eps, g):
    act.wait_ge(nm.s_meanvar, (g + 1) * GT)
    act.activation(nm.logvar[:, :], nm.meanvar[:, :, 1], ACT.Ln, bias=eps).then_inc(nm.s_logvar, 1)
    act.wait_ge(nm.s_logvar, g + 1)
    act.activation(nm.rstd[:, :], nm.logvar[:, :], ACT.Exp, scale=-0.5).then_inc(nm.s_rstd, 1)


def norm_apply(dve, nm, out, x, g, s_out):
    dve.wait_ge(nm.s_rstd, g + 1)
    for j in range(GT):
        dve.tensor_scalar(out(j), x[:, g * GT + j, :], nm.meanvar[:, j, 0:1], nm.rstd[:, j:j + 1],
                          ALU.subtract, ALU.mult).then_inc(s_out, 1)


def first(i, lag):
    return isinstance(i, int) and i == lag


def window_attention(nc, t, dram):
    with ExitStack() as ctx:
        def sb(name, shape, dt=F32):
            return ctx.enter_context(nc.sbuf_tensor(name, shape, dt))

        def ps(name, shape):
            return ctx.enter_context(nc.psum_tensor(name, shape, F32))

        sem = Semaphores(nc)
        ctx.callback(sem.clear)

        X, c = t["X"], t["c"]
        kpad, vpad = t["kpad"], t["vpad"]
        nm = Norm(sb, sem, "an")
        shift = sb("a_shift", [P, GT])
        h = sb("a_h", [P, GT, D])
        hT = sb("a_hT", [P, GN])
        q = sb("a_q", [P, GS, SEQ])
        prod = sb("a_prod", [P, WIN, GN])
        scT = sb("a_scT", [WIN * AH, GN])
        score = sb("a_score", [P, GT, WIN, AH])
        prob = sb("a_prob", [P, GT, WIN, AH])
        pnorm = sb("a_pnorm", [P, GT, WIN, AH])
        smax = sb("a_smax", [P, GT, AH])
        ssum = sb("a_ssum", [P, GT, AH])
        sinv = sb("a_sinv", [P, GT, AH])
        p_hi, p_lo = sb("a_p_hi", [WIN * AH, GN], F32R), sb("a_p_lo", [WIN * AH, GN], F32R)
        pv = sb("a_pv", [P, WIN, GN])
        acc = sb("a_acc", [P, WIN - 2, GN])
        attnT = sb("a_attnT", [P, GN])

        ps_turn = ps("a_ps_turn", [P, GN])
        ps_qkv = ps("a_ps_qkv", [P, 3, GN])
        ps_score = ps("a_ps_score", [P, 512])
        ps_spread = ps("a_ps_spread", [P, 2, GN])
        ps_out = ps("a_ps_out", [P, GT, D])
        ps_pT = ps_out[0:WIN * AH, :, :].rearrange("p j d -> p (j d)")

        s_shift, s_h, s_turned, s_hT = sem("a_shift_ready"), sem("a_h_ready"), sem("a_h_turned"), sem("a_hT_ready")
        s_qkv, s_q, s_k, s_v = sem("a_qkv_done"), sem("a_q_ready"), sem("a_k_ready"), sem("a_v_ready")
        s_prod_d, s_prod_p = sem("a_prod_vector"), sem("a_prod_pool")
        s_sc, s_masked, s_max, s_sub = sem("a_scores_done"), sem("a_masked"), sem("a_max_done"), sem("a_shifted")
        s_exp, s_sum, s_inv, s_pn = sem("a_exp_done"), sem("a_sum_done"), sem("a_inverse_done"), sem("a_probs_ready")
        s_pturned, s_phi, s_plo = sem("a_probs_turned"), sem("a_p_hi_ready"), sem("a_p_lo_ready")
        s_folded, s_scT, s_apart = sem("a_scores_folded"), sem("a_scT_ready"), sem("a_apart")
        s_spread, s_pv, s_acc = sem("a_probs_spread"), sem("a_pv_ready"), sem("a_sum_of_pv")
        s_out, s_res, s_bias = sem("a_out_done"), sem("a_residual_done"), sem("a_bias_added")

        eps = c("eps")[:, 0:1]
        s_const, s_consts = sem("a_first_constants_loaded"), sem("a_constants_loaded")
        s_x = [sem(f"a_x_loaded{g}") for g in range(GROUPS)]
        s_w, s_small, s_fold_in, s_spread_in = (sem(f"a_{n}_loaded") for n in ("weights", "small_inputs", "winfold",
                                                                               "winspread"))
        s_pads, s_cast, s_made = sem("a_pads_zeroed"), sem("a_winspread_ready"), sem("a_later_constants_ready")
        maskb = c("winmask").unsqueeze(1).broadcast_to([P, GT, WIN * AH])
        N = GROUPS
        LAG = 4
        block = ctx.enter_context(nc.Block())

        @block.sync
        def _(sp):
            x_in = dram["x"].rearrange("(t p) f -> p t f", p=P)
            for g in range(GROUPS):
                sp.dma_start(group_rows(X, g), x_in[:, g * GT:(g + 1) * GT, :]).then_inc(s_x[g], 16)
                if g == 0:
                    sp.dma_start(t["const"][:, EARLY:], dram["const"][:, EARLY:]).then_inc(s_consts, 16)
            for name in LAYER_INPUTS:
                for layer in range(DEPTH):
                    sp.dma_start(t[name][layer][:], dram[f"{name}{layer}"]).then_inc(t["s_layers"], 16)

        @block.tensor
        def _(pe):
            pe.wait_ge(s_const, 16)
            pe.wait_ge(s_w, 16)

            def project(g, names):
                for n, w in names:
                    wait(pe, (s_q, s_k, s_v)[n], g)
                    pe.matmul(ps_qkv[:, n, :], t[w], hT[:, :], start=True, stop=True).then_inc(s_qkv, 1)

            def spread(g, places):
                for w in places:
                    wait(pe, s_pv, WIN * g + max(w - 1, 0))
                    pe.matmul(ps_spread[:, w % 2, :], t["winspread_r"][:, w, :], p_hi[:, :], start=True, stop=False)
                    pe.matmul(ps_spread[:, w % 2, :], t["winspread_r"][:, w, :], p_lo[:, :],
                              start=False, stop=True).then_inc(s_spread, 1)

            def fold(places):
                for w in places:
                    mm = pe.matmul(ps_turn[0:WIN * AH, :], t["winfold"][:, w, :], prod[:, w, :],
                                   start=(w == 0), stop=(w == WIN - 1), skip_group_check=True)
                return mm

            def step(i, _):
                if live(i, 1, N):
                    g = i - 1
                    pe.wait_ge(s_h, GT * (g + 1))
                    wait(pe, s_scT, g - 1)
                    for j in range(GT):
                        mm = pe.transpose(ps_turn[:, j * P:(j + 1) * P], h[:, j, :], c("ident"))
                    mm.then_inc(s_turned, 1)
                if live(i, 4, N):
                    spread(i - 4, (3,))
                if live(i, 4, N):
                    spread(i - 4, (4,))
                if live(i, 2, N):
                    g = i - 2
                    pe.wait_ge(s_prod_d, 3 * (g + 1))
                    pe.wait_ge(s_prod_p, 2 * (g + 1))
                    pe.wait_ge(s_hT, g + 2 if live(i, 1, N) else N)
                    if first(i, 2):
                        pe.wait_ge(s_fold_in, 16)
                    fold((0, 1))
                if live(i, 2, N):
                    fold((2, 3, 4)).then_inc(s_folded, 1)
                if live(i, 4, N):
                    g = i - 4
                    pe.wait_ge(s_acc, 4 * (g + 1))
                    pe.wait_ge(s_plo, g + 1)
                    for j in range(GT):
                        mm = pe.matmul(ps_out[:, j, :], attnT[:, j * P:(j + 1) * P], t["wo"],
                                       start=True, stop=True)
                    mm.then_inc(s_out, 1)
                if live(i, 1, N):
                    pe.wait_ge(s_hT, i)
                    project(i - 1, ((0, "wq"),))
                if live(i, 2, N):
                    g = i - 2
                    pe.wait_ge(s_scT, g + 1)
                    wait(pe, s_masked, g)
                    apart(pe, s_apart)
                    for j in range(GT):
                        mm = pe.transpose(ps_score[:, j * WIN * AH:(j + 1) * WIN * AH], scT[:, j * P:(j + 1) * P],
                                          c("ident")[0:WIN * AH, 0:WIN * AH])
                    mm.then_inc(s_sc, 1)
                if live(i, 3, N):
                    g = i - 3
                    pe.wait_ge(s_pn, g + 1)
                    wait(pe, s_res, g)
                    for j in range(GT):
                        mm = pe.transpose(ps_pT[:, j * P:(j + 1) * P],
                                          pnorm[:, j, :, :].rearrange("p w h -> p (w h)"), c("ident"))
                    mm.then_inc(s_pturned, 1)
                if live(i, 1, N):
                    project(i - 1, ((1, "wk"),))
                if live(i, 1, N):
                    project(i - 1, ((2, "wv"),))
                if live(i, 3, N):
                    pe.wait_ge(s_plo, i - 2)
                    if first(i, 3):
                        pe.wait_ge(s_cast, 1)
                    spread(i - 3, (0, 1))
                if live(i, 3, N):
                    spread(i - 3, (2,))
            sweep(pe, N, LAG, 1, step)

        @block.scalar
        def _(act):
            act.dma_start(t["const"][:, 0:EARLY], dram["const"][:, 0:EARLY]).then_inc(s_const, 16)
            act.dma_start(t["w4"][:], dram["w4"]).then_inc(s_w, 16)
            act.dma_start(t["small"][:], dram["small"]).then_inc(s_small, 16)
            act.dma_start(t["winfold"][:], dram["winfold"]).then_inc(s_fold_in, 16)
            act.dma_start(t["winspread"][:], dram["winspread"]).then_inc(s_spread_in, 16)
            act.preload_act_table_set("natural_log_exp_and_others")
            act.wait_ge(s_const, 16)

            def step(i, _):
                if live(i, 1, N):
                    g = i - 1
                    act.wait_ge(s_turned, g + 1)
                    wait(act, s_qkv, 3 * g)
                    act.activation(hT[:], ps_turn[:], ACT.Copy).then_inc(s_hT, 1)
                if live(i, 0, N):
                    norm_rstd(act, nm, eps, i)
                if live(i, 2, N):
                    g = i - 2
                    act.wait_ge(s_folded, g + 1)
                    wait(act, s_sc, g)
                    act.activation(scT[:], ps_turn[0:WIN * AH, :], ACT.Copy).then_inc(s_scT, 1)
                if live(i, 1, N):
                    g = i - 1
                    if first(i, 1):
                        act.wait_ge(s_small, 16)
                        act.wait_ge(s_pads, 4)
                    act.wait_ge(s_qkv, 3 * g + 1)
                    wait(act, s_prod_d, 3 * g)
                    wait(act, s_prod_p, 2 * g)
                    act.activation(q[:], ps_qkv[:, 0, :].rearrange("p (s t) -> p s t", t=SEQ), ACT.Identity,
                                   bias=t["abias"][:, 0:1]).then_inc(s_q, 1)
                if live(i, 3, N):
                    g = i - 3
                    act.wait_ge(s_pturned, g + 1)
                    wait(act, s_spread, WIN * g)
                    act.activation(p_hi[:], ps_pT, ACT.Copy).then_inc(s_phi, 1)
                if live(i, 1, N):
                    g = i - 1
                    act.wait_ge(s_qkv, 3 * g + 2)
                    act.activation(kpad[:, :, HALF:HALF + SEQ],
                                   ps_qkv[:, 1, :].rearrange("p (s t) -> p s t", t=SEQ), ACT.Identity,
                                   bias=t["abias"][:, 1:2]).then_inc(s_k, 1)
                if live(i, 0, N):
                    act.wait_ge(s_shift, i + 1)
                    wait(act, s_turned, i)
                    for j in range(GT):
                        act.activation(h[:, j, :], X[:, i * GT + j, :], ACT.Identity, bias=shift[:, j:j + 1],
                                       scale=nm.rstd[:, j:j + 1]).then_inc(s_h, 1)
                if live(i, 2, N):
                    g = i - 2
                    act.wait_ge(s_sub, g + 1)
                    wait(act, s_pn, g)
                    act.activation(prob[:], score[:], ACT.Exp, scale=float(AHD) ** -0.5).then_inc(s_exp, 1)
                if live(i, 1, N):
                    g = i - 1
                    act.wait_ge(s_qkv, 3 * g + 3)
                    act.activation(vpad[:, bass.ds(g * GS, GS), HALF:HALF + SEQ],
                                   ps_qkv[:, 2, :].rearrange("p (s t) -> p s t", t=SEQ), ACT.Identity,
                                   bias=t["abias"][:, 2:3]).then_inc(s_v, 1)
            sweep(act, N, LAG, 1, step)

        def window_product(eng, w, s):
            eng.tensor_tensor(prod[:, w, :].rearrange("p (s t) -> p s t", t=SEQ), q[:], kpad[:, :, w:w + SEQ],
                              ALU.mult).then_inc(s, 1)

        @block.vector
        def _(dve):
            def weighted(g, w):
                dve.wait_ge(s_spread, WIN * g + w + 1)
                dve.tensor_tensor(pv[:, w, :].rearrange("p (s t) -> p s t", t=SEQ),
                                  ps_spread[:, w % 2, :].rearrange("p (s t) -> p s t", t=SEQ),
                                  vpad[:, bass.ds(g * GS, GS), w:w + SEQ], ALU.mult).then_inc(s_pv, 1)

            def step(i, _):
                if live(i, 4, N):
                    weighted(i - 4, 3)
                if live(i, 4, N):
                    weighted(i - 4, 4)
                if live(i, 3, N):
                    g = i - 3
                    dve.wait_ge(s_exp, g + 1)
                    dve.tensor_reduce(ssum[:], prob[:].rearrange("p j w h -> p j h w"), X_AXIS,
                                      ALU.add).then_inc(s_sum, 1)
                if live(i, 3, N):
                    g = i - 3
                    dve.wait_ge(s_sum, g + 1)
                    dve.reciprocal(sinv[:], ssum[:]).then_inc(s_inv, 1)
                if live(i, 3, N):
                    g = i - 3
                    dve.wait_ge(s_inv, g + 1)
                    wait(dve, s_pturned, g)
                    dve.tensor_tensor(pnorm[:], prob[:], sinv[:].unsqueeze(2).broadcast_to([P, GT, WIN, AH]),
                                      ALU.mult).then_inc(s_pn, 1)
                if live(i, 0, N):
                    wait(dve, s_h, GT * i)
                    if isinstance(i, int):
                        for later in range(i, i + 1 if i < LAG else N):
                            dve.wait_ge(s_x[later], 16)
                    norm_stats(dve, nm, X, i)
                if live(i, 0, N):
                    dve.wait_ge(nm.s_rstd, i + 1)
                    dve.scalar_tensor_tensor(out=shift[:], in0=nm.meanvar[:, :, 0], scalar=-1.0, in1=nm.rstd[:],
                                             op0=ALU.mult, op1=ALU.mult).then_inc(s_shift, 1)
                if live(i, 4, N):
                    g = i - 4
                    dve.wait_ge(s_out, g + 1)
                    dve.wait_ge(s_bias, g + 1)
                    dve.tensor_tensor(group_rows(X, g), ps_out[:], group_rows(X, g), ALU.add).then_inc(s_res, 1)
                if live(i, 2, N):
                    g = i - 2
                    if first(i, 2):
                        dve.wait_ge(s_const, 16)
                    dve.wait_ge(s_sc, g + 1)
                    wait(dve, s_exp, g)
                    flat = score[:].rearrange("p j w h -> p j (w h)")
                    dve.tensor_tensor(flat, ps_score[:, 0:GT * WIN * AH].rearrange("p (j x) -> p j x", j=GT), maskb,
                                      ALU.add).then_inc(s_masked, 1)
                    dve.wait_ge(s_masked, g + 1)
                    dve.tensor_reduce(smax[:], score[:].rearrange("p j w h -> p j h w"), X_AXIS,
                                      ALU.max).then_inc(s_max, 1)
                    dve.wait_ge(s_max, g + 1)
                    dve.tensor_tensor(score[:], score[:], smax[:].unsqueeze(2).broadcast_to([P, GT, WIN, AH]),
                                      ALU.subtract).then_inc(s_sub, 1)
                if live(i, 3, N):
                    g = i - 3
                    dve.wait_ge(s_phi, g + 1)
                    dve.tensor_tensor(p_lo[:], ps_pT, p_hi[:].bitcast(F32), ALU.subtract).then_inc(s_plo, 1)
                if live(i, 1, N):
                    g = i - 1
                    dve.wait_ge(s_q, g + 1)
                    dve.wait_ge(s_k, g + 1)
                    wait(dve, s_folded, g)
                    window_product(dve, 0, s_prod_d)
                    window_product(dve, 1, s_prod_d)
                if live(i, 3, N):
                    wait(dve, s_acc, 4 * (i - 3))
                    weighted(i - 3, 0)
                if live(i, 1, N):
                    window_product(dve, 2, s_prod_d)
                if live(i, 3, N):
                    weighted(i - 3, 1)
                if live(i, 3, N):
                    weighted(i - 3, 2)
            sweep(dve, N, LAG, 1, step)

        @block.gpsimd
        def _(pool):
            for pads in (kpad, vpad):
                for at in (0, HALF + SEQ):
                    pool.memset(pads[:, :, at:at + HALF], 0.0).then_inc(s_pads, 1)
            pool.wait_ge(s_spread_in, 16)
            pool.tensor_copy(t["winspread_r"][:], t["winspread"][:]).then_inc(s_cast, 1)
            pool.memset(t["ctxpad"][:], 1.0).then_inc(s_made, 1)
            pool.memset(t["qdiag"][:], 0.0).then_inc(s_made, 1)

            def step(i, _):
                if live(i, 4, N):
                    g = i - 4
                    wait(pool, s_out, g)
                    sums = [acc[:, 0, :], acc[:, 1, :], acc[:, 2, :], attnT[:, :]]
                    for w in range(1, WIN):
                        pool.wait_ge(s_pv, WIN * g + w + 1)
                        if w > 1:
                            pool.wait_ge(s_acc, 4 * g + w - 1)
                        pool.tensor_tensor(sums[w - 1], pv[:, 0, :] if w == 1 else sums[w - 2], pv[:, w, :],
                                           ALU.add).then_inc(s_acc, 1)
                if live(i, 1, N):
                    g = i - 1
                    if first(i, 1):
                        pool.wait_ge(s_small, 16)
                    pool.wait_ge(s_h, GT * (g + 1))
                    pool.tensor_tensor(group_rows(X, g), group_rows(X, g),
                                       t["bo"].unsqueeze(1).broadcast_to([P, GT, D]), ALU.add).then_inc(s_bias, 1)
                    pool.wait_ge(s_q, g + 1)
                    pool.wait_ge(s_k, g + 1)
                    wait(pool, s_folded, g)
                    for w in range(3, WIN):
                        window_product(pool, w, s_prod_p)
            sweep(pool, N, LAG, 1, step)

            pool.wait_ge(s_consts, 16)
            pool.tensor_copy(t["sameseq_r"][:], c("sameseq")).then_inc(s_made, 1)
            pool.tensor_copy(t["ident16"][:], c("ident")).then_inc(s_made, 1)
            for out, name in ((t["causal16"], "causal"), (t["keyquery16"], "keyquery")):
                pool.tensor_copy(out[:], c(name).unsqueeze(1).broadcast_to([P, 8, SEQ])).then_inc(s_made, 1)
            pool.tensor_tensor(t["gate_kv"][:], t["gate_k"], t["gate_v"], ALU.add).then_inc(s_made, 1)
            pool.tensor_scalar(t["rms1"][:], t["rms"], 1.0, None, ALU.add).then_inc(s_made, 1)


def mlstm(nc, t, dram):
    with ExitStack() as ctx:
        def sb(name, shape, dt=F32):
            return ctx.enter_context(nc.sbuf_tensor(name, shape, dt))

        def ps(name, shape):
            return ctx.enter_context(nc.psum_tensor(name, shape, F32))

        sem = Semaphores(nc)
        ctx.callback(sem.clear)

        X, Y, c = t["X"], t["Y"], t["c"]
        ctxpad, qdiag = t["ctxpad"], t["qdiag"]
        GH = GT * MH
        nm, ny = Norm(sb, sem, "bn"), Norm(sb, sem, "yn")
        h = sb("b_h", [P, GT, D])
        ctx_in = sb("b_ctx", [P, 2, GT, D])
        qT = sb("b_qT", [P, GN])
        ctxT_in = sb("b_ctxT", [P, 2, GN])
        cT = sb("b_cT", [P, 2, GN])
        gate = sb("b_gate", [P, GT, 2 * MH])
        fabs, fexp, fln = sb("b_fabs", [P, GT, MH]), sb("b_fexp", [P, GT, MH]), sb("b_fln", [P, GT, MH])
        logf = sb("b_logf", [P, GH])
        csum = sb("b_csum", [P, GH])
        u = sb("b_u", [P, 2, GH])
        umaxT = sb("b_umaxT", [GH, P])
        umax, umax_r = sb("b_umax", [P, GH]), sb("b_umax_r", [P, GH], F32R)
        negm = sb("b_negm", [P, GH])
        floor = sb("b_floor", [P, 2, GH])
        umax_lo = sb("b_umax_lo", [P, GH])
        spread_hi, spread_lo = sb("b_spread_hi", [P, GH, SEQ], F32R), sb("b_spread_lo", [P, GH, SEQ], F32R)
        decay_log = sb("b_decay_log", [P, GH, SEQ])
        decay = sb("b_decay", [P, GH, SEQ])
        weight = sb("b_weight", [P, GH, SEQ])
        norm, norm_eps, inv = sb("b_norm", [P, GH]), sb("b_norm_eps", [P, GH]), sb("b_inv", [P, GH])
        ho = sb("b_ho", [P, 2, GH, MHD])
        hsq, hn, hr = (sb(f"b_{n}", [P, GH, MHD]) for n in ("hsq", "hn", "hr"))
        shift = sb("b_shift", [P, GT])
        ms, lms, rms = sb("b_ms", [P, GH]), sb("b_lms", [P, GH]), sb("b_rms", [P, GH])

        ps_turn = ps("b_ps_turn", [P, GN])
        ps_gate = ps("b_ps_gate", [P, GT, P])
        ps_small = ps("b_ps_small", [P, 512])
        ps_decay = ps("b_ps_decay", [P, 2, 512])
        ps_score = ps("b_ps_score", [P, 2, 512])
        C0, U0, M0 = 64, 128, 256

        s_ctx, s_pad = [sem("b_ctx_loaded0"), sem("b_ctx_loaded1")], sem("b_ctxpad_ready")
        s_ctxT, s_cT = [sem("b_ctxT_loaded0"), sem("b_ctxT_loaded1")], sem("b_cT_ready")
        s_h, s_turned, s_qT, s_qdiag = (sem(f"b_{n}") for n in ("h_ready", "turned", "qT_ready", "qdiag_ready"))
        s_gate, s_gsb, s_fabs, s_fexp, s_fln, s_logf = (sem(f"b_{n}") for n in
                                                        ("gates_done", "gates_ready", "fabs", "fexp", "fln", "logf"))
        s_cs, s_u, s_csum, s_uT, s_scan, s_mT, s_umax, s_negm, s_floor = (
            sem(f"b_{n}") for n in ("cs_done", "u_ready", "csum_ready", "uT_done", "scan_done", "umax_turned",
                                    "umax_ready", "negm_ready", "floor_ready"))
        s_spread, s_mbc, s_dlog, s_decay, s_st, s_weight, s_av = (
            sem(f"b_{n}") for n in ("spread_ready", "decay_log_done", "decay_log_ready", "decay_ready",
                                    "scores_done", "weights_ready", "output_done"))
        s_norm, s_neps, s_inv, s_ho, s_hsq, s_ms, s_lms, s_rms, s_hn, s_hr, s_x, s_y = (
            sem(f"b_{n}") for n in ("norm", "norm_eps", "inverse", "ho", "ho_squared", "meansquare", "log_ms",
                                    "rms", "hn_ready", "hr_ready", "x_updated", "y_ready"))
        s_mr, s_mlo, s_shift = sem("b_umax_rounded"), sem("b_umax_lo_ready"), sem("b_shift_ready")
        s_split = sem("b_weights_split")
        s_apart, s_apart_pool = sem("b_apart"), sem("b_apart_pool")
        N, LAG = GROUPS, 5
        block = ctx.enter_context(nc.Block())

        @block.sync
        def _(sp):
            def step(i, par):
                if live(i, 0, N):
                    wait(sp, s_cT, i - 1)
                    sp.dma_start(ctxT_in[:, par, :], dram["ctxT"][:, bass.ds(i * GN, GN)]).then_inc(s_ctxT[par], 16)
                    wait(sp, s_pad, i - 1)
                    sp.dma_start(ctx_in[:, par, :, :], dram["ctx"].rearrange("(t p) f -> p t f", p=P)[
                        :, bass.ds(i * GT, GT), :]).then_inc(s_ctx[par], 16)
            sweep(sp, N, LAG, 2, step)

        def ctx_count(g, par):
            return 16 * (g // 2 + 1) if isinstance(g, int) else (g - par + 2) * 8

        @block.tensor
        def _(pe):
            def output(tiles, par):
                for j in tiles:
                    for hd in range(MH):
                        for s in range(2):
                            at = (j % 2) * MH * (MHD + 1) + hd * (MHD + 1)
                            mm = pe.matmul(ps_score[s * SEQ:(s + 1) * SEQ, j // 2, at:at + MHD + 1],
                                           weight[s * SEQ:(s + 1) * SEQ, j * MH + hd, :],
                                           ctxpad[s * SEQ:(s + 1) * SEQ, par, j, hd, :], start=True, stop=True)
                mm.then_inc(s_av, 1)

            def step(i, par):
                if live(i, 2, N):
                    g = i - 2
                    pe.wait_ge(s_logf, g + 1)
                    wait(pe, s_negm, g)
                    wait(pe, s_mlo, g)
                    pe.matmul(ps_small[:, C0:C0 + GH], c("tri"), logf[:], start=True, stop=True).then_inc(s_cs, 1)
                if live(i, 1, N):
                    g = i - 1
                    pe.wait_ge(s_h, GT * (g + 1))
                    wait(pe, s_qdiag, 4 * g)
                    for j in range(GT):
                        mm = pe.transpose(ps_turn[:, j * P:(j + 1) * P], h[:, j, :], c("ident"))
                    mm.then_inc(s_turned, 1)
                if live(i, 2, N):
                    g = i - 2
                    pe.wait_ge(s_u, g + 1)
                    pe.wait_ge(s_csum, g + 1)
                    pe.transpose(ps_small[0:GH, U0:U0 + P], u[:, par, :], c("ident")).then_inc(s_uT, 1)
                if live(i, 2, N):
                    g = i - 2
                    pe.wait_ge(s_scan, g + 1)
                    apart(pe, s_apart)
                    pe.transpose(ps_small[:, M0:M0 + GH], umaxT[:], c("ident")[0:GH, 0:GH]).then_inc(s_mT, 1)
                if live(i, 1, N):
                    g = i - 1
                    pe.wait_ge(s_qT, g + 1)
                    pe.wait_ge(s_cT, g + 1)
                    wait(pe, s_gsb, g)
                    for j in range(GT):
                        pe.matmul(ps_gate[:, j, 0:2 * MH], qT[:, j * P:(j + 1) * P], t["gate_q"],
                                  start=True, stop=False)
                        mm = pe.matmul(ps_gate[:, j, 0:2 * MH], cT[:, 1 - par, j * P:(j + 1) * P],
                                       t["gate_kv"][:], start=False, stop=True)
                    mm.then_inc(s_gate, 1)
                if live(i, 3, N):
                    g = i - 3
                    pe.wait_ge(s_weight, 2 * (g + 1))
                    pe.wait_ge(s_pad, g + 1)
                    apart(pe, s_apart)
                    output((0, 1), 1 - par)
                    output((2, 3), 1 - par)
                if live(i, 2, N):
                    g = i - 2
                    pe.wait_ge(s_spread, 2 * (g + 1))
                    wait(pe, s_dlog, 2 * g)
                    for b in range(2):
                        pe.matmul(ps_decay[:, b, :], t["sameseq_r"][:], spread_hi[:, b * 8:(b + 1) * 8, :],
                                  start=True, stop=False)
                        pe.matmul(ps_decay[:, b, :], t["sameseq_r"][:], spread_lo[:, b * 8:(b + 1) * 8, :],
                                  start=False, stop=False)
                        pe.matmul(ps_decay[:, b, :], t["ident16"][:], t["keyquery16"][:],
                                  start=False, stop=True).then_inc(s_mbc, 1)
                if live(i, 2, N):
                    g = i - 2
                    wait(pe, s_ho, g)
                    for j in range(GT):
                        for s in range(2):
                            mm = pe.matmul(ps_score[s * SEQ:(s + 1) * SEQ, j // 2, (j % 2) * 256:(j % 2) * 256 + 256],
                                           cT[:, par, j * P + s * SEQ:j * P + (s + 1) * SEQ],
                                           qdiag[:, par, 2 * j + s, :, :], start=True, stop=True)
                        if j % 2:
                            mm.then_inc(s_st, 1)
            sweep(pe, N, LAG, 2, step)

        @block.scalar
        def _(act):
            act.preload_act_table_set("natural_log_exp_and_others")
            eps, one = c("eps")[:, 0:1], c("eps")[:, 2:3]
            small_eps = c("eps")[:, 1:2]

            def step(i, par):
                if live(i, 4, N):
                    g = i - 4
                    act.wait_ge(s_ms, g + 1)
                    act.activation(lms[:], ms[:], ACT.Ln, bias=small_eps, scale=1.0 / MHD).then_inc(s_lms, 1)
                    act.wait_ge(s_lms, g + 1)
                    wait(act, s_hn, g)
                    act.activation(rms[:], lms[:], ACT.Exp, scale=-0.5).then_inc(s_rms, 1)
                if live(i, 1, N):
                    g = i - 1
                    act.wait_ge(s_ctxT[1 - par], ctx_count(g, 1 - par))
                    wait(act, s_st, 2 * (g - 1))
                    act.activation(cT[:, 1 - par, :], ctxT_in[:, 1 - par, :], ACT.Copy).then_inc(s_cT, 1)
                    act.wait_ge(s_turned, g + 1)
                    wait(act, s_gate, g)
                    act.activation(qT[:], ps_turn[:], ACT.Copy).then_inc(s_qT, 1)
                if live(i, 3, N):
                    g = i - 3
                    wait(act, s_weight, 2 * g)
                    for b in range(2):
                        act.wait_ge(s_dlog, 2 * g + b + 1)
                        act.activation(decay[:, b * 8:(b + 1) * 8, :], decay_log[:, b * 8:(b + 1) * 8, :],
                                       ACT.Exp).then_inc(s_decay, 1)
                if live(i, 2, N):
                    g = i - 2
                    act.wait_ge(s_negm, g + 1)
                    wait(act, s_norm, g - 1)
                    act.activation(floor[:, par, :], negm[:], ACT.Exp).then_inc(s_floor, 1)
                if live(i, 1, N):
                    g = i - 1
                    wait(act, s_st, 2 * (g - 1))
                    for hd in range(MH):
                        rows = slice(hd * MHD, (hd + 1) * MHD)
                        act.activation(qdiag[rows, 1 - par, :, hd, :],
                                       ps_turn[rows, :].rearrange("p (s t) -> p s t", t=SEQ),
                                       ACT.Copy).then_inc(s_qdiag, 1)
                if live(i, 0, N):
                    norm_rstd(act, nm, eps, i)
                if live(i, 3, N):
                    g = i - 3
                    act.wait_ge(s_ho, g + 1)
                    wait(act, s_ms, g)
                    act.activation(hsq[:], ho[:, 1 - par], ACT.Square).then_inc(s_hsq, 1)
                if live(i, 1, N):
                    g = i - 1
                    act.wait_ge(s_gsb, g + 1)
                    wait(act, s_logf, g)
                    act.activation(fabs[:], gate[:, :, MH:2 * MH], ACT.Abs).then_inc(s_fabs, 1)
                    act.wait_ge(s_fabs, g + 1)
                    act.activation(fexp[:], fabs[:], ACT.Exp, scale=-1.0).then_inc(s_fexp, 1)
                    act.wait_ge(s_fexp, g + 1)
                    act.activation(fln[:], fexp[:], ACT.Ln, bias=one).then_inc(s_fln, 1)
                if live(i, 5, N):
                    norm_rstd(act, ny, eps, i - 5)
                if live(i, 5, N):
                    g = i - 5
                    act.wait_ge(s_shift, g + 1)
                    for j in range(GT):
                        act.activation(Y[:, g * GT + j, :], X[:, g * GT + j, :], ACT.Identity,
                                       bias=shift[:, j:j + 1], scale=ny.rstd[:, j:j + 1]).then_inc(s_y, 1)
            sweep(act, N, LAG, 2, step)

        @block.vector
        def _(dve):
            def step(i, par):
                if live(i, 4, N):
                    g = i - 4
                    dve.wait_ge(s_hsq, g + 1)
                    wait(dve, s_lms, g)
                    dve.tensor_reduce(ms[:], hsq[:], X_AXIS, ALU.add).then_inc(s_ms, 1)
                if live(i, 3, N):
                    g = i - 3
                    wait(dve, s_decay, 2 * g)
                    for b in range(2):
                        dve.wait_ge(s_mbc, 2 * g + b + 1)
                        dve.tensor_tensor(decay_log[:, b * 8:(b + 1) * 8, :],
                                          ps_decay[:, b, :].rearrange("p (x t) -> p x t", t=SEQ),
                                          u[:, 1 - par, b * 8:(b + 1) * 8].unsqueeze(2).broadcast_to([P, 8, SEQ]),
                                          ALU.add).then_inc(s_dlog, 1)
                if live(i, 2, N):
                    g = i - 2
                    dve.wait_ge(s_cs, g + 1)
                    dve.tensor_tensor(u[:, par, :].rearrange("p (j x) -> p j x", j=GT), gate[:, :, 0:MH],
                                      ps_small[:, C0:C0 + GH].rearrange("p (j x) -> p j x", j=GT),
                                      ALU.subtract).then_inc(s_u, 1)
                    dve.tensor_copy(csum[:], ps_small[:, C0:C0 + GH]).then_inc(s_csum, 1)
                if live(i, 4, N):
                    g = i - 4
                    dve.wait_ge(s_rms, g + 1)
                    wait(dve, s_hr, g)
                    dve.tensor_tensor(hn[:], ho[:, par], rms[:].unsqueeze(2).broadcast_to([P, GH, MHD]),
                                      ALU.mult).then_inc(s_hn, 1)
                if live(i, 2, N):
                    g = i - 2
                    dve.wait_ge(s_uT, g + 1)
                    dve.tensor_tensor_scan(umaxT[:], c("seqstart")[0:GH, :], ps_small[0:GH, U0:U0 + P], 0.0,
                                           ALU.add, ALU.max).then_inc(s_scan, 1)
                if live(i, 3, N):
                    g = i - 3
                    wait(dve, s_av, 2 * g)
                    for b in range(2):
                        dve.wait_ge(s_decay, 2 * g + b + 1)
                        dve.wait_ge(s_st, 2 * g + b + 1)
                        dve.scalar_tensor_tensor(out=weight[:, b * 8:(b + 1) * 8, :].rearrange("p x t -> p (x t)"),
                                                 in0=ps_score[:, b, :], scalar=float(MHD) ** -0.5,
                                                 in1=decay[:, b * 8:(b + 1) * 8, :].rearrange("p x t -> p (x t)"),
                                                 op0=ALU.mult, op1=ALU.mult).then_inc(s_weight, 1)
                if live(i, 2, N):
                    g = i - 2
                    dve.wait_ge(s_mT, g + 1)
                    wait(dve, s_mlo, g)
                    dve.tensor_copy(umax[:], ps_small[:, M0:M0 + GH]).then_inc(s_umax, 1)
                    wait(dve, s_floor, g)
                    dve.wait_ge(s_csum, g + 1)
                    dve.scalar_tensor_tensor(out=negm[:], in0=csum[:], scalar=-1.0, in1=ps_small[:, M0:M0 + GH],
                                             op0=ALU.mult, op1=ALU.subtract).then_inc(s_negm, 1)
                    wait(dve, s_spread, 2 * g)
                    dve.wait_ge(s_umax, g + 1)
                    dve.tensor_copy(umax_r[:], umax[:]).then_inc(s_mr, 1)
                    dve.wait_ge(s_mr, g + 1)
                    dve.tensor_tensor(umax_lo[:], umax[:], umax_r[:].bitcast(F32), ALU.subtract).then_inc(s_mlo, 1)
                if live(i, 0, N):
                    wait(dve, s_h, GT * i)
                    norm_stats(dve, nm, X, i)
                if live(i, 1, N):
                    g = i - 1
                    dve.wait_ge(s_gate, g + 1)
                    wait(dve, s_u, g)
                    dve.tensor_tensor(gate[:], ps_gate[:, :, 0:2 * MH],
                                      t["gate_bias"].unsqueeze(1).broadcast_to([P, GT, 2 * MH]),
                                      ALU.add).then_inc(s_gsb, 1)
                if live(i, 3, N):
                    g = i - 3
                    dve.wait_ge(s_av, 2 * (g + 1))
                    dve.wait_ge(s_floor, g + 1)
                    out = ps_score[:, :, 0:2 * MH * (MHD + 1)].rearrange("p b (x d) -> p b x d", d=MHD + 1)
                    dve.tensor_tensor(norm[:].rearrange("p (b x) -> p b x", b=2), out[:, :, :, MHD],
                                      floor[:, 1 - par, :].rearrange("p (b x) -> p b x", b=2),
                                      ALU.max).then_inc(s_norm, 1)
                    dve.wait_ge(s_norm, g + 1)
                    dve.tensor_scalar(norm_eps[:], norm[:], 1e-6, None, ALU.add).then_inc(s_neps, 1)
                    dve.wait_ge(s_neps, g + 1)
                    dve.reciprocal(inv[:], norm_eps[:]).then_inc(s_inv, 1)
                    dve.wait_ge(s_inv, g + 1)
                    wait(dve, s_hn, g - 1)
                    dve.tensor_tensor(ho[:, 1 - par].rearrange("p (b x) d -> p b x d", b=2), out[:, :, :, 0:MHD],
                                      inv[:].rearrange("p (b x) -> p b x", b=2).unsqueeze(3).broadcast_to(
                                          [P, 2, 8, MHD]), ALU.mult).then_inc(s_ho, 1)
                if live(i, 5, N):
                    g = i - 5
                    dve.wait_ge(s_x, g + 1)
                    wait(dve, s_y, GT * g)
                    norm_stats(dve, ny, X, g)
                if live(i, 1, N):
                    g = i - 1
                    dve.wait_ge(s_fln, g + 1)
                    dve.wait_ge(s_gsb, g + 1)
                    wait(dve, s_cs, g)
                    dve.scalar_tensor_tensor(out=logf[:].rearrange("p (j x) -> p j x", j=GT),
                                             in0=gate[:, :, MH:2 * MH], scalar=0.0, in1=fln[:],
                                             op0=ALU.min, op1=ALU.subtract).then_inc(s_logf, 1)
                if live(i, 0, N):
                    wait(dve, s_turned, i)
                    norm_apply(dve, nm, lambda j: h[:, j, :], X, i, s_h)
                if live(i, 5, N):
                    g = i - 5
                    dve.wait_ge(ny.s_rstd, g + 1)
                    dve.scalar_tensor_tensor(out=shift[:], in0=ny.meanvar[:, :, 0], scalar=-1.0, in1=ny.rstd[:],
                                             op0=ALU.mult, op1=ALU.mult).then_inc(s_shift, 1)
            sweep(dve, N, LAG, 2, step)

        @block.gpsimd
        def _(pool):
            pool.wait_ge(t["s_layers"], t["layers_loaded"])
            split_weights(pool, t["wqkv"][0], t["wqkv_hi"], t["wqkv_lo"], s_split)

            def step(i, par):
                if live(i, 4, N):
                    g = i - 4
                    pool.wait_ge(s_hn, g + 1)
                    wait(pool, s_x, g)
                    pool.tensor_tensor(hr[:], hn[:], t["rms1"][:].unsqueeze(1).broadcast_to([P, GH, MHD]),
                                       ALU.mult).then_inc(s_hr, 1)
                if live(i, 2, N):
                    g = i - 2
                    wait(pool, s_mbc, 2 * g)
                    pool.wait_ge(s_mlo, g + 1)
                    for part, out in ((umax_r[:].bitcast(F32), spread_hi), (umax_lo[:], spread_lo)):
                        pool.tensor_tensor(out[:], c("negfold").unsqueeze(1).broadcast_to([P, GH, SEQ]),
                                           part.unsqueeze(2).broadcast_to([P, GH, SEQ]), ALU.mult).then_inc(s_spread, 1)
                if live(i, 4, N):
                    g = i - 4
                    pool.wait_ge(s_hr, g + 1)
                    pool.tensor_tensor(group_rows(X, g), group_rows(X, g),
                                       hr[:].rearrange("p (j h) d -> p j (h d)", j=GT), ALU.add).then_inc(s_x, 1)
                if live(i, 2, N):
                    g = i - 2
                    pool.wait_ge(s_ctx[par], ctx_count(g, par))
                    wait(pool, s_av, 2 * (g - 1))
                    apart(pool, s_apart_pool)
                    pool.tensor_scalar(ctxpad[:, par, :, :, 0:MHD],
                                       ctx_in[:, par, :, :].rearrange("p j (h d) -> p j h d", d=MHD),
                                       1.0, None, ALU.mult).then_inc(s_pad, 1)
            sweep(pool, N, LAG, 2, step)


def causal_attention(nc, t, layer):
    with ExitStack() as ctx:
        def sb(name, shape, dt=F32):
            return ctx.enter_context(nc.sbuf_tensor(f"c{layer}_{name}", shape, dt))

        def ps(name, shape):
            return ctx.enter_context(nc.psum_tensor(f"c{layer}_{name}", shape, F32))

        phase_sems = Semaphores(nc)
        ctx.callback(phase_sems.clear)

        def sem(name):
            return phase_sems(f"c{layer}_{name}")

        Y, c = t["Y"], t["c"]
        wo, qks = t["lwo"][layer], t["qks"][layer]
        HT = LHD // 2
        w_hi, w_lo = t["wqkv_hi"], t["wqkv_lo"]
        costab, sintab = sb("costab", [P, 2, LHD]), sb("sintab", [P, 2, LHD])
        xin = sb("xin", [P, D])
        xT = sb("xT", [P, P])
        x_hi, x_lo = sb("x_hi", [P, P], F32R), sb("x_lo", [P, P], F32R)
        qk = sb("qk", [P, 2 * LH, LHD])
        sq = sb("sq", [P, 2 * LH, LHD])
        rcos, rsin = sb("rcos", [P, 2 * LH, LHD]), sb("rsin", [P, 2 * LH, LHD])
        rsum, rot = sb("rsum", [P, 2 * LH, LHD]), sb("rot", [P, 2 * LH, LHD])
        ss, ssc, lss, inv = (sb(n, [P, 2 * LH]) for n in ("ss", "ssc", "lss", "inv"))
        v = sb("v", [P, 4, INNER])
        qkT = sb("qkT", [P, 2 * LH // 2, P])
        smax, ssum, sinv = (sb(n, [P, LH]) for n in ("smax", "ssum", "sinv"))
        score, prob, pnorm = (sb(n, [P, LH, SEQ]) for n in ("score", "prob", "pnorm"))
        pT = sb("pT", [P, INNER])
        oT = sb("oT", [P, LH // 2, P])

        ps_qkv = ps("ps_qkv", [P, 3, INNER])
        ps_qkT = ps("ps_qkT", [P, 2, 512])
        ps_score = ps("ps_score", [P, 512])
        ps_o0 = ps("ps_o0", [P, 512])
        ps_o1 = ps("ps_o1", [P, 512])
        ps_y, ps_xT = ps_qkv[:, 2, 0:D], ps_o1[:, 384:512]

        s_tab, s_split, s_zero = sem("tables_ready"), sem("weights_split"), sem("xT_zeroed")
        s_xin, s_xturned, s_xT, s_xhi, s_xlo = (sem(n) for n in ("xin_ready", "x_turned", "xT_ready", "x_hi_ready",
                                                                 "x_lo_ready"))
        s_qkv, s_qk, s_v, s_sq, s_rcos, s_rsin = (sem(n) for n in ("qkv_done", "qk_ready", "v_ready", "sq_ready",
                                                                   "rcos_ready", "rsin_ready"))
        s_ss, s_ssc, s_lss, s_inv, s_rsum, s_rot = (sem(n) for n in ("ss_ready", "ss_clipped", "log_ss", "inv_ready",
                                                                     "rsum_ready", "rot_ready"))
        s_rturned, s_qkT, s_sc, s_max, s_sub, s_exp = (sem(n) for n in ("rot_turned", "qkT_ready", "scores_done",
                                                                        "max_ready", "shifted", "exp_ready"))
        s_sum, s_sinv, s_pn, s_pturned, s_pT, s_av, s_oT, s_y, s_res = (
            sem(n) for n in ("sum_ready", "sum_inverse", "probs_ready", "probs_turned", "pT_ready", "output_done",
                             "oT_ready", "y_done", "residual_done"))
        s_apart = sem("apart")
        N, LAG = TILES, 5
        block = ctx.enter_context(nc.Block())

        @block.tensor
        def _(pe):
            def step(i, par):
                if live(i, 1, N):
                    g = i - 1
                    pe.wait_ge(s_xlo, g + 1)
                    for n in range(3):
                        if n < 2:
                            wait(pe, s_qk, 2 * (g - 1) + n + 1)
                        else:
                            wait(pe, s_v, g)
                            wait(pe, s_pT, g - 3)
                            wait(pe, s_res, g - 4)
                        cols = slice(n * INNER, (n + 1) * INNER)
                        pe.matmul(ps_qkv[:, n, :], x_hi[:], w_hi[:, cols], start=True, stop=False)
                        pe.matmul(ps_qkv[:, n, :], x_hi[:], w_lo[:, cols], start=False, stop=False)
                        pe.matmul(ps_qkv[:, n, :], x_lo[:], w_hi[:, cols], start=False,
                                  stop=True).then_inc(s_qkv, 1)
                if live(i, 0, N):
                    pe.wait_ge(s_xin, i + 1)
                    wait(pe, s_oT, 2 * (i - 4))
                    pe.transpose(ps_xT, xin[:], c("ident")).then_inc(s_xturned, 1)
                if live(i, 3, N):
                    g = i - 3
                    wait(pe, s_sub, g)
                    pe.wait_ge(s_qkT, 2 * (g + 1))
                    pe.matmul(ps_score[:], t["ident16"][:], t["causal16"][:], start=True, stop=False,
                              skip_group_check=True)
                    for x in range(LH // 2):
                        for s in range(2):
                            for e in range(2):
                                mm = pe.matmul(ps_score[e * SEQ:(e + 1) * SEQ, x * P + s * SEQ:x * P + (s + 1) * SEQ],
                                               qkT[e * LHD:(e + 1) * LHD, x, s * SEQ:(s + 1) * SEQ],
                                               qkT[e * LHD:(e + 1) * LHD, LH // 2 + x, s * SEQ:(s + 1) * SEQ],
                                               start=False, stop=True, skip_group_check=True)
                    mm.then_inc(s_sc, 1)
                if live(i, 4, N):
                    g = i - 4
                    pe.wait_ge(s_pn, g + 1)
                    pe.wait_ge(s_v, g + 4 if live(i, 1, N) else N)
                    wait(pe, s_res, g - 1)
                    for x in range(LH // 2):
                        mm = pe.transpose(ps_qkv[:, 2, x * P:(x + 1) * P],
                                          pnorm[:, 2 * x:2 * x + 2, :].rearrange("p s k -> p (s k)"), c("ident"))
                    mm.then_inc(s_pturned, 1)
                if live(i, 2, N):
                    g = i - 2
                    pe.wait_ge(s_rot, g + 1)
                    wait(pe, s_qkT, 2 * g)
                    for x in range(LH):
                        mm = pe.transpose(ps_qkT[:, x // 4, (x % 4) * P:(x % 4 + 1) * P],
                                          rot[:, 2 * x:2 * x + 2, :].rearrange("p s k -> p (s k)"), c("ident"))
                        if x % 4 == 3:
                            mm.then_inc(s_rturned, 1)
                if live(i, 5, N):
                    g = i - 5
                    pe.wait_ge(s_oT, 2 * (g + 1))
                    pe.wait_ge(s_pT, g + 2 if live(i, 4, N) else N)
                    wait(pe, s_res, g)
                    for x in range(LH // 2):
                        mm = pe.matmul(ps_y, oT[:, x, :], wo[:, x, :], start=(x == 0), stop=(x == LH // 2 - 1))
                    mm.then_inc(s_y, 1)
                if live(i, 4, N):
                    g = i - 4
                    pe.wait_ge(s_pT, g + 1)
                    if live(i, 0, N):
                        pe.wait_ge(s_xT, 2 * (i + 1))
                    apart(pe, s_apart)
                    for x in range(LH // 2):
                        for s, bank in ((0, ps_o0), (1, ps_o1)):
                            for e in range(2):
                                mm = pe.matmul(bank[e * LHD:(e + 1) * LHD, x * SEQ:(x + 1) * SEQ],
                                               v[s * SEQ:(s + 1) * SEQ, (par - 4) % 4,
                                                 (2 * x + e) * LHD:(2 * x + e + 1) * LHD],
                                               pT[s * SEQ:(s + 1) * SEQ, x * P + e * SEQ:x * P + (e + 1) * SEQ],
                                               start=True, stop=True)
                    mm.then_inc(s_av, 1)
            sweep(pe, N, LAG, 4, step)

        @block.scalar
        def _(act):
            act.preload_act_table_set("natural_log_exp_and_others")
            act.wait_ge(s_zero, 1)

            def step(i, par):
                if live(i, 1, N):
                    g = i - 1
                    wait(act, s_rcos, g)
                    wait(act, s_rsin, 2 * g)
                    act.wait_ge(s_qkv, 3 * g + 1)
                    act.activation(qk[:, 0:LH, :].rearrange("p h d -> p (h d)"), ps_qkv[:, 0, :],
                                   ACT.Copy).then_inc(s_qk, 1)
                if live(i, 1, N):
                    g = i - 1
                    act.wait_ge(s_qkv, 3 * g + 2)
                    act.activation(qk[:, LH:2 * LH, :].rearrange("p h d -> p (h d)"), ps_qkv[:, 1, :],
                                   ACT.Copy).then_inc(s_qk, 1)
                if live(i, 1, N):
                    g = i - 1
                    act.wait_ge(s_qkv, 3 * (g + 1))
                    wait(act, s_av, g - 3)
                    act.activation(v[:, (par - 1) % 4, :], ps_qkv[:, 2, :], ACT.Copy).then_inc(s_v, 1)
                if live(i, 0, N):
                    act.wait_ge(s_xturned, i + 1)
                    wait(act, s_xlo, i)
                    act.activation(xT[0:D // 2, :], ps_xT[0:D // 2, :], ACT.Copy).then_inc(s_xT, 1)
                    act.activation(xT[D // 2:D, :].rearrange("p (s t) -> p s t", t=SEQ)[:, :, 1:SEQ],
                                   ps_xT[D // 2:D, :].rearrange("p (s t) -> p s t", t=SEQ)[:, :, 0:SEQ - 1],
                                   ACT.Copy).then_inc(s_xT, 1)
                if live(i, 1, N):
                    g = i - 1
                    act.wait_ge(s_qk, 2 * (g + 1))
                    wait(act, s_ss, g)
                    act.activation(sq[:], qk[:], ACT.Square).then_inc(s_sq, 1)
                if live(i, 4, N):
                    g = i - 4
                    act.wait_ge(s_pturned, g + 1)
                    wait(act, s_av, g)
                    act.activation(pT[:], ps_qkv[:, 2, :], ACT.Copy).then_inc(s_pT, 1)
                if live(i, 0, N):
                    act.wait_ge(s_xT, 2 * (i + 1))
                    wait(act, s_qkv, 3 * i)
                    act.activation(x_hi[:], xT[:], ACT.Copy).then_inc(s_xhi, 1)
                if live(i, 2, N):
                    g = i - 2
                    wait(act, s_sc, g)
                    for n in range(2):
                        act.wait_ge(s_rturned, 2 * g + n + 1)
                        act.activation(qkT[:, 4 * n:4 * n + 4, :].rearrange("p x t -> p (x t)"), ps_qkT[:, n, :],
                                       ACT.Copy).then_inc(s_qkT, 1)
                if live(i, 3, N):
                    g = i - 3
                    act.wait_ge(s_sub, g + 1)
                    wait(act, s_pn, g)
                    act.activation(prob[:], score[:], ACT.Exp, scale=8.0).then_inc(s_exp, 1)
                if live(i, 1, N):
                    g = i - 1
                    act.wait_ge(s_ssc, g + 1)
                    act.activation(lss[:], ssc[:], ACT.Ln).then_inc(s_lss, 1)
                    act.wait_ge(s_lss, g + 1)
                    wait(act, s_rot, g)
                    act.activation(inv[:], lss[:], ACT.Exp, scale=-0.5).then_inc(s_inv, 1)
                if live(i, 4, N):
                    g = i - 4
                    act.wait_ge(s_av, g + 1)
                    wait(act, s_y, g)
                    for s, bank in ((0, ps_o0), (1, ps_o1)):
                        act.activation(oT[:, :, s * SEQ:(s + 1) * SEQ],
                                       bank[:, 0:LH // 2 * SEQ].rearrange("p (x t) -> p x t", t=SEQ),
                                       ACT.Copy).then_inc(s_oT, 1)
            sweep(act, N, LAG, 4, step)

        @block.vector
        def _(dve):
            cos, sin = c("rot")[:, 0:2 * LHD], c("rot")[:, 2 * LHD:4 * LHD]
            two = lambda a: a.rearrange("p (n d) -> p n d", d=LHD)
            heads = lambda a: a.rearrange("p (n h) d -> p n h d", n=2)
            tab = lambda a: a.unsqueeze(2).broadcast_to([P, 2, LH, a.shape[-1]])
            flat = ps_score[:].rearrange("p (h k) -> p h k", k=SEQ)
            dve.tensor_tensor(costab[:], two(cos), qks[:], ALU.mult).then_inc(s_tab, 1)
            dve.tensor_tensor(sintab[:, :, 0:HT], two(sin)[:, :, 0:HT], qks[:, :, HT:LHD], ALU.mult).then_inc(s_tab, 1)
            dve.tensor_tensor(sintab[:, :, HT:LHD], two(sin)[:, :, HT:LHD], qks[:, :, 0:HT],
                              ALU.mult).then_inc(s_tab, 1)
            dve.memset(xT[:], 0.0).then_inc(s_zero, 1)
            dve.wait_ge(s_tab, 3)

            def step(i, par):
                if live(i, 0, N):
                    wait(dve, s_xturned, i)
                    dve.tensor_copy(xin[:], Y[:, i, :]).then_inc(s_xin, 1)
                if live(i, 1, N):
                    g = i - 1
                    dve.wait_ge(s_qk, 2 * (g + 1))
                    wait(dve, s_rsum, g)
                    dve.tensor_tensor(heads(rcos[:]), heads(qk[:]), tab(costab[:]), ALU.mult).then_inc(s_rcos, 1)
                if live(i, 1, N):
                    for lo, hi in ((0, HT), (HT, 0)):
                        dve.tensor_tensor(heads(rsin[:])[:, :, :, lo:lo + HT], heads(qk[:])[:, :, :, hi:hi + HT],
                                          tab(sintab[:, :, lo:lo + HT]), ALU.mult).then_inc(s_rsin, 1)
                if live(i, 3, N):
                    g = i - 3
                    dve.wait_ge(s_sc, g + 1)
                    dve.tensor_reduce(smax[:], flat, X_AXIS, ALU.max).then_inc(s_max, 1)
                if live(i, 0, N):
                    dve.wait_ge(s_xhi, i + 1)
                    dve.tensor_tensor(x_lo[:], xT[:], x_hi[:].bitcast(F32), ALU.subtract).then_inc(s_xlo, 1)
                if live(i, 3, N):
                    g = i - 3
                    dve.wait_ge(s_max, g + 1)
                    wait(dve, s_exp, g)
                    dve.tensor_tensor(score[:], flat, smax[:].unsqueeze(2).broadcast_to([P, LH, SEQ]),
                                      ALU.subtract).then_inc(s_sub, 1)
                if live(i, 1, N):
                    g = i - 1
                    dve.wait_ge(s_sq, g + 1)
                    dve.tensor_reduce(ss[:], sq[:], X_AXIS, ALU.add).then_inc(s_ss, 1)
                if live(i, 1, N):
                    g = i - 1
                    dve.wait_ge(s_ss, g + 1)
                    wait(dve, s_lss, g)
                    dve.tensor_scalar(ssc[:], ss[:], 1e-24, None, ALU.max).then_inc(s_ssc, 1)
                if live(i, 3, N):
                    g = i - 3
                    dve.wait_ge(s_exp, g + 1)
                    dve.tensor_reduce(ssum[:], prob[:], X_AXIS, ALU.add).then_inc(s_sum, 1)
                if live(i, 5, N):
                    g = i - 5
                    dve.wait_ge(s_y, g + 1)
                    dve.tensor_tensor(Y[:, g, :], ps_y, Y[:, g, :], ALU.add).then_inc(s_res, 1)
                if live(i, 3, N):
                    g = i - 3
                    dve.wait_ge(s_sum, g + 1)
                    wait(dve, s_pn, g)
                    dve.reciprocal(sinv[:], ssum[:]).then_inc(s_sinv, 1)
            sweep(dve, N, LAG, 4, step)

        @block.gpsimd
        def _(pool):
            def step(i, par):
                if live(i, 1, N):
                    g = i - 1
                    pool.wait_ge(s_rcos, g + 1)
                    pool.wait_ge(s_rsin, 2 * (g + 1))
                    wait(pool, s_rot, g)
                    pool.tensor_tensor(rsum[:], rcos[:], rsin[:], ALU.add).then_inc(s_rsum, 1)
                    pool.wait_ge(s_rsum, g + 1)
                    pool.wait_ge(s_inv, g + 1)
                    wait(pool, s_rturned, 2 * g)
                    pool.tensor_tensor(rot[:], rsum[:], inv[:].unsqueeze(2).broadcast_to([P, 2 * LH, LHD]),
                                       ALU.mult).then_inc(s_rot, 1)
                if live(i, 3, N):
                    g = i - 3
                    pool.wait_ge(s_sinv, g + 1)
                    wait(pool, s_pturned, g)
                    pool.tensor_tensor(pnorm[:], prob[:], sinv[:].unsqueeze(2).broadcast_to([P, LH, SEQ]),
                                       ALU.mult).then_inc(s_pn, 1)
            sweep(pool, N, LAG, 4, step)
            split_weights(pool, t["w1"][layer], t["w1_hi"], t["w1_lo"], s_split)


def gated_ffn(nc, t, dram, layer):
    last = layer == DEPTH - 1
    with ExitStack() as ctx:
        def sb(name, shape, dt=F32):
            return ctx.enter_context(nc.sbuf_tensor(f"f{layer}_{name}", shape, dt))

        def ps(name, shape):
            return ctx.enter_context(nc.psum_tensor(f"f{layer}_{name}", shape, F32))

        phase_sems = Semaphores(nc)
        ctx.callback(phase_sems.clear)

        def sem(name):
            return phase_sems(f"f{layer}_{name}")

        X, Y, c = t["X"], t["Y"], t["c"]
        w2, cols, b2 = t["w2"][layer], t["ffncols"][layer], t["b2"][layer]
        H2 = D // 2
        NCH = len(HCH)
        w_hi, w_lo = t["w1_hi"], t["w1_lo"]
        x_in = sb("x_in", [P, 2, GT, D])
        stats, meanvar = sb("stats", [P, GT, 6]), sb("meanvar", [P, 2, GT, 2])
        vareps, rstd = sb("vareps", [P, GT]), sb("rstd", [P, GT])
        h = sb("h", [P, GT, D])
        hT = sb("hT", [P, GN])
        h_hi, h_lo = sb("h_hi", [P, 2, GN], F32R), sb("h_lo", [P, 2, GN], F32R)
        gelu = sb("gelu", [P, 2, GN])
        gated = sb("gated", [P, 2, NCH, GN])

        ps_shift = ps("ps_shift", [P, GT, P])
        ps_turn = ps("ps_turn", [P, GN])
        ps_a = ps("ps_a", [P, 2, GN])
        ps_g = ps("ps_g", [P, 2, GN])
        ps_out = ps("ps_out", [P, GT, D])

        s_split = sem("weights_split")
        s_shift, s_in, s_stats, s_meanvar, s_rstd = (sem(n) for n in ("shifted", "x_in_ready", "stats_done",
                                                                      "meanvar_done", "rstd_ready"))
        s_h, s_turned, s_hT, s_hhi, s_hlo = (sem(n) for n in ("h_ready", "h_turned", "hT_ready", "h_hi_ready",
                                                              "h_lo_ready"))
        s_a, s_g, s_gelu, s_gated, s_out, s_bias, s_bias2, s_res = (
            sem(n) for n in ("a_done", "g_done", "gelu_ready", "gated_ready", "out_done", "bias_added", "x_added",
                             "residual_done"))
        s_store, s_apart, s_vareps = sem("stored"), sem("apart"), sem("variance_ready")
        N, LAG = GROUPS, 3
        block = ctx.enter_context(nc.Block())

        if last:
            @block.sync
            def _(sp):
                def step(i, par):
                    if live(i, 3, N):
                        g = i - 3
                        sp.wait_ge(s_res, g + 1)
                        dst = dram["out"].rearrange("(t p) f -> p t f", p=P)
                        sp.dma_start(dst[:, bass.ds(g * GT, GT), :], group_rows(Y, g)).then_inc(s_store, 16)
                sweep(sp, N, LAG, 2, step)
                sp.wait_ge(s_store, 16 * N)

        @block.tensor
        def _(pe):
            def hidden(g, par, chunks):
                for n in chunks:
                    m, b = HCH[n], (NCH * par + n) % 2
                    for bank, at, done, used in ((ps_g, HID, s_g, s_gelu), (ps_a, 0, s_a, s_gated)):
                        wait(pe, used, NCH * g + n - 1)
                        part = slice(at + n * P, at + n * P + m)
                        out = bank[0:m, b, :]
                        pe.matmul(out, w_hi[:, part], h_hi[:, par, :], start=True, stop=False)
                        pe.matmul(out, w_hi[:, part], h_lo[:, par, :], start=False, stop=False)
                        pe.matmul(out, w_lo[:, part], h_hi[:, par, :], start=False, stop=True).then_inc(done, 1)

            def step(i, par):
                if live(i, 2, N):
                    pe.wait_ge(s_hlo, i - 1)
                    hidden(i - 2, par, (0,))
                if live(i, 3, N):
                    g = i - 3
                    pe.wait_ge(s_gated, NCH * (g + 1))
                    wait(pe, s_res, g)
                    for j in range(GT):
                        for n, m in enumerate(HCH):
                            mm = pe.matmul(ps_out[:, j, :], gated[0:m, 1 - par, n, j * P:(j + 1) * P], w2[0:m, n, :],
                                           start=(n == 0), stop=(n == NCH - 1))
                    mm.then_inc(s_out, 1)
                if live(i, 0, N):
                    wait(pe, s_in, 2 * i)
                    pe.matmul(ps_shift[:, :, H2:D], c("shift"), Y[:, bass.ds(i * GT, GT), H2:D],
                              start=True, stop=True).then_inc(s_shift, 1)
                if live(i, 1, N):
                    g = i - 1
                    pe.wait_ge(s_h, GT * (g + 1))
                    wait(pe, s_hT, g)
                    for j in range(GT):
                        mm = pe.transpose(ps_turn[:, j * P:(j + 1) * P], h[:, j, :], c("ident"))
                    mm.then_inc(s_turned, 1)
                if live(i, 2, N):
                    hidden(i - 2, par, (1,))
                if live(i, 2, N):
                    hidden(i - 2, par, (2,))
            sweep(pe, N, LAG, 2, step)

        @block.scalar
        def _(act):
            act.preload_act_table_set("gelu_and_others")

            def gelus(g, par, chunks):
                for n in chunks:
                    m, b = HCH[n], (NCH * par + n) % 2
                    act.wait_ge(s_g, NCH * g + n + 1)
                    wait(act, s_gated, NCH * g + n - 1)
                    act.activation(gelu[0:m, b, :], ps_g[0:m, b, :], ACT.Gelu,
                                   bias=cols[0:m, 3 + n:4 + n]).then_inc(s_gelu, 1)

            def step(i, par):
                if live(i, 2, N):
                    gelus(i - 2, par, (0,))
                if live(i, 0, N):
                    wait(act, s_h, GT * (i - 1))
                    act.activation(x_in[:, par, :, 0:H2], Y[:, bass.ds(i * GT, GT), 0:H2], ACT.Copy).then_inc(s_in, 1)
                    act.wait_ge(s_shift, i + 1)
                    act.activation(x_in[:, par, :, H2:D], ps_shift[:, :, H2:D], ACT.Copy).then_inc(s_in, 1)
                if live(i, 1, N):
                    g = i - 1
                    act.wait_ge(s_turned, g + 1)
                    wait(act, s_hlo, g)
                    act.activation(hT[:], ps_turn[:], ACT.Identity, bias=cols[:, 7:8],
                                   scale=cols[:, 6:7]).then_inc(s_hT, 1)
                if live(i, 2, N):
                    gelus(i - 2, par, (1,))
                if live(i, 2, N):
                    gelus(i - 2, par, (2,))
            sweep(act, N, LAG, 2, step)

        @block.vector
        def _(dve):
            def gate(g, par, n):
                m, b = HCH[n], (NCH * par + n) % 2
                wait(dve, s_out, g - 1)
                dve.wait_ge(s_a, NCH * g + n + 1)
                dve.wait_ge(s_gelu, NCH * g + n + 1)
                dve.scalar_tensor_tensor(out=gated[0:m, par, n, :], in0=ps_a[0:m, b, :],
                                         scalar=cols[0:m, n:n + 1], in1=gelu[0:m, b, :],
                                         op0=ALU.add, op1=ALU.mult).then_inc(s_gated, 1)

            def step(i, par):
                if live(i, 1, N):
                    g = i - 1
                    dve.wait_ge(s_rstd, g + 1)
                    wait(dve, s_turned, g)
                    for j in range(GT):
                        dve.tensor_scalar(h[:, j, :], x_in[:, 1 - par, j, :], meanvar[:, 1 - par, j, 0:1],
                                          rstd[:, j:j + 1], ALU.subtract, ALU.mult).then_inc(s_h, 1)
                if live(i, 2, N):
                    gate(i - 2, par, 0)
                if live(i, 3, N):
                    g = i - 3
                    dve.wait_ge(s_out, g + 1)
                    dve.wait_ge(s_bias2 if last else s_bias, g + 1)
                    dve.tensor_tensor(group_rows(Y, g), ps_out[:], group_rows(Y, g), ALU.add).then_inc(s_res, 1)
                if live(i, 0, N):
                    dve.wait_ge(s_in, 2 * (i + 1))
                    wait(dve, s_meanvar, GT * i)
                    for j in range(GT):
                        dve.bn_stats(stats[:, j, :], x_in[:, par, j, :]).then_inc(s_stats, 1)
                    dve.wait_ge(s_stats, GT * (i + 1))
                    apart(dve, s_apart)
                    for j in range(GT):
                        dve.bn_aggr(meanvar[:, par, j, :], stats[:, j, :]).then_inc(s_meanvar, 1)
                    dve.wait_ge(s_meanvar, GT * (i + 1))
                    wait(dve, s_rstd, i)
                    dve.tensor_scalar(vareps[:], meanvar[:, par, :, 1], LN_EPS, None, ALU.add).then_inc(s_vareps, 1)
                if live(i, 1, N):
                    g = i - 1
                    dve.wait_ge(s_hT, g + 1)
                    wait(dve, s_a, NCH * (g - 1))
                    dve.tensor_copy(h_hi[:, 1 - par, :], hT[:]).then_inc(s_hhi, 1)
                    dve.wait_ge(s_hhi, g + 1)
                    dve.tensor_tensor(h_lo[:, 1 - par, :], hT[:], h_hi[:, 1 - par, :].bitcast(F32),
                                      ALU.subtract).then_inc(s_hlo, 1)
                if live(i, 2, N):
                    gate(i - 2, par, 1)
                if live(i, 2, N):
                    gate(i - 2, par, 2)
            sweep(dve, N, LAG, 2, step)

        @block.gpsimd
        def _(pool):
            def step(i, par):
                if live(i, 0, N):
                    pool.wait_ge(s_vareps, i + 1)
                    wait(pool, s_h, GT * i)
                    pool.tensor_tensor(rstd[:], vareps[:], c("eps")[:, 3:4].broadcast_to([P, GT]),
                                       ALU.pow).then_inc(s_rstd, 1)
                if live(i, 1, N):
                    g = i - 1
                    pool.wait_ge(s_in, 2 * (g + 1))
                    pool.tensor_tensor(group_rows(Y, g), group_rows(Y, g),
                                       b2[:].unsqueeze(1).broadcast_to([P, GT, D]), ALU.add).then_inc(s_bias, 1)
                    if last:
                        pool.wait_ge(s_bias, g + 1)
                        pool.tensor_tensor(group_rows(Y, g), group_rows(Y, g), group_rows(X, g),
                                           ALU.add).then_inc(s_bias2, 1)
            sweep(pool, N, LAG, 2, step)
            if not last:
                split_weights(pool, t["wqkv"][layer + 1], t["wqkv_hi"], t["wqkv_lo"], s_split)


def build(nc, dram):
    with ExitStack() as ctx:
        def sb(name, shape, dt=F32):
            return ctx.enter_context(nc.sbuf_tensor(name, shape, dt))

        t = {"const": sb("const", [P, NCONST]), "X": sb("X", [P, TILES, D])}
        t["c"] = lambda name: t["const"][:, CONSTS[name][0]:CONSTS[name][1]]
        t["w4"] = sb("w4", [P, 4 * D])
        for n, name in enumerate(("wq", "wk", "wv", "wo")):
            t[name] = t["w4"][:, n * D:(n + 1) * D]
        t["small"] = sb("small", [P, NSMALL])
        for name, (lo, hi) in SMALLS.items():
            t[name] = t["small"][:, lo:hi]
        t["winspread"] = sb("winspread", [WIN * AH, WIN, P])
        t["winfold"] = sb("winfold", [P, WIN, WIN * AH])
        t["winspread_r"] = sb("winspread_r", [WIN * AH, WIN, P], F32R)
        t["gate_kv"] = sb("gate_kv", [P, 2 * MH])
        t["kpad"] = sb("kpad", [P, GS, PADSEQ])
        t["vpad"] = sb("vpad", [P, NSEQ, PADSEQ])
        t["ctxpad"] = sb("ctxpad", [P, 2, GT, MH, MHD + 1])
        t["qdiag"] = sb("qdiag", [P, 2, GS, MH, SEQ])
        t["sameseq_r"] = sb("sameseq_r", [P, P], F32R)
        t["ident16"] = sb("ident16", [P, P], BF16)
        t["causal16"] = sb("causal16", [P, 8, SEQ], BF16)
        t["keyquery16"] = sb("keyquery16", [P, 8, SEQ], BF16)
        t["Y"] = sb("Y", [P, TILES, D])
        t["rms1"] = sb("rms1", [P, MHD])
        for name, shape in (("wqkv", [P, 3 * INNER]), ("lwo", [P, LH // 2, D]), ("qks", [P, 2, LHD]),
                            ("w1", [P, 2 * HID]), ("w2", [P, len(HCH), D]), ("ffncols", [P, 8]), ("b2", [P, D])):
            t[name] = [sb(f"{name}{layer}", shape) for layer in range(DEPTH)]
        for name, n in (("wqkv", 3 * INNER), ("w1", 2 * HID)):
            for part in ("hi", "lo"):
                t[f"{name}_{part}"] = sb(f"{name}_{part}", [P, n], F32R)
        t["s_layers"] = ctx.enter_context(nc.semaphore("layer_weights_loaded"))
        t["layers_loaded"] = 16 * DEPTH * len(LAYER_INPUTS)
        window_attention(nc, t, dram)
        mlstm(nc, t, dram)
        for layer in range(DEPTH):
            causal_attention(nc, t, layer)
            gated_ffn(nc, t, dram, layer)


def shape_constants():
    p = np.arange(P)
    tok = p % SEQ
    out = np.zeros((P, NCONST), np.float32)

    def put(name, a):
        out[:, CONSTS[name][0]:CONSTS[name][1]] = a
    same = (p[:, None] // SEQ) == (p[None, :] // SEQ)
    put("ident", np.eye(P))
    place = tok[:, None] + np.arange(WIN)[None, :] - HALF
    put("winmask", np.repeat(np.where((place >= 0) & (place < SEQ), 0.0, NEG), AH, axis=1))
    put("causal", np.where(np.arange(SEQ)[None, :] > tok[:, None], NEG, 0.0))
    put("keyquery", np.where(np.arange(SEQ)[None, :] < tok[:, None], NEG, 0.0))
    put("tri", same & (p[:, None] <= p[None, :]))
    put("negfold", -(tok[:, None] == np.arange(SEQ)[None, :]).astype(np.float32))
    put("sameseq", same)
    put("shift", same & (p[:, None] + 1 == p[None, :]))
    put("eps", np.tile(np.array([LN_EPS, 1e-6, 1.0, -0.5], np.float32), (P, 1)))
    put("seqstart", np.where(p[None, :] % SEQ == 0, NEG, 0.0) * np.ones((P, 1)))
    half = np.arange(0, LHD, 2, dtype=np.float32)
    freq = np.arange(SEQ, dtype=np.float32)[:, None] * (np.float32(1.0) / np.float32(10000.0) ** (half / LHD))[None, :]
    freq = np.concatenate([freq, freq], -1)
    base = (half + np.float32(0.4 * LHD)) / np.float32(1.4 * LHD)
    power = (np.arange(SEQ, dtype=np.float32) - SEQ // 2) / np.float32(32.0)
    scale = base[None, :] ** power[:, None]
    scale = np.concatenate([scale, scale], -1)
    sign = np.where(np.arange(LHD) < LHD // 2, -1.0, 1.0).astype(np.float32)
    cos, sin = np.cos(freq), np.sin(freq) * sign
    put("rot", np.tile(np.concatenate([cos * scale, cos / scale, sin * scale, sin / scale], 1), (2, 1)))
    spread = np.zeros((WIN, AH, WIN, P), np.float32)
    for w in range(WIN):
        spread[w, :, w, :] = np.arange(AH)[:, None] == p[None, :] // AHD
    spread = spread.reshape(WIN * AH, WIN, P)
    return out, spread, spread.transpose(2, 1, 0)


def kernel(**inputs):
    import concourse.bacc as bacc
    from concourse.bass_utils import run_bass_kernel_spmd

    def arr(name):
        return np.asarray(inputs[name])

    def rows(a):
        return np.ascontiguousarray(np.broadcast_to(np.asarray(a).reshape(1, -1), (P, np.asarray(a).size)))

    const, spread, fold = shape_constants()
    ins = {
        "x": arr("x").reshape(TOKENS, D), "ctx": arr("ctx_1024").reshape(TOKENS, D),
        "ctxT": arr("ctx_1024").reshape(TOKENS, D).T, "const": const,
        "winspread": spread, "winfold": fold,
        "w4": np.concatenate([arr(f"L0_attn_W{n}").T for n in "qkvo"], 1),
    }
    gates = np.concatenate([arr("L0_xattn_igate_kernel"), arr("L0_xattn_fgate_kernel")], 1)
    ins["small"] = np.concatenate([
        np.stack([arr("L0_attn_bq"), arr("L0_attn_bk"), arr("L0_attn_bv")], 1), rows(arr("L0_attn_bo")),
        gates[:D], gates[D:2 * D], gates[2 * D:],
        rows(np.concatenate([arr("L0_xattn_igate_bias"), arr("L0_xattn_fgate_bias")])),
        rows(arr("L0_xattn_rms_scale"))], 1)

    pad = np.zeros(P - HCH[-1], np.float32)
    for layer in range(DEPTH):
        w1b = arr("L0_ffn_b1")[layer]
        chunks = []
        for at in (0, HID):
            for n, m in enumerate(HCH):
                col = w1b[at + n * P:at + n * P + m]
                chunks.append(col if m == P else np.concatenate([col, pad]))
        w2 = arr("L0_ffn_w2")[layer]
        ins[f"wqkv{layer}"] = arr("L0_ffn_wqkv")[layer]
        ins[f"lwo{layer}"] = arr("L0_ffn_wo")[layer].reshape(LH // 2, P, D).transpose(1, 0, 2)
        ins[f"qks{layer}"] = rows(np.stack([arr("L0_ffn_q_scale")[layer], arr("L0_ffn_k_scale")[layer]])).reshape(
            P, 2, LHD)
        ins[f"w1{layer}"] = arr("L0_ffn_w1")[layer]
        ins[f"w2{layer}"] = np.concatenate([w2, np.zeros((len(HCH) * P - HID, D), np.float32)]).reshape(
            len(HCH), P, D).transpose(1, 0, 2)
        ins[f"ffncols{layer}"] = np.stack(chunks + [arr("L0_ffn_ln_g")[layer], arr("L0_ffn_ln_b")[layer]], 1)
        ins[f"b2{layer}"] = rows(arr("L0_ffn_b2")[layer])

    nc = bacc.Bacc("TRN2", target_bir_lowering=False, num_devices=1)
    arrays, dram = {}, {}
    for name, a in ins.items():
        a = np.ascontiguousarray(a)
        arrays[f"in_{name}"] = a
        dram[name] = nc.dram_tensor(f"in_{name}", list(a.shape), mybir.dt.from_np(a.dtype), kind="ExternalInput").ap()
    dram["out"] = nc.dram_tensor("out", [TOKENS, D], F32, kind="ExternalOutput").ap()
    build(nc, dram)
    r = run_bass_kernel_spmd(nc, [arrays], core_ids=[0])
    return np.asarray(r.results[0]["out"]).reshape(NSEQ, SEQ, D)
```
